# Optimizing a Trainium2 kernel written in Bass

```python
import numpy as np
import jax
import jax.numpy as jnp

def _softmax(x, axis=-1):
    return jax.nn.softmax(x, axis=axis)

def _gelu(x):
    return jax.nn.gelu(x, approximate=True)

def _silu(x):
    return jax.nn.silu(x)

def _sigmoid(x):
    return jax.nn.sigmoid(x)

def _layernorm(x, axis=-1, eps=1e-05):
    m = jnp.mean(x, axis=axis, keepdims=True)
    v = jnp.var(x, axis=axis, keepdims=True)
    return (x - m) / jnp.sqrt(v + eps)

def _scatter_add(tgt, idx, src, axis=0):
    return tgt.at[idx].add(src)

def _segment_sum(src, seg, n):
    return jax.ops.segment_sum(src, seg, n)
kernel_name = 'mk_adaln_ffn_d2_seqx_r8_3f1e5d'

def setup_inputs(seed: int=0):
    np.random.seed(seed)
    _w = jnp.asarray

    def _rec_inputs():
        import jax
        import jax.numpy as jnp
        _rk = jax.random.key(seed)
        x = -0.0003929 + 0.9999 * jax.random.normal(jax.random.fold_in(_rk, 1), (64, 32, 512), jnp.float32)
        _lenS = 32 - jax.random.randint(jax.random.fold_in(_rk, 7), (64,), 0, max(1, 32 // 4) + 1, jnp.int32)
        _lenS2 = 32 - jax.random.randint(jax.random.fold_in(_rk, 8), (64,), 0, max(1, 32 // 4) + 1, jnp.int32)
        itok_B_78_3631 = jax.random.randint(jax.random.fold_in(_rk, 11), (64,), 78, 454, jnp.int32)
        itok_B_2_6 = jax.random.randint(jax.random.fold_in(_rk, 12), (64,), 2, 7, jnp.int32)
        return (x, itok_B_78_3631, itok_B_2_6)
    x, itok_B_78_3631, itok_B_2_6 = _rec_inputs()

    def _L0_cond_setup():
        import math
        import jax, jax.numpy as jnp
        import numpy as np
        B, H, N, L = (16, 32, 64, 512)
        DT_MIN, DT_MAX = (0.001, 0.1)

        def _get_kernel(log_dt, C, log_A_real, A_imag, length):
            dt = jnp.exp(log_dt)
            Cc = C[..., 0] + 1j * C[..., 1]
            A = -jnp.exp(log_A_real) + 1j * A_imag
            dtA = A * dt[:, None]
            Ct = Cc * (jnp.exp(dtA) - 1.0) / A
            P = dtA[:, :, None] * jnp.arange(length, dtype=jnp.float32)
            K = 2.0 * jnp.einsum('hn,hnl->hl', Ct, jnp.exp(P)).real
            return K
        key = jax.random.key(seed)
        ks = jax.random.split(key, 5)
        u = jax.random.normal(ks[0], (B, H, L), dtype=jnp.float32)
        log_dt = jax.random.uniform(ks[1], (H,), dtype=jnp.float32) * (math.log(DT_MAX) - math.log(DT_MIN)) + math.log(DT_MIN)
        C = jax.random.normal(ks[2], (H, N, 2), dtype=jnp.float32)
        log_A_real = jnp.log(0.5 * jnp.ones((H, N), dtype=jnp.float32))
        A_imag = math.pi * jnp.broadcast_to(jnp.arange(N, dtype=jnp.float32), (H, N))
        D = jax.random.normal(ks[3], (H,), dtype=jnp.float32)
        length = jax.random.randint(ks[4], (B,), 1, L + 1, dtype=jnp.int32)
        return {'u': u, 'log_dt': log_dt, 'C': C, 'log_A_real': log_A_real, 'A_imag': A_imag, 'D': D, 'length': length}
    _L0_cond_all = _L0_cond_setup()
    _L0_cond_in = {k: v for k, v in _L0_cond_all.items() if k in ('log_dt', 'C', 'log_A_real', 'A_imag', 'D')}
    del _L0_cond_all

    def _L0_ffn_setup():
        import jax, jax.numpy as jnp
        import numpy as np
        BS = 128
        FP8_MAX = 448.0

        def act_quant(x):
            T, K = x.shape
            xb = x.reshape(T, K // BS, BS)
            amax = jnp.max(jnp.abs(xb), axis=-1)
            scale = amax / FP8_MAX + 1e-12
            xq = (xb / scale[:, :, None]).reshape(T, K)
            return (xq, scale)

        def linear_dsv3(x, wq, w_scale):
            T, K = x.shape
            N = wq.shape[0]
            xq, xs = act_quant(x)
            xdq = (xq.reshape(T, K // BS, BS) * xs[:, :, None]).reshape(T, K)
            wdq = (wq.reshape(N // BS, BS, K // BS, BS) * w_scale[:, None, :, None]).reshape(N, K)
            return xdq @ wdq.T
        key = jax.random.key(seed)
        ks = jax.random.split(key, 4)
        DIM, INTER = (512, 1792)

        def make_qweight(k, n, m):
            w = jax.random.normal(k, (n, m), dtype=jnp.float32) * 0.02
            wb = w.reshape(n // BS, BS, m // BS, BS)
            amax = jnp.max(jnp.abs(wb), axis=(1, 3))
            scale = amax / FP8_MAX + 1e-12
            wq = (wb / scale[:, None, :, None]).reshape(n, m)
            return (wq, scale)
        x = jax.random.normal(ks[0], (2, 128, DIM), dtype=jnp.float32)
        w1, w1_scale = make_qweight(ks[1], INTER, DIM)
        w3, w3_scale = make_qweight(ks[2], INTER, DIM)
        w2, w2_scale = make_qweight(ks[3], DIM, INTER)
        return {'x': x, 'w1': w1, 'w1_scale': w1_scale, 'w3': w3, 'w3_scale': w3_scale, 'w2': w2, 'w2_scale': w2_scale}
    _L0_ffn_all = _L0_ffn_setup()
    _L0_ffn_in = {k: v for k, v in _L0_ffn_all.items() if k in ('w1', 'w1_scale', 'w3', 'w3_scale', 'w2', 'w2_scale')}
    del _L0_ffn_all

    def _L1_cond_setup():
        import jax, jax.numpy as jnp
        import numpy as np
        B, N, H, F = (4, 64, 512, 1376)
        L, R, RANK = (1, 16, 16)
        SCALE = 0.5
        key = jax.random.key(seed)
        ks = jax.random.split(key, 12)
        nrm = lambda k, shape, fan: jax.random.normal(k, shape, jnp.float32) * fan ** (-0.5)
        inp = {'x': jax.random.normal(ks[0], (B, N, H), jnp.float32), 'W_gate': nrm(ks[1], (F, H), H), 'W_up': nrm(ks[2], (F, H), H), 'W_down': nrm(ks[3], (H, F), F), 'A_gate': nrm(ks[4], (L, R, RANK, H), H), 'B_gate': nrm(ks[5], (L, R, F, RANK), RANK), 'A_up': nrm(ks[6], (L, R, RANK, H), H), 'B_up': nrm(ks[7], (L, R, F, RANK), RANK), 'A_down': nrm(ks[8], (L, R, RANK, F), F), 'B_down': nrm(ks[9], (L, R, H, RANK), RANK), 'lora_indices': jax.random.randint(ks[10], (B,), 0, R), 'layer_idx': 0}
        return inp
    _L1_cond_all = _L1_cond_setup()
    _L1_cond_in = {k: v for k, v in _L1_cond_all.items() if k in ('W_gate', 'W_up', 'W_down', 'A_gate', 'B_gate', 'A_up', 'B_up', 'A_down', 'B_down')}
    del _L1_cond_all

    def _L1_ffn_setup():
        import jax, jax.numpy as jnp
        import numpy as np
        EPS = 1e-05

        def rms_norm(x):
            return x * jax.lax.rsqrt(jnp.mean(x * x, axis=-1, keepdims=True) + EPS)

        def activation_quant(x):
            scale = 127.0 / jnp.clip(jnp.max(jnp.abs(x), axis=-1, keepdims=True), EPS, None)
            return jnp.clip(jnp.round(x * scale), -128.0, 127.0) / scale

        def weight_quant(w):
            scale = 1.0 / jnp.clip(jnp.mean(jnp.abs(w)), EPS, None)
            return jnp.clip(jnp.round(w * scale), -1.0, 1.0) / scale
        key = jax.random.key(seed)
        k1, k2, k3 = jax.random.split(key, 3)
        B, S, D = (4, 256, 512)
        x = jax.random.normal(k1, (B, S, D), dtype=jnp.float32)
        W = jax.random.normal(k2, (D, D), dtype=jnp.float32) * (1.0 / np.sqrt(D))
        b = jax.random.normal(k3, (D,), dtype=jnp.float32) * 0.02
        return {'x': x, 'W': W, 'b': b}
    _L1_ffn_all = _L1_ffn_setup()
    _L1_ffn_in = {k: v for k, v in _L1_ffn_all.items() if k in ('W', 'b')}
    del _L1_ffn_all
    return {'x': x, 'itok_B_78_3631': itok_B_78_3631, 'itok_B_2_6': itok_B_2_6, 'L0_cond_log_dt': _L0_cond_in['log_dt'], 'L0_cond_C': _L0_cond_in['C'], 'L0_cond_log_A_real': _L0_cond_in['log_A_real'], 'L0_cond_A_imag': _L0_cond_in['A_imag'], 'L0_cond_D': _L0_cond_in['D'], 'L0_ffn_w1': _L0_ffn_in['w1'], 'L0_ffn_w1_scale': _L0_ffn_in['w1_scale'], 'L0_ffn_w3': _L0_ffn_in['w3'], 'L0_ffn_w3_scale': _L0_ffn_in['w3_scale'], 'L0_ffn_w2': _L0_ffn_in['w2'], 'L0_ffn_w2_scale': _L0_ffn_in['w2_scale'], 'L1_cond_W_gate': _L1_cond_in['W_gate'], 'L1_cond_W_up': _L1_cond_in['W_up'], 'L1_cond_W_down': _L1_cond_in['W_down'], 'L1_cond_A_gate': _L1_cond_in['A_gate'], 'L1_cond_B_gate': _L1_cond_in['B_gate'], 'L1_cond_A_up': _L1_cond_in['A_up'], 'L1_cond_B_up': _L1_cond_in['B_up'], 'L1_cond_A_down': _L1_cond_in['A_down'], 'L1_cond_B_down': _L1_cond_in['B_down'], 'L1_ffn_W': _L1_ffn_in['W'], 'L1_ffn_b': _L1_ffn_in['b']}

def reference(x, itok_B_78_3631, itok_B_2_6, L0_cond_log_dt, L0_cond_C, L0_cond_log_A_real, L0_cond_A_imag, L0_cond_D, L0_ffn_w1, L0_ffn_w1_scale, L0_ffn_w3, L0_ffn_w3_scale, L0_ffn_w2, L0_ffn_w2_scale, L1_cond_W_gate, L1_cond_W_up, L1_cond_W_down, L1_cond_A_gate, L1_cond_B_gate, L1_cond_A_up, L1_cond_B_up, L1_cond_A_down, L1_cond_B_down, L1_ffn_W, L1_ffn_b):
    import jax
    import jax.numpy as jnp

    def _L0_cond_ref(u, log_dt, C, log_A_real, A_imag, D, length):
        import math
        import jax, jax.numpy as jnp
        import numpy as np
        B, H, N, L = (16, 32, 64, 512)
        DT_MIN, DT_MAX = (0.001, 0.1)

        def _get_kernel(log_dt, C, log_A_real, A_imag, length):
            dt = jnp.exp(log_dt)
            Cc = C[..., 0] + 1j * C[..., 1]
            A = -jnp.exp(log_A_real) + 1j * A_imag
            dtA = A * dt[:, None]
            Ct = Cc * (jnp.exp(dtA) - 1.0) / A
            P = dtA[:, :, None] * jnp.arange(length, dtype=jnp.float32)
            K = 2.0 * jnp.einsum('hn,hnl->hl', Ct, jnp.exp(P)).real
            return K
        Bq, Hq, Lq = u.shape
        K = _get_kernel(log_dt, C, log_A_real, A_imag, Lq)
        n = 2 * Lq
        kf = jnp.fft.rfft(K, n=n)
        uf = jnp.fft.rfft(u, n=n)
        y = jnp.fft.irfft(uf * kf[None], n=n)[..., :Lq]
        y = y + u * D[:, None]
        mask = (jnp.arange(Lq)[None, :] < length[:, None]).astype(u.dtype)
        return y * mask[:, None, :]

    def _L0_ffn_ref(x, w1, w1_scale, w3, w3_scale, w2, w2_scale):
        import jax, jax.numpy as jnp
        import numpy as np
        BS = 128
        FP8_MAX = 448.0

        def act_quant(x):
            T, K = x.shape
            xb = x.reshape(T, K // BS, BS)
            amax = jnp.max(jnp.abs(xb), axis=-1)
            scale = amax / FP8_MAX + 1e-12
            xq = (xb / scale[:, :, None]).reshape(T, K)
            return (xq, scale)

        def linear_dsv3(x, wq, w_scale):
            T, K = x.shape
            N = wq.shape[0]
            xq, xs = act_quant(x)
            xdq = (xq.reshape(T, K // BS, BS) * xs[:, :, None]).reshape(T, K)
            wdq = (wq.reshape(N // BS, BS, K // BS, BS) * w_scale[:, None, :, None]).reshape(N, K)
            return xdq @ wdq.T
        B, S, D = x.shape
        xf = x.reshape(-1, D)
        g = linear_dsv3(xf, w1, w1_scale)
        u = linear_dsv3(xf, w3, w3_scale)
        h = jax.nn.silu(g) * u
        y = linear_dsv3(h, w2, w2_scale)
        return y.reshape(B, S, D)

    def _L1_cond_ref(x, W_gate, W_up, W_down, A_gate, B_gate, A_up, B_up, A_down, B_down, lora_indices, layer_idx):
        import jax, jax.numpy as jnp
        import numpy as np
        B, N, H, F = (4, 64, 512, 1376)
        L, R, RANK = (1, 16, 16)
        SCALE = 0.5

        def lora_add(base, inp, A, B):
            Ab = A[layer_idx][lora_indices]
            Bb = B[layer_idx][lora_indices]
            t = jnp.einsum('bri,bni->bnr', Ab, inp)
            return base + jnp.einsum('bor,bnr->bno', Bb, t) * SCALE
        gate = lora_add(jnp.einsum('bnh,fh->bnf', x, W_gate), x, A_gate, B_gate)
        up = lora_add(jnp.einsum('bnh,fh->bnf', x, W_up), x, A_up, B_up)
        act = jax.nn.silu(gate) * up
        down = lora_add(jnp.einsum('bnf,hf->bnh', act, W_down), act, A_down, B_down)
        return down

    def _L1_ffn_ref(x, W, b):
        import jax, jax.numpy as jnp
        import numpy as np
        EPS = 1e-05

        def rms_norm(x):
            return x * jax.lax.rsqrt(jnp.mean(x * x, axis=-1, keepdims=True) + EPS)

        def activation_quant(x):
            scale = 127.0 / jnp.clip(jnp.max(jnp.abs(x), axis=-1, keepdims=True), EPS, None)
            return jnp.clip(jnp.round(x * scale), -128.0, 127.0) / scale

        def weight_quant(w):
            scale = 1.0 / jnp.clip(jnp.mean(jnp.abs(w)), EPS, None)
            return jnp.clip(jnp.round(w * scale), -1.0, 1.0) / scale
        xn = rms_norm(x)
        xq = xn + jax.lax.stop_gradient(activation_quant(xn) - xn)
        wq = W + jax.lax.stop_gradient(weight_quant(W) - W)
        y = jnp.einsum('bsd,od->bso', xq, wq) + b
        return x + jax.nn.gelu(y, approximate=False)
    x = x + _L0_ffn_ref(_L0_cond_ref(x, L0_cond_log_dt, L0_cond_C, L0_cond_log_A_real, L0_cond_A_imag, L0_cond_D, itok_B_78_3631), L0_ffn_w1, L0_ffn_w1_scale, L0_ffn_w3, L0_ffn_w3_scale, L0_ffn_w2, L0_ffn_w2_scale)
    x = x + _L1_ffn_ref(_L1_cond_ref(x, L1_cond_W_gate, L1_cond_W_up, L1_cond_W_down, L1_cond_A_gate, L1_cond_B_gate, L1_cond_A_up, L1_cond_B_up, L1_cond_A_down, L1_cond_B_down, itok_B_2_6, 0), L1_ffn_W, L1_ffn_b)
    return x

_drawn_inputs = setup_inputs


def setup_inputs(seed=0):
    import zlib

    import numpy as np

    out = dict(_drawn_inputs(seed))
    spreads = {'L0_cond_log_A_real': (-0.6931471824645996, 0.6)}
    factors = {'L0_ffn_w3_scale': 2.916, 'L0_ffn_w2_scale': 3.793, 'L1_ffn_b': 56.248, 'L1_ffn_W': 2.797}
    for name, (base, spread) in spreads.items():
        noise = np.random.default_rng([zlib.crc32(name.encode()), seed]).standard_normal(out[name].shape)
        drawn = base * np.exp(spread * noise) if base else spread * noise
        out[name] = jnp.asarray(drawn.astype(out[name].dtype))
    for name, factor in factors.items():
        out[name] = (out[name] * factor).astype(out[name].dtype)
    return out
```

```python
from contextlib import ExitStack

import numpy as np

import concourse.bass as bass
from concourse import mybir

F32 = mybir.dt.float32
F32R = mybir.dt.float32r
BF16 = mybir.dt.bfloat16
I32 = mybir.dt.int32
ALU = mybir.AluOpType
ACT = mybir.ActivationFunctionType
AX = mybir.AxisListType

P = 128
BATCH, HEADS, L = 64, 32, 512
TOK = BATCH * HEADS
KB = L // P
NT = 4
TT = TOK // NT
HPT = HEADS // NT
BPT = BATCH // NT
F0, F1 = 1792, 1376
NF0 = F0 // P
NF1 = -(-F1 // P)
NC0 = NF0 // 2
NC1 = -(-NF1 // 2)
EXP, RANK = 16, 16
GB = P // RANK
NG = BATCH // GB
GT = GB * HEADS
NSTATE = 64
NA, NB = 16, 32
KROW = L + P
MAGIC = float(3 << 22)
LN2_HI, LN2_LO = 0.693359375, -2.12194440e-4
LOG2E = 1.4426950408889634
TWO_PI = 6.283185
EPS = 1e-5


def bc(ap, dim, n):
    ap = ap.unsqueeze(dim)
    shape = list(ap.shape)
    shape[dim] = n
    return ap.to_broadcast(shape)


def build(nc, x_t, par, d_row, length, idx, w0, sc0, w1, tab_a, tab_b, tab_ad, tab_bd, wq, bias, rowbase, out):
    with ExitStack() as top:
        scope = [top]

        def sb(name, shape, dt=F32):
            return scope[0].enter_context(nc.sbuf_tensor(name, shape, dt))

        def sem(name):
            return top.enter_context(nc.semaphore(name))

        krev = nc.dram_tensor("krev", (HEADS, KROW), F32, kind="Internal").ap()

        ps_gu = [top.enter_context(nc.psum_tensor(f"ps_gu{i}", [P, 512], F32))[:] for i in range(3)]
        ps_d = top.enter_context(nc.psum_tensor("ps_d", [P, 4, 512], F32))
        ps_t = top.enter_context(nc.psum_tensor("ps_t", [P, 512], F32))
        G_BANK, U_BANK = (0, 2), (1, 0)

        acc = sb("acc", [P, KB, TOK])
        a_hi = sb("a_hi", [P, KB, TOK], F32R)
        a_lo = sb("a_lo", [P, KB, TOK], F32R)
        gu_hi = sb("gu_hi", [P, 2, 2, KB, P], F32R)
        gu_lo = sb("gu_lo", [P, 2, 2, KB, P], F32R)
        dn_hi = sb("dn_hi", [P, 2, L], F32R)
        dn_lo = sb("dn_lo", [P, 2, L], F32R)
        raw = sb("raw", [P, 2, 3, L])
        s_act = sb("s_act", [P, 2, TT])
        h_hi = sb("h_hi", [P, 2, TT], F32R)
        h_lo = sb("h_lo", [P, 2, TT], F32R)
        lmask = sb("lmask", [P, GT])
        ix = sb("ix", [1, BATCH], I32)
        z = acc[:].rearrange("p k t -> p (k t)").rearrange("p (s n) -> p s n", n=L)

        chain = [0]
        s_chain = sem("s_chain")

        def by_head(t):
            return t[:].rearrange("p k (b h) -> p k b h", h=HEADS)

        def mm3(pe, out_ap, st_hi, st_lo, mv_hi, mv_lo, start, stop, skip=False):
            pe.matmul(out_ap, st_hi, mv_hi, start=start, stop=False, skip_group_check=skip)
            pe.matmul(out_ap, st_hi, mv_lo, start=False, stop=False, skip_group_check=skip)
            return pe.matmul(out_ap, st_lo, mv_hi, start=False, stop=stop, skip_group_check=skip)

        s_par, s_drow, s_len, s_ix = sem("s_par"), sem("s_drow"), sem("s_len"), sem("s_ix")
        s_x = sem("s_x")
        s_raw0 = [sem(f"s_raw0_{f}") for f in range(2)]
        s_sc0 = sem("s_sc0")
        s_grid, s_sin, s_theta, s_sf, s_kp, s_ks, s_kw, s_kz = (sem(n) for n in (
            "s_grid", "s_sin", "s_theta", "s_sf", "s_kp", "s_ks", "s_kw", "s_kz"))
        s_wsc = [sem(f"s_wsc{f}") for f in range(2)]
        s_whg = [sem(f"s_whg{f}") for f in range(2)]
        s_wlg = [sem(f"s_wlg{f}") for f in range(2)]
        s_whd = [sem(f"s_whd{f}") for f in range(2)]
        s_wld = [sem(f"s_wld{f}") for f in range(2)]
        s_T = sem("s_T")

        with ExitStack() as l0:
            scope[0] = l0
            scale0 = sb("scale0", [P, NF0, 12])
            cmask = sb("cmask", [P, KB, BATCH])
            toep = sb("toep", [P, HPT, L])
            ytmp = sb("ytmp", [P, 2, 2, KB * BATCH])

            with ExitStack() as pa:
                scope[0] = pa
                par_sb = sb("par_sb", [P, 5, HEADS])
                drow = sb("drow", [1, HEADS])
                len_i = sb("len_i", [P, BATCH], I32)
                len_f = sb("len_f", [P, BATCH])
                pos = sb("pos", [P, KB, BATCH])
                pow2 = sb("pow2", [P, 9])
                lgrid = sb("lgrid", [P, 64])
                phase = sb("phase", [P, 64])
                dm = sb("dm", [1, HEADS, NB])
                onehot = sb("onehot", [1, NA])
                zero = sb("zero", [HEADS, P])
                k_sb = sb("k_sb", [NA, HEADS, NB])
                e2 = sb("e2", [P, 2, HEADS])
                sm = [sb(f"sm{i}", [P, HEADS]) for i in range(16)]
                pin = sb("pin", [P, 9, HEADS])
                pw = sb("pw", [P, 9, HEADS])
                tmp = [sb(f"tmp{i}", [P, 9 * HEADS]) for i in range(4)]
                kint = sb("kint", [P, 9 * HEADS], I32)
                mag = sb("mag", [P, HEADS, NA + NB])
                theta = toep[:, 0:4].rearrange("p a n -> p (a n)").rearrange("p (h n) -> p h n", n=64)
                trig = toep[:, 4:8].rearrange("p a n -> p (a n)").rearrange("p (h n) -> p h n", n=64)
                rnd = trig
                S = sb("S", [P, HEADS, NA])
                S2 = sb("S2", [P, HEADS, NA])
                Fm = sb("Fm", [P, HEADS, NB])
                trig_small = (sb("sin1", [P, HEADS])[:], sb("sin2", [P, HEADS])[:])
                pk = ps_d[0:NA, 0:2, :].rearrange("a c (h b) -> a (c h) b", b=NB)

                with nc.Block() as block:
                    @block.sync
                    def _(sp):
                        sp.dma_start(par_sb[:], par).then_inc(s_par, 16)
                        sp.dma_start(drow[:], d_row).then_inc(s_drow, 16)
                        sp.dma_start(len_i[:], bass.AP(tensor=length.tensor, offset=0, ap=[[0, P], [1, BATCH]])).then_inc(s_len, 16)
                        sp.dma_start(ix[:], idx).then_inc(s_ix, 16)
                        sp.dma_start(scale0[:].rearrange("p f c -> p (f c)"),
                                     bass.AP(tensor=sc0.tensor, offset=0, ap=[[0, P], [1, NF0 * 12]])).then_inc(s_sc0, 16)
                        for f in range(2):
                            sp.dma_start(raw[:, f].rearrange("p a n -> p (a n)"), w0[f]).then_inc(s_raw0[f], 16)
                        sp.dma_start(acc[:], x_t).then_inc(s_x, 16)
                        sp.wait_ge(s_grid, 1)
                        sp.dma_start(krev[:, L:KROW], zero[:]).then_inc(s_kz, 16)
                        sp.wait_ge(s_ks, 1)
                        sp.dma_start(krev[:, 0:L].rearrange("h (a b) -> a h b", b=NB), k_sb[:]).then_inc(s_kw, 16)
                        sp.wait_ge(s_kw, 16)
                        sp.wait_ge(s_kz, 16)
                        sp.dma_start(toep[:], bass.AP(tensor=krev.tensor, offset=0,
                                                      ap=[[1, P], [KROW, HPT], [1, L]])).then_inc(s_T, 16)

                    @block.gpsimd
                    def _(pool):
                        pool.memset(zero[:], 0.0).then_inc(s_grid, 1)
                        pool.memset(dm[:], 0.0)
                        pool.memset(onehot[:], 0.0)
                        for k in range(9):
                            pool.memset(pow2[:, k:k + 1], float(1 << k))
                        pool.memset(phase[:, 0:NA], 0.25)
                        pool.memset(phase[:, NA:2 * NA], 0.0)
                        pool.memset(phase[:, 2 * NA:64], 0.25).then_inc(s_grid, 1)
                        pool.iota(lgrid[:, 0:2 * NA], [[0, 2], [-NB, NA]], base=NB * (NA - 1), channel_multiplier=0,
                                  allow_small_or_imprecise_dtypes=True)
                        pool.iota(lgrid[:, 2 * NA:64], [[-1, NB]], base=NB - 1, channel_multiplier=0,
                                  allow_small_or_imprecise_dtypes=True).then_inc(s_grid, 1)
                        pool.iota(pos[:], [[P, KB], [0, BATCH]], base=P - 1, channel_multiplier=-1,
                                  allow_small_or_imprecise_dtypes=True).then_inc(s_grid, 1)
                        pool.memset(lmask[:], 0.5).then_inc(s_grid, 1)
                        pool.wait_ge(s_grid, 5)
                        lm = lmask[:].rearrange("p (b h) -> p b h", h=HEADS)
                        pool.affine_select(out=lm, in_=lm, compare_op=ALU.is_ge, fill=0.0, base=0,
                                           pattern=[[-RANK, GB], [0, HEADS]], channel_multiplier=1).then_inc(s_grid, 1)
                        pool.wait_ge(s_grid, 6)
                        pool.affine_select(out=lm, in_=lm, compare_op=ALU.is_ge, fill=0.0, base=RANK - 1,
                                           pattern=[[RANK, GB], [0, HEADS]], channel_multiplier=-1).then_inc(s_grid, 1)

                    @block.vector
                    def _(dve):
                        def link(ins):
                            chain[0] += 1
                            ins.then_inc(s_chain, 1)
                            dve.wait_ge(s_chain, chain[0])

                        def ts(o, i, a, b, op0, op1=None):
                            link(dve.tensor_scalar(o, i, a, b, op0, op1) if op1 is not None
                                 else dve.tensor_scalar(o, i, a, None, op0))

                        def tt(o, i, j, op):
                            link(dve.tensor_tensor(o, i, j, op))

                        def stt(o, i, s, j, op0, op1):
                            link(dve.scalar_tensor_tensor(out=o, in0=i, scalar=s, in1=j, op0=op0, op1=op1))

                        def poly_expm1(p, r):
                            ts(p, r, 1.0 / 5040, None, ALU.mult)
                            for c in (1.0 / 720, 1.0 / 120, 1.0 / 24, 1.0 / 6, 0.5, 1.0):
                                stt(p, p, c, r, ALU.add, ALU.mult)

                        def exp32(o, i, n):
                            xc, k, r, p = (t[:, 0:n] for t in tmp)
                            ki = kint[:, 0:n]
                            ts(xc, i, -87.0, 88.0, ALU.max, ALU.min)
                            ts(k, xc, LOG2E, MAGIC, ALU.mult, ALU.add)
                            ts(k, k, MAGIC, None, ALU.subtract)
                            stt(r, k, -LN2_HI, xc, ALU.mult, ALU.add)
                            stt(r, k, -LN2_LO, r, ALU.mult, ALU.add)
                            poly_expm1(p, r)
                            ts(ki, k, 127.0, float(1 << 23), ALU.add, ALU.mult)
                            stt(o, p, 1.0, ki.bitcast(F32), ALU.add, ALU.mult)

                        dve.wait_ge(s_par, 16)
                        exp32(e2[:].rearrange("p a h -> p (a h)"), par_sb[:, 0:2].rearrange("p a h -> p (a h)"), 2 * HEADS)
                        dt, ea = e2[:, 0], e2[:, 1]
                        ai_in, c_re, c_im = par_sb[:, 2], par_sb[:, 3], par_sb[:, 4]
                        ar, ai, ut, r0, em, y, nr, ni, den, wr, wi, cr, ci, c1, c2, t0 = (t[:] for t in sm)
                        stt(ar, ea, -1.0, dt, ALU.mult, ALU.mult)
                        tt(ai, ai_in, dt, ALU.mult)
                        ts(ut, ai, 0.15915494309189535, None, ALU.mult)
                        ts(r0, ut, MAGIC, MAGIC, ALU.add, ALU.subtract)
                        tt(r0, ut, r0, ALU.subtract)
                        dve.wait_ge(s_grid, 3)
                        link(dve.memset(phase[64:P, 2 * NA:64], 0.0))
                        tt(theta, bc(r0, 2, 64), bc(lgrid[:], 1, HEADS), ALU.mult)
                        tt(theta, theta, bc(phase[:], 1, HEADS), ALU.add)
                        ts(rnd, theta, MAGIC, MAGIC, ALU.add, ALU.subtract)
                        dve.tensor_tensor(theta, theta, rnd, ALU.subtract).then_inc(s_theta, 1)
                        tt(pin[:], bc(ar, 1, 9), bc(pow2[:], 2, HEADS), ALU.mult)
                        exp32(pw[:].rearrange("p a h -> p (a h)"), pin[:].rearrange("p a h -> p (a h)"), 9 * HEADS)
                        link(dve.memset(mag[:, :, NA - 1:NA], 1.0))
                        link(dve.memset(mag[:, :, NA + NB - 1:NA + NB], 1.0))
                        for k in range(5):
                            n, e = 1 << k, NA + NB
                            tt(mag[:, :, e - 2 * n:e - n], mag[:, :, e - n:e], bc(pw[:, k], 2, n), ALU.mult)
                        for k in range(4):
                            n, e = 1 << k, NA
                            tt(mag[:, :, e - 2 * n:e - n], mag[:, :, e - n:e], bc(pw[:, 5 + k], 2, n), ALU.mult)
                        ts(y, ar, -60.0, 1.0 / 64, ALU.max, ALU.mult)
                        poly_expm1(em, y)
                        for _ in range(6):
                            stt(em, em, 2.0, em, ALU.add, ALU.mult)
                        dve.wait_ge(s_sin, 2)
                        sn, sh = trig_small[0], trig_small[1]
                        tt(t0, sh, sh, ALU.mult)
                        ts(t0, t0, 2.0, None, ALU.mult)
                        tt(nr, em, t0, ALU.mult)
                        tt(nr, em, nr, ALU.subtract)
                        tt(nr, nr, t0, ALU.subtract)
                        stt(ni, em, 1.0, sn, ALU.add, ALU.mult)
                        tt(den, ea, ea, ALU.mult)
                        tt(t0, ai_in, ai_in, ALU.mult)
                        tt(den, den, t0, ALU.add)
                        link(dve.reciprocal(den, den))
                        tt(wr, ni, ai_in, ALU.mult)
                        tt(t0, nr, ea, ALU.mult)
                        tt(wr, wr, t0, ALU.subtract)
                        tt(wr, wr, den, ALU.mult)
                        tt(wi, ni, ea, ALU.mult)
                        tt(t0, nr, ai_in, ALU.mult)
                        tt(wi, wi, t0, ALU.add)
                        stt(wi, wi, -1.0, den, ALU.mult, ALU.mult)
                        tt(cr, c_re, wr, ALU.mult)
                        tt(t0, c_im, wi, ALU.mult)
                        tt(cr, cr, t0, ALU.subtract)
                        tt(ci, c_re, wi, ALU.mult)
                        tt(t0, c_im, wr, ALU.mult)
                        tt(ci, ci, t0, ALU.add)
                        ts(c1[0:64], cr[0:64], 2.0, None, ALU.mult)
                        ts(c1[64:P], ci[64:P], -2.0, None, ALU.mult)
                        ts(c2[0:64], ci[0:64], -2.0, None, ALU.mult)
                        ts(c2[64:P], cr[64:P], -2.0, None, ALU.mult)
                        dve.wait_ge(s_sin, 3)
                        tt(S[:], bc(c1, 2, NA), trig[:, :, 0:NA], ALU.mult)
                        tt(S2[:], bc(c2, 2, NA), trig[:, :, NA:2 * NA], ALU.mult)
                        tt(S[:], S[:], S2[:], ALU.add)
                        dve.tensor_tensor(S[:], S[:], mag[:, :, 0:NA], ALU.mult).then_inc(s_sf, 1)
                        dve.tensor_tensor(Fm[:], trig[:, :, 2 * NA:64], mag[:, :, NA:NA + NB], ALU.mult).then_inc(s_sf, 1)
                        dve.wait_ge(s_drow, 16)
                        dve.tensor_copy(dm[:, :, NB - 1], drow[:]).then_inc(s_sf, 1)
                        dve.memset(onehot[:, NA - 1:NA], 1.0).then_inc(s_sf, 1)
                        dve.wait_ge(s_kp, 1)
                        dve.tensor_copy(k_sb[:], pk).then_inc(s_ks, 1)
                        dve.wait_ge(s_len, 16)
                        link(dve.tensor_copy(len_f[:], len_i[:]))
                        dve.wait_ge(s_grid, 4)
                        link(dve.tensor_tensor(cmask[:], pos[:], bc(len_f[:], 1, KB), ALU.is_lt))
                        dve.wait_ge(s_sc0, 16)
                        for f in range(2):
                            dve.wait_ge(s_raw0[f], 16)
                            w = raw[:, f].rearrange("p a (k n) -> p (a k) n", n=P)
                            dve.tensor_tensor(w, w, bc(scale0[:, f], 2, P), ALU.mult).then_inc(s_wsc[f], 1)
                        for f in range(2):
                            dve.wait_ge(s_whg[f], 1)
                            dve.tensor_tensor(gu_lo[:, f].rearrange("p a k n -> p (a k n)"), raw[:, f, 0:2].rearrange("p a n -> p (a n)"),
                                              gu_hi[:, f].rearrange("p a k n -> p (a k n)").bitcast(F32),
                                              ALU.subtract).then_inc(s_wlg[f], 1)
                            dve.wait_ge(s_whd[f], 1)
                            dve.tensor_tensor(dn_lo[:, f], raw[:, f, 2], dn_hi[:, f].bitcast(F32), ALU.subtract).then_inc(s_wld[f], 1)

                    @block.scalar
                    def _(act):
                        act.wait_ge(s_theta, 1)
                        act.activation(trig_small[0], sm[3][:], ACT.Sin, scale=TWO_PI).then_inc(s_sin, 1)
                        act.activation(trig_small[1], sm[3][:], ACT.Sin, scale=TWO_PI / 2).then_inc(s_sin, 1)
                        act.activation(trig, theta, ACT.Sin, scale=TWO_PI).then_inc(s_sin, 1)
                        for f in range(2):
                            act.wait_ge(s_wsc[f], 1)
                            act.activation(gu_hi[:, f].rearrange("p a k n -> p (a k n)"),
                                           raw[:, f, 0:2].rearrange("p a n -> p (a n)"), ACT.Copy).then_inc(s_whg[f], 1)
                            act.activation(dn_hi[:, f], raw[:, f, 2], ACT.Copy).then_inc(s_whd[f], 1)

                    @block.tensor
                    def _(pe):
                        pe.wait_ge(s_sf, 4)
                        pe.wait_ge(s_grid, 2)
                        hb = HEADS // 2
                        for c in range(2):
                            pe.matmul(pk[:, c * hb:(c + 1) * hb, :], onehot[:], dm[:, c * hb:(c + 1) * hb, :],
                                      start=True, stop=True)
                            for h in range(c * hb, (c + 1) * hb):
                                last = pe.matmul(pk[:, h, :], S[:, h, :], Fm[:, h, :], start=False, stop=True,
                                                 skip_group_check=True)
                        last.then_inc(s_kp, 1)

            scope[0] = l0
            s_conv, s_cmul, s_yhi, s_ylo = sem("s_conv"), sem("s_cmul"), sem("s_yhi"), sem("s_ylo")
            s_x1h, s_x1l = sem("s_x1h"), sem("s_x1l")
            s_g = [sem(f"s_g{f}") for f in range(2)]
            s_u = [sem(f"s_u{f}") for f in range(2)]
            s_silu = [sem(f"s_silu{f}") for f in range(2)]
            s_mul = [sem(f"s_mul{f}") for f in range(2)]
            s_hh = [sem(f"s_hh{f}") for f in range(2)]
            s_hl = [sem(f"s_hl{f}") for f in range(2)]
            s_d = [sem(f"s_d{f}") for f in range(2)]
            s_ev = sem("s_ev")
            a_hi4, a_lo4, acc4 = by_head(a_hi), by_head(a_lo), by_head(acc)
            conv_bank = (ps_t[:], ps_gu[2])
            acc_tile = [acc4[:, :, :, t * HPT:(t + 1) * HPT] for t in range(NT)]

            with nc.Block() as block:
                @block.sync
                def _(sp):
                    def weights(c):
                        for f in range(2):
                            sp.wait_ge(s_wlg[f], c)
                            sp.wait_ge(s_wld[f], c)
                            sp.dma_start(raw[:, f].rearrange("p a n -> p (a n)"),
                                         w0[bass.ds(c * 2 + f, 1)].rearrange("a p n -> p (a n)")).then_inc(s_raw0[f], 16)

                    weights(1)
                    for t in range(1, NT):
                        sp.wait_ge(s_conv, 4 * t)
                        sp.dma_start(toep[:], bass.AP(tensor=krev.tensor, offset=t * HPT * KROW,
                                                      ap=[[1, P], [KROW, HPT], [1, L]])).then_inc(s_T, 16)
                    with sp.Fori(2, NC0) as c:
                        weights(c)

                @block.tensor
                def _(pe):
                    def conv(t):
                        pe.wait_ge(s_T, 16 * (t + 1))
                        for q in range(4):
                            j = 4 * t + q
                            bank = conv_bank[q % 2].rearrange("p (i k b) -> p i k b", i=2, k=KB)
                            if j >= 2:
                                pe.wait_ge(s_cmul, j - 1)
                            if q == 1 and t:
                                pe.wait_ge(s_silu[1], t)
                            for i in range(2):
                                hh = 2 * q + i
                                for d in range(KB):
                                    last = pe.matmul(bank[:, i, d:KB, :], toep[:, hh, L - P * (d + 1):L - P * d],
                                                     acc4[:, 0:KB - d, :, t * HPT + hh], start=(d == 0), stop=True,
                                                     skip_group_check=True)
                            last.then_inc(s_conv, 1)

                    def chunk(c, first, last_chunk):
                        for t in range(NT):
                            m = c * NT + t
                            if first:
                                conv(t)
                                pe.wait_ge(s_ylo, 4 * (t + 1))
                            for f in range(2):
                                if t == 0:
                                    pe.wait_ge(s_wlg[f], c + 1)
                                if not (first and t == 0):
                                    pe.wait_ge((s_mul, s_silu)[f][1], m)
                                for k in range(KB):
                                    mv = (a_hi4[:, k, :, t * HPT:(t + 1) * HPT], a_lo4[:, k, :, t * HPT:(t + 1) * HPT])
                                    last = mm3(pe, ps_gu[G_BANK[f]], gu_hi[:, f, 0, k], gu_lo[:, f, 0, k], *mv,
                                               start=(k == 0), stop=(k == KB - 1))
                                last.then_inc(s_g[f], 1)
                                if f:
                                    pe.wait_ge(s_silu[0], m + 1)
                                elif not (first and t == 0):
                                    pe.wait_ge(s_mul[0], m)
                                for k in range(KB):
                                    mv = (a_hi4[:, k, :, t * HPT:(t + 1) * HPT], a_lo4[:, k, :, t * HPT:(t + 1) * HPT])
                                    last = mm3(pe, ps_gu[U_BANK[f]], gu_hi[:, f, 1, k], gu_lo[:, f, 1, k], *mv,
                                               start=(k == 0), stop=(k == KB - 1))
                                last.then_inc(s_u[f], 1)
                            for f in range(2):
                                if t == 0:
                                    pe.wait_ge(s_wld[f], c + 1)
                                pe.wait_ge(s_hl[f], m + 1)
                                if f == 0 and not (first and t == 0):
                                    pe.wait_ge(s_ev, m)
                                for k in range(KB):
                                    last = mm3(pe, ps_d[:, k], dn_hi[:, f, k * P:(k + 1) * P], dn_lo[:, f, k * P:(k + 1) * P],
                                               h_hi[:, f], h_lo[:, f], start=(f == 0), stop=(f == 1), skip=True)
                                last.then_inc(s_d[f], 1)

                    chunk(0, True, False)
                    with pe.Fori(1, NC0 - 1) as c:
                        chunk(c, False, False)
                    chunk(NC0 - 1, False, True)

                @block.scalar
                def _(act):
                    def chunk(c, first, last_chunk):
                        for t in range(NT):
                            m = c * NT + t
                            if first:
                                for q in range(4):
                                    h0 = t * HPT + 2 * q
                                    act.wait_ge(s_cmul, 4 * t + q + 1)
                                    act.activation(a_hi4[:, :, :, h0:h0 + 2].rearrange("p k b h -> p h k b"),
                                                   ytmp[:, q % 2].rearrange("p h (k b) -> p h k b", k=KB), ACT.Copy).then_inc(s_yhi, 1)
                            for f in range(2):
                                act.wait_ge(s_g[f], m + 1)
                                if not (first and t == 0):
                                    act.wait_ge(s_hl[f], m)
                                act.activation(s_act[:, f], ps_gu[G_BANK[f]], ACT.Silu).then_inc(s_silu[f], 1)
                                act.wait_ge(s_mul[f], m + 1)
                                if not (first and t == 0):
                                    act.wait_ge(s_d[f], m)
                                act.activation(h_hi[:, f], s_act[:, f], ACT.Copy).then_inc(s_hh[f], 1)
                                if t == NT - 1 and not last_chunk:
                                    act.wait_ge(s_wsc[f], c + 2)
                                    act.wait_ge(s_u[f], m + 1)
                                    act.activation(gu_hi[:, f].rearrange("p a k n -> p (a k n)"),
                                                   raw[:, f, 0:2].rearrange("p a n -> p (a n)"), ACT.Copy).then_inc(s_whg[f], 1)
                            if t == NT - 1 and not last_chunk:
                                for f in range(2):
                                    act.wait_ge(s_d[f], m + 1)
                                    act.activation(dn_hi[:, f], raw[:, f, 2], ACT.Copy).then_inc(s_whd[f], 1)
                            if last_chunk:
                                act.wait_ge(s_ev, m + 1)
                                act.activation(a_hi4[:, :, :, t * HPT:(t + 1) * HPT], acc_tile[t], ACT.Copy).then_inc(s_x1h, 1)

                    chunk(0, True, False)
                    with act.Fori(1, NC0 - 1) as c:
                        chunk(c, False, False)
                    chunk(NC0 - 1, False, True)

                @block.vector
                def _(dve):
                    def low_half(t, q):
                        j = 4 * t + q
                        h0 = t * HPT + 2 * q
                        dve.wait_ge(s_yhi, j + 1)
                        hv = a_hi4[:, :, :, h0:h0 + 2].rearrange("p k b h -> p h k b").bitcast(F32)
                        dve.tensor_tensor(a_lo4[:, :, :, h0:h0 + 2].rearrange("p k b h -> p h k b"),
                                          ytmp[:, q % 2].rearrange("p h (k b) -> p h k b", k=KB), hv, ALU.subtract).then_inc(s_ylo, 1)

                    def chunk(c, first, last_chunk):
                        for t in range(NT):
                            m = c * NT + t
                            if first:
                                for q in range(4):
                                    dve.wait_ge(s_conv, 4 * t + q + 1)
                                    if 4 * t + q >= 2:
                                        dve.wait_ge(s_yhi, 4 * t + q - 1)
                                        dve.wait_ge(s_ylo, 4 * t + q - 1)
                                    dve.tensor_tensor(ytmp[:, q % 2], conv_bank[q % 2].rearrange("p (i n) -> p i n", i=2),
                                                      bc(cmask[:].rearrange("p k b -> p (k b)"), 1, 2), ALU.mult).then_inc(s_cmul, 1)
                                    if q:
                                        low_half(t, q - 1)
                                low_half(t, 3)
                            for f in range(2):
                                dve.wait_ge(s_u[f], m + 1)
                                dve.wait_ge(s_silu[f], m + 1)
                                dve.tensor_tensor(s_act[:, f], s_act[:, f], ps_gu[U_BANK[f]], ALU.mult).then_inc(s_mul[f], 1)
                                dve.wait_ge(s_hh[f], m + 1)
                                if not (first and t == 0):
                                    dve.wait_ge(s_d[f], m)
                                dve.tensor_tensor(h_lo[:, f], s_act[:, f], h_hi[:, f].bitcast(F32), ALU.subtract).then_inc(s_hl[f], 1)
                                if t == NT - 1 and not last_chunk:
                                    dve.wait_ge(s_whg[f], c + 2)
                                    dve.tensor_tensor(gu_lo[:, f].rearrange("p a k n -> p (a k n)"),
                                                      raw[:, f, 0:2].rearrange("p a n -> p (a n)"),
                                                      gu_hi[:, f].rearrange("p a k n -> p (a k n)").bitcast(F32),
                                                      ALU.subtract).then_inc(s_wlg[f], 1)
                            if t == 1 and not last_chunk:
                                for f in range(2):
                                    dve.wait_ge(s_raw0[f], c * 16 + 32)
                                    w = raw[:, f].rearrange("p a (k n) -> p (a k) n", n=P)
                                    sc = scale0[:, bass.ds(c * 2 + (2 + f), 1)].rearrange("p a c -> p (a c)")
                                    dve.tensor_tensor(w, w, bc(sc, 2, P), ALU.mult).then_inc(s_wsc[f], 1)
                            dve.wait_ge(s_d[1], m + 1)
                            dve.tensor_tensor(acc_tile[t], acc_tile[t],
                                              ps_d[:].rearrange("p k (b h) -> p k b h", h=HPT), ALU.add).then_inc(s_ev, 1)
                            if t == NT - 1 and not last_chunk:
                                for f in range(2):
                                    dve.wait_ge(s_whd[f], c + 2)
                                    dve.tensor_tensor(dn_lo[:, f], raw[:, f, 2], dn_hi[:, f].bitcast(F32),
                                                      ALU.subtract).then_inc(s_wld[f], 1)
                            if last_chunk:
                                dve.wait_ge(s_x1h, t + 1)
                                dve.tensor_tensor(a_lo4[:, :, :, t * HPT:(t + 1) * HPT], acc_tile[t],
                                                  a_hi4[:, :, :, t * HPT:(t + 1) * HPT].bitcast(F32), ALU.subtract).then_inc(s_x1l, 1)

                    chunk(0, True, False)
                    with dve.Fori(1, NC0 - 1) as c:
                        chunk(c, False, False)
                    chunk(NC0 - 1, False, True)

        with ExitStack() as l1:
            scope[0] = l1
            t_hi = sb("t_hi", [P, 2, TOK], F32R)
            t_lo = sb("t_lo", [P, 2, TOK], F32R)

            s_ar = [sem(f"s_ar{i}") for i in range(2)]
            s_ah = [sem(f"s_ah{i}") for i in range(2)]
            s_al = [sem(f"s_al{i}") for i in range(2)]
            s_tp = [sem(f"s_tp{i}") for i in range(2)]
            s_tm = [sem(f"s_tm{i}") for i in range(2)]
            s_th = [sem(f"s_th{i}") for i in range(2)]
            s_tl = [sem(f"s_tl{i}") for i in range(2)]
            s_raw1 = [sem(f"s_raw1_{f}") for f in range(2)]
            v_hg = [sem(f"v_hg{f}") for f in range(2)]
            v_lg = [sem(f"v_lg{f}") for f in range(2)]
            v_hd = [sem(f"v_hd{f}") for f in range(2)]
            v_ld = [sem(f"v_ld{f}") for f in range(2)]
            v_zero = sem("v_zero")

            with ExitStack() as pc:
                scope[0] = pc
                ar_raw = sb("ar_raw", [P, 2, GB, 2 * KB * RANK])
                ar_hi = sb("ar_hi", [P, 2, 2 * KB, P], F32R)
                ar_lo = sb("ar_lo", [P, 2, 2 * KB, P], F32R)
                tm = sb("tm", [P, 2, 2 * GT])
                tbank = (ps_t[:], ps_gu[2])

                with nc.Block() as block:
                    @block.sync
                    def _(sp):
                        for f in range(2):
                            sp.dma_start(raw[:, f].rearrange("p a n -> p (a n)"), w1[f]).then_inc(s_raw1[f], 16)
                        with sp.Fori(0, NG // 2) as i:
                            for u in range(2):
                                sp.wait_ge(s_al[u], i)
                                for j in range(GB):
                                    if True:
                                        e = sp.value_load(ix[0:1, bass.ds(i * (2 * GB) + (u * GB + j), 1)], min_val=0, max_val=EXP - 1)
                                        sp.dma_start(ar_raw[:, u, j], tab_a[bass.ds(e, 1)].rearrange("a p n -> p (a n)")).then_inc(s_ar[u], 16)

                    @block.gpsimd
                    def _(pool):
                        pool.memset(acc[:], 0.0).then_inc(v_zero, 1)

                    @block.scalar
                    def _(act):
                        with act.Fori(0, NG // 2) as i:
                            for u in range(2):
                                act.wait_ge(s_ar[u], i * (16 * GB) + 16 * GB)
                                act.wait_ge(s_tp[u], i)
                                act.activation(ar_hi[:, u].rearrange("p k (b r) -> p b k r", r=RANK),
                                               ar_raw[:, u].rearrange("p b (k r) -> p b k r", r=RANK), ACT.Copy).then_inc(s_ah[u], 1)
                                act.wait_ge(s_tm[u], i + 1)
                                act.activation(t_hi[:, :, bass.ds(i * (2 * GT) + u * GT, GT)],
                                               tm[:, u].rearrange("p (a n) -> p a n", a=2), ACT.Copy).then_inc(s_th[u], 1)
                        for f in range(2):
                            act.wait_ge(s_raw1[f], 16)
                            act.activation(gu_hi[:, f].rearrange("p a k n -> p (a k n)"),
                                           raw[:, f, 0:2].rearrange("p a n -> p (a n)"), ACT.Copy).then_inc(v_hg[f], 1)
                            act.activation(dn_hi[:, f], raw[:, f, 2], ACT.Copy).then_inc(v_hd[f], 1)

                    @block.tensor
                    def _(pe):
                        with pe.Fori(0, NG // 2) as i:
                            for u in range(2):
                                pe.wait_ge(s_al[u], i + 1)
                                pe.wait_ge(s_tm[u], i)
                                bank = tbank[u].rearrange("p (a n) -> p a n", a=2)
                                for w in range(2):
                                    for k in range(KB):
                                        at = bass.ds(i * (2 * GT) + u * GT, GT)
                                        last = mm3(pe, bank[:, w], ar_hi[:, u, 2 * k + w], ar_lo[:, u, 2 * k + w],
                                                   a_hi[:, k, at], a_lo[:, k, at], start=(k == 0), stop=(k == KB - 1), skip=True)
                                last.then_inc(s_tp[u], 1)

                    @block.vector
                    def _(dve):
                        with dve.Fori(0, NG // 2) as i:
                            for u in range(2):
                                dve.wait_ge(s_ah[u], i + 1)
                                dve.tensor_tensor(ar_lo[:, u].rearrange("p k (b r) -> p b k r", r=RANK),
                                                  ar_raw[:, u].rearrange("p b (k r) -> p b k r", r=RANK),
                                                  ar_hi[:, u].rearrange("p k (b r) -> p b k r", r=RANK).bitcast(F32),
                                                  ALU.subtract).then_inc(s_al[u], 1)
                                dve.wait_ge(s_tp[u], i + 1)
                                dve.wait_ge(s_tl[u], i)
                                dve.tensor_tensor(tm[:, u].rearrange("p (a n) -> p a n", a=2), tbank[u].rearrange("p (a n) -> p a n", a=2),
                                                  bc(lmask[:], 1, 2), ALU.mult).then_inc(s_tm[u], 1)
                                dve.wait_ge(s_th[u], i + 1)
                                at = bass.ds(i * (2 * GT) + u * GT, GT)
                                dve.tensor_tensor(t_lo[:, :, at], tm[:, u].rearrange("p (a n) -> p a n", a=2),
                                                  t_hi[:, :, at].bitcast(F32), ALU.subtract).then_inc(s_tl[u], 1)
                        for f in range(2):
                            dve.wait_ge(v_hg[f], 1)
                            dve.tensor_tensor(gu_lo[:, f].rearrange("p a k n -> p (a k n)"), raw[:, f, 0:2].rearrange("p a n -> p (a n)"),
                                              gu_hi[:, f].rearrange("p a k n -> p (a k n)").bitcast(F32),
                                              ALU.subtract).then_inc(v_lg[f], 1)
                            dve.wait_ge(v_hd[f], 1)
                            dve.tensor_tensor(dn_lo[:, f], raw[:, f, 2], dn_hi[:, f].bitcast(F32), ALU.subtract).then_inc(v_ld[f], 1)

            scope[0] = l1
            with ExitStack() as pd:
                scope[0] = pd
                BR = 2 * 2 * P
                b_raw = sb("b_raw", [P, 2, 2, 2 * P])
                b_hi = sb("b_hi", [P, 2, 2, 2 * P], F32R)
                b_lo = sb("b_lo", [P, 2, 2, 2 * P], F32R)
                ad_raw = sb("ad_raw", [P, BPT, 2 * RANK])
                ad_hi = sb("ad_hi", [P, 2, BPT * RANK], F32R)
                ad_lo = sb("ad_lo", [P, 2, BPT * RANK], F32R)
                td = sb("td", [P, TOK])
                rows = sb("rows", [P, 2, NG], I32)
                rowb = sb("rowb", [P, 2, NG], I32)
                ixr = sb("ixr", [P, NG], I32)

                r_ix, r_rb, r_row = sem("r_ix"), sem("r_rb"), sem("r_row")
                r_b = [sem(f"r_b{f}") for f in range(2)]
                r_bh = [sem(f"r_bh{f}") for f in range(2)]
                r_bl = [sem(f"r_bl{f}") for f in range(2)]
                r_turn, r_turns = sem("r_turn"), sem("r_turns")
                r_ad, r_adh, r_adl = sem("r_ad"), sem("r_adh"), sem("r_adl")
                q_g = [sem(f"q_g{f}") for f in range(2)]
                q_u = [sem(f"q_u{f}") for f in range(2)]
                q_silu = [sem(f"q_silu{f}") for f in range(2)]
                q_mul = [sem(f"q_mul{f}") for f in range(2)]
                q_hh = [sem(f"q_hh{f}") for f in range(2)]
                q_hl = [sem(f"q_hl{f}") for f in range(2)]
                q_d, q_td, q_ev, q_tev = sem("q_d"), sem("q_td"), sem("q_ev"), sem("q_tev")
                r_tdm, r_tdh, r_tdl = sem("r_tdm"), sem("r_tdh"), sem("r_tdl")
                r_bd, r_bdh, r_bdl = sem("r_bd"), sem("r_bdh"), sem("r_bdl")
                n_steps = NC1 * NT

                tdm = s_act[:, 1]
                bd_raw = raw[:, 1, 0:2]

                def lanes(t):
                    return t[:, 0:2].rearrange("p a n -> p (a n)")

                with nc.Block() as block:
                    @block.sync
                    def _(sp):
                        sp.dma_start(rowb[:].rearrange("p a g -> p (a g)"), rowbase).then_inc(r_rb, 16)
                        with nc.allow_non_contiguous_dma(reason="512 small integers"):
                            for b in range(GB):
                                sp.dma_start(ixr[b * RANK:(b + 1) * RANK, :],
                                             bass.AP(tensor=idx.tensor, offset=b, ap=[[0, RANK], [GB, NG]])).then_inc(r_ix, 16)

                        def chunk(c, nf, last_chunk):
                            for t in range(NT):
                                m = c * NT + t
                                if t == 1 and not last_chunk:
                                    for f in range(2):
                                        sp.wait_ge(v_lg[f], c + 1)
                                        sp.wait_ge(v_ld[f], c + 1)
                                        sp.dma_start(raw[:, f].rearrange("p a n -> p (a n)"),
                                                     w1[bass.ds(c * 2 + (2 + f), 1)].rearrange("a p n -> p (a n)")).then_inc(s_raw1[f], 16)
                                sp.wait_ge(s_ix, 16)
                                sp.wait_ge(r_adl, m)
                                sp.sem_inc(r_turns, 1)
                                with sp.Fori(0, BPT) as j:
                                    e = sp.value_load(ix[0:1, bass.ds(j + t * BPT, 1)], min_val=0, max_val=EXP - 1)
                                    sp.dma_start(ad_raw[:, bass.ds(j, 1)].rearrange("p a n -> p (a n)"),
                                                 tab_ad[bass.ds(c * EXP + e, 1)].rearrange("a p n -> p (a n)")).then_inc(r_ad, 16)
                                if last_chunk:
                                    if t:
                                        sp.wait_ge(r_bdl, t)
                                    for g in range(2):
                                        for b in range(GB):
                                            e = sp.value_load(ix[0:1, (2 * t + g) * GB + b:(2 * t + g) * GB + b + 1], min_val=0, max_val=EXP - 1)
                                            sp.dma_start(bd_raw[b * RANK:(b + 1) * RANK, g],
                                                         tab_bd[bass.ds(e, 1)].rearrange("a r n -> r (a n)")).then_inc(r_bd, 16)

                        with sp.Fori(0, NC1 - 1) as c:
                            chunk(c, 2, False)
                        sp.wait_ge(v_ld[1], NC1)
                        chunk(NC1 - 1, 1, True)

                    @block.gpsimd
                    def _(pool):
                        pool.memset(td[:], 0.0).then_inc(v_zero, 1)
                        pool.wait_ge(r_rb, 16)
                        pool.wait_ge(r_ix, 16 * GB)
                        r0 = pool.tensor_scalar
                        for f in range(2):
                            pool.tensor_scalar(rows[:, f], ixr[:], float(RANK), 0.0, ALU.mult, ALU.add).then_inc(r_row, 1)
                        pool.wait_ge(r_row, 2)
                        pool.tensor_tensor(rows[:], rows[:], rowb[:], ALU.add).then_inc(r_row, 1)

                        def gather(c, t, f):
                            for g in range(2):
                                pool.indirect_dma_start(
                                    out=b_raw[:, f, g], out_offset=None, in_=tab_b,
                                    in_offset=bass.IndirectOffsetOnAxis(ap=rows[:, f, 2 * t + g:2 * t + g + 1], axis=0)
                                ).then_inc(r_b[f], 16)

                        def chunk(c, nf, last_chunk):
                            pool.wait_ge(r_row, c + 3)
                            for t in range(NT):
                                for f in range(nf if t else 2):
                                    pool.wait_ge(r_row, 3)
                                    pool.wait_ge(r_bl[f], c * NT + t)
                                    pool.sem_inc(r_turn, 1)
                                    gather(c, t, f)
                            if not last_chunk:
                                pool.wait_ge(r_row, 3)
                                for f in range(2):
                                    pool.wait_ge(r_b[f], c * (32 * NT) + 32 * NT)
                                pool.sem_inc(r_turn, 1)
                                pool.tensor_scalar(rows[:], rows[:], float(2 * EXP * RANK), 0.0, ALU.add, ALU.add).then_inc(r_row, 1)

                        with pool.Fori(0, NC1 - 1) as c:
                            chunk(c, 2, False)
                        chunk(NC1 - 1, 1, True)

                    @block.tensor
                    def _(pe):
                        def chunk(c, nf, last_chunk, zero_ok):
                            for t in range(NT):
                                m = c * NT + t
                                for f in range(nf):
                                    if t == 0:
                                        pe.wait_ge(v_lg[f], c + 1)
                                    for w in range(2):
                                        if w == 0:
                                            if f:
                                                pe.wait_ge(q_silu[1], m)
                                            elif nf == 1 and t:
                                                pe.wait_ge(q_silu[0], m)
                                            else:
                                                pe.wait_ge(q_mul[1], m)
                                        elif f:
                                            pe.wait_ge(q_silu[0], m + 1)
                                        else:
                                            pe.wait_ge(q_mul[0], m)
                                        bank = ps_gu[(G_BANK, U_BANK)[w][f]]
                                        for k in range(KB):
                                            at = slice(t * TT, (t + 1) * TT)
                                            mm3(pe, bank, gu_hi[:, f, w, k], gu_lo[:, f, w, k], a_hi[:, k, at], a_lo[:, k, at],
                                                start=(k == 0), stop=(k == KB - 1))
                                        if w == 0:
                                            pe.wait_ge(r_bl[f], m + 1)
                                        for g in range(2):
                                            at = slice((2 * t + g) * GT, (2 * t + g + 1) * GT)
                                            wn = slice(w * P, (w + 1) * P)
                                            last = mm3(pe, bank[:, g * GT:(g + 1) * GT], b_hi[:, f, g, wn], b_lo[:, f, g, wn],
                                                       t_hi[:, w, at], t_lo[:, w, at], start=False, stop=True, skip=True)
                                        last.then_inc((q_g, q_u)[w][f], 1)
                                if last_chunk:
                                    td_products(t, m, nf)
                                    down(t, m, nf, c, last_chunk)
                                    pe.wait_ge(r_tdl, t + 1)
                                    pe.wait_ge(r_bdl, t + 1)
                                    for s in range(4):
                                        sl = slice(s * P, (s + 1) * P)
                                        last = mm3(pe, ps_d[:, s], h_hi[:, 1, sl], h_lo[:, 1, sl],
                                                   gu_hi2[:, s // 2], gu_lo2[:, s // 2], start=False, stop=True, skip=True)
                                    last.then_inc(q_d, 1)
                                else:
                                    down(t, m, nf, c, last_chunk)
                                    td_products(t, m, nf)

                        def down(t, m, nf, c, last_chunk):
                            for f in range(nf):
                                if t == 0:
                                    pe.wait_ge(v_ld[f], c + 1)
                                pe.wait_ge(q_hl[f], m + 1)
                                if f == 0:
                                    pe.wait_ge(q_ev, m)
                                for s in range(4):
                                    sl = slice(s * P, (s + 1) * P)
                                    last = mm3(pe, ps_d[:, s], h_hi[:, f, sl], h_lo[:, f, sl], dn_hi[:, f], dn_lo[:, f],
                                               start=(f == 0), stop=(f == nf - 1 and not last_chunk), skip=True)
                            if not last_chunk:
                                last.then_inc(q_d, 1)

                        def td_products(t, m, nf):
                            pe.wait_ge(r_adl, m + 1)
                            pe.wait_ge(q_tev, m)
                            for f in range(nf):
                                pe.wait_ge(q_hl[f], m + 1)
                                for g in range(2):
                                    last = mm3(pe, ps_t[:, g * GT:(g + 1) * GT], ad_hi[:, f, g * P:(g + 1) * P], ad_lo[:, f, g * P:(g + 1) * P],
                                               h_hi[:, f, g * GT:(g + 1) * GT], h_lo[:, f, g * GT:(g + 1) * GT],
                                               start=(f == 0 and g == 0), stop=(f == nf - 1), skip=True)
                            last.then_inc(q_td, 1)

                        gu_hi2 = gu_hi[:, 1].rearrange("p a k n -> p a (k n)")
                        gu_lo2 = gu_lo[:, 1].rearrange("p a k n -> p a (k n)")
                        with pe.Fori(0, NC1 - 1) as c:
                            chunk(c, 2, False, True)
                        chunk(NC1 - 1, 1, True, False)

                    @block.scalar
                    def _(act):
                        def b_split(f, n):
                            act.wait_ge(r_b[f], n * 32)
                            act.activation(b_hi[:, f].rearrange("p g n -> p (g n)"), b_raw[:, f].rearrange("p g n -> p (g n)"),
                                           ACT.Copy).then_inc(r_bh[f], 1)

                        def chunk(c, nf, last_chunk):
                            for t in range(NT):
                                m = c * NT + t
                                act.wait_ge(r_ad, m * (16 * BPT) + 16 * BPT)
                                act.wait_ge(q_td, m)
                                act.activation(ad_hi[:].rearrange("p f (b r) -> p b f r", r=RANK),
                                               ad_raw[:].rearrange("p b (f r) -> p b f r", r=RANK), ACT.Copy).then_inc(r_adh, 1)
                                if last_chunk:
                                    act.wait_ge(r_bd, (t + 1) * 32 * GB)
                                    if t:
                                        act.wait_ge(q_d, m)
                                    act.activation(gu_hi[:, 1].rearrange("p a k n -> p a (k n)"), bd_raw, ACT.Copy).then_inc(r_bdh, 1)
                                for f in range(nf):
                                    act.wait_ge(q_g[f], m + 1)
                                    act.wait_ge(q_hl[f], m)
                                    act.activation(s_act[:, f], ps_gu[G_BANK[f]], ACT.Silu).then_inc(q_silu[f], 1)
                                    act.wait_ge(q_mul[f], m + 1)
                                    act.wait_ge(q_d, m)
                                    act.wait_ge(q_td, m)
                                    act.activation(h_hi[:, f], s_act[:, f], ACT.Copy).then_inc(q_hh[f], 1)
                                    if not last_chunk or t < NT - 1:
                                        act.wait_ge(q_u[f], m + 1)
                                        b_split(f, m + 2)
                                    if t == NT - 1 and not last_chunk:
                                        act.wait_ge(s_raw1[f], c * 16 + 32)
                                        act.wait_ge(q_u[f], m + 1)
                                        act.activation(gu_hi[:, f].rearrange("p a k n -> p (a k n)"), lanes(raw[:, f]),
                                                       ACT.Copy).then_inc(v_hg[f], 1)
                                if t == NT - 1 and not last_chunk:
                                    for f in range(2):
                                        act.wait_ge(q_d, m + 1)
                                        act.activation(dn_hi[:, f], raw[:, f, 2], ACT.Copy).then_inc(v_hd[f], 1)
                                if last_chunk:
                                    act.wait_ge(r_tdm, t + 1)
                                    act.activation(h_hi[:, 1], tdm, ACT.Copy).then_inc(r_tdh, 1)

                        for f in range(2):
                            b_split(f, 1)
                        with act.Fori(0, NC1 - 1) as c:
                            chunk(c, 2, False)
                        chunk(NC1 - 1, 1, True)

                    @block.vector
                    def _(dve):
                        def b_split(f, n):
                            dve.wait_ge(r_bh[f], n)
                            dve.tensor_tensor(b_lo[:, f].rearrange("p g n -> p (g n)"), b_raw[:, f].rearrange("p g n -> p (g n)"),
                                              b_hi[:, f].rearrange("p g n -> p (g n)").bitcast(F32), ALU.subtract).then_inc(r_bl[f], 1)

                        def chunk(c, nf, last_chunk):
                            for t in range(NT):
                                m = c * NT + t
                                dve.wait_ge(r_adh, m + 1)
                                dve.tensor_tensor(ad_lo[:].rearrange("p f (b r) -> p b f r", r=RANK),
                                                  ad_raw[:].rearrange("p b (f r) -> p b f r", r=RANK),
                                                  ad_hi[:].rearrange("p f (b r) -> p b f r", r=RANK).bitcast(F32),
                                                  ALU.subtract).then_inc(r_adl, 1)
                                if last_chunk:
                                    dve.wait_ge(r_bdh, t + 1)
                                    dve.tensor_tensor(gu_lo[:, 1].rearrange("p a k n -> p a (k n)"), bd_raw,
                                                      gu_hi[:, 1].rearrange("p a k n -> p a (k n)").bitcast(F32),
                                                      ALU.subtract).then_inc(r_bdl, 1)
                                for f in range(nf):
                                    dve.wait_ge(q_u[f], m + 1)
                                    dve.wait_ge(q_silu[f], m + 1)
                                    dve.tensor_tensor(s_act[:, f], s_act[:, f], ps_gu[U_BANK[f]], ALU.mult).then_inc(q_mul[f], 1)
                                    dve.wait_ge(q_hh[f], m + 1)
                                    dve.wait_ge(q_d, m)
                                    dve.tensor_tensor(h_lo[:, f], s_act[:, f], h_hi[:, f].bitcast(F32), ALU.subtract).then_inc(q_hl[f], 1)
                                    if not last_chunk or t < NT - 1:
                                        b_split(f, m + 2)
                                    if t == NT - 1 and not last_chunk:
                                        dve.wait_ge(v_hg[f], c + 2)
                                        dve.tensor_tensor(gu_lo[:, f].rearrange("p a k n -> p (a k n)"), lanes(raw[:, f]),
                                                          gu_hi[:, f].rearrange("p a k n -> p (a k n)").bitcast(F32),
                                                          ALU.subtract).then_inc(v_lg[f], 1)
                                tslice = td[:, t * TT:(t + 1) * TT]
                                if last_chunk:
                                    dve.wait_ge(q_td, m + 1)
                                    dve.tensor_tensor(tslice, tslice, ps_t[:], ALU.add).then_inc(q_tev, 1)
                                    dve.wait_ge(q_tev, m + 1)
                                    if t:
                                        dve.wait_ge(r_tdl, t)
                                    dve.tensor_tensor(tdm.rearrange("p (g n) -> p g n", g=2), tslice.rearrange("p (g n) -> p g n", g=2),
                                                      bc(lmask[:], 1, 2), ALU.mult).then_inc(r_tdm, 1)
                                    dve.wait_ge(r_tdh, t + 1)
                                    dve.tensor_tensor(h_lo[:, 1], tdm, h_hi[:, 1].bitcast(F32), ALU.subtract).then_inc(r_tdl, 1)
                                dve.wait_ge(q_d, m + 1)
                                if t == 0:
                                    dve.wait_ge(v_zero, 2)
                                dve.tensor_tensor(z[:, 4 * t:4 * t + 4], z[:, 4 * t:4 * t + 4], ps_d[:], ALU.add).then_inc(q_ev, 1)
                                if not last_chunk:
                                    dve.wait_ge(q_td, m + 1)
                                    dve.tensor_tensor(tslice, tslice, ps_t[:], ALU.add).then_inc(q_tev, 1)
                                if t == NT - 1 and not last_chunk:
                                    for f in range(2):
                                        dve.wait_ge(v_hd[f], c + 2)
                                        dve.tensor_tensor(dn_lo[:, f], raw[:, f, 2], dn_hi[:, f].bitcast(F32),
                                                          ALU.subtract).then_inc(v_ld[f], 1)

                        for f in range(2):
                            b_split(f, 1)
                        with dve.Fori(0, NC1 - 1) as c:
                            chunk(c, 2, False)
                        chunk(NC1 - 1, 1, True)

        with ExitStack() as pe_scope:
            scope[0] = pe_scope
            NSUB = TOK // P
            w_sb = sb("w_sb", [P, KB, L])
            w_t = sb("w_t", [P, KB * L])
            w_q = sb("w_q", [P, KB, L], BF16)
            bias_sb = sb("bias_sb", [P, L])
            ident_b = sb("ident_b", [P, P], BF16)
            ident_r = sb("ident_r", [P, P], F32R)
            ident_f = sb("ident_f", [P, P])
            ones = sb("ones", [P, P])
            wsum = sb("wsum", [P, 1])
            wm = sb("wm", [P, 1])
            wi = sb("wi", [P, 1])
            ss = sb("ss", [P, NSUB])
            am = sb("am", [P, NSUB])
            ra = sb("ra", [P, NSUB])
            cc = sb("cc", [P, NSUB])
            dq = sb("dq", [P, NSUB])
            epsb = sb("epsb", [P, 1])
            junk = sb("junk", [P, 2, L])
            qf = sb("qf", [P, 2, L])
            qb = sb("qb", [P, 2, L], BF16)
            qT = sb("qT", [P, 2, L], BF16)
            yb = sb("yb", [P, 2, L])
            gb = sb("gb", [P, 2, L])
            o1 = sb("o1", [P, 2, L])
            o2 = sb("o2", [P, 2, L])
            e_w, e_b, e_id, e_ws, e_wp, e_wq, e_ss, e_am, e_rt, e_c = (sem(n) for n in (
                "e_w", "e_b", "e_id", "e_ws", "e_wp", "e_wq", "e_ss", "e_am", "e_rt", "e_c"))
            e_q, e_tp, e_qt, e_y, e_x, e_yb, e_gb, e_o1, e_o2 = (sem(n) for n in (
                "e_q", "e_tp", "e_qt", "e_y", "e_x", "e_yb", "e_gb", "e_o1", "e_o2"))
            e_out = [sem(f"e_out{i}") for i in range(2)]
            ps_tp = [ps_gu[i].bitcast(BF16)[:, 0:L] for i in range(2)]
            ps_y = [ps_gu[2], ps_t[:]]
            ps_x = [ps_d[:, i] for i in range(2)]
            o_rows = out.rearrange("b h n -> (b h) n")

            with nc.Block() as block:
                @block.sync
                def _(sp):
                    sp.dma_start(w_sb[:], wq).then_inc(e_w, 16)
                    sp.dma_start(bias_sb[:], bass.AP(tensor=bias.tensor, offset=0, ap=[[0, P], [1, L]])).then_inc(e_b, 16)
                    for s in range(NSUB):
                        sp.wait_ge(e_o2, s + 1)
                        sp.dma_start(o_rows[s * P:(s + 1) * P, :], o2[:, s % 2]).then_inc(e_out[s % 2], 16)
                    for i in range(2):
                        sp.wait_ge(e_out[i], 16 * (NSUB // 2))

                @block.gpsimd
                def _(pool):
                    pool.memset(epsb[:], EPS).then_inc(e_c, 1)
                    pool.memset(ones[:], 1.0).then_inc(e_id, 1)
                    pool.memset(ident_f[:], 0.0).then_inc(e_id, 1)
                    pool.wait_ge(e_id, 2)
                    pool.affine_select(out=ident_f[:], in_=ident_f[:], compare_op=ALU.not_equal, fill=1.0, base=0,
                                       pattern=[[-1, P]], channel_multiplier=1).then_inc(e_id, 1)
                    for s in range(NSUB):
                        pool.wait_ge(e_gb, s + 1)
                        pool.wait_ge(e_o1, s + 1)
                        if s >= 2:
                            pool.wait_ge(e_out[s % 2], 16 * (s // 2))
                        pool.tensor_tensor(o2[:, s % 2], o1[:, s % 2], gb[:, s % 2], ALU.add).then_inc(e_o2, 1)

                @block.vector
                def _(dve):
                    def link(ins):
                        chain[0] += 1
                        ins.then_inc(s_chain, 1)
                        dve.wait_ge(s_chain, chain[0])

                    dve.wait_ge(e_id, 3)
                    dve.tensor_copy(ident_b[:], ident_f[:]).then_inc(e_id, 1)
                    dve.tensor_copy(ident_r[:], ident_f[:]).then_inc(e_id, 1)
                    dve.wait_ge(e_w, 16)
                    wf = w_sb[:].rearrange("p k n -> p (k n)")
                    dve.tensor_reduce(wsum[:], wf, AX.X, ALU.add, apply_absolute_value=True).then_inc(e_ws, 1)
                    for s in range(NSUB):
                        dve.tensor_reduce(am[:, s:s + 1], z[:, s], AX.X, ALU.max, apply_absolute_value=True).then_inc(e_am, 1)
                    dve.wait_ge(e_wp, 1)
                    link(dve.tensor_scalar(wm[:], ps_d[:, 3, 0:1], 1.0 / (L * L), EPS, ALU.mult, ALU.max))
                    link(dve.reciprocal(wi[:], wm[:]))
                    link(dve.tensor_scalar(w_t[:], wf, wi[:], MAGIC, ALU.mult, ALU.add))
                    link(dve.tensor_scalar(w_t[:], w_t[:], MAGIC, 1.0, ALU.subtract, ALU.min))
                    dve.tensor_scalar(w_q[:].rearrange("p k n -> p (k n)"), w_t[:], -1.0, None, ALU.max).then_inc(e_wq, 1)
                    dve.wait_ge(e_rt, 1)
                    link(dve.reciprocal(ra[:], ra[:]))
                    dve.wait_ge(e_am, NSUB)
                    link(dve.tensor_tensor(am[:], am[:], ra[:], ALU.mult))
                    link(dve.tensor_scalar(am[:], am[:], EPS, None, ALU.max))
                    link(dve.reciprocal(cc[:], am[:]))
                    link(dve.scalar_tensor_tensor(out=cc[:], in0=cc[:], scalar=127.0, in1=ra[:], op0=ALU.mult, op1=ALU.mult))
                    link(dve.tensor_scalar(dq[:], am[:], wm[:], 1.0 / 127, ALU.mult, ALU.mult))

                    def quant(s):
                        i = s % 2
                        link(dve.tensor_scalar(qf[:, i], z[:, s], cc[:, s:s + 1], MAGIC, ALU.mult, ALU.add))
                        link(dve.tensor_scalar(qf[:, i], qf[:, i], MAGIC, 127.0, ALU.subtract, ALU.min))
                        if s >= 2:
                            dve.wait_ge(e_tp, s - 1)
                        dve.tensor_scalar(qb[:, i], qf[:, i], -128.0, None, ALU.max).then_inc(e_q, 1)

                    quant(0)
                    for s in range(NSUB):
                        i = s % 2
                        if s + 1 < NSUB:
                            quant(s + 1)
                        if s == 0:
                            dve.wait_ge(e_b, 16)
                        dve.wait_ge(e_x, s + 1)
                        if s >= 2:
                            dve.wait_ge(e_o2, s - 1)
                        dve.tensor_tensor(o1[:, i], z[:, s], ps_x[i], ALU.add).then_inc(e_o1, 1)
                        dve.wait_ge(e_y, s + 1)
                        if s >= 2:
                            dve.wait_ge(e_gb, s - 1)
                        dve.scalar_tensor_tensor(out=yb[:, i], in0=ps_y[i], scalar=dq[:, s:s + 1], in1=bias_sb[:],
                                                 op0=ALU.mult, op1=ALU.add).then_inc(e_yb, 1)

                @block.scalar
                def _(act):
                    for s in range(NSUB):
                        if s >= 2:
                            act.wait_ge(e_ss, s - 1)
                        act.activation(junk[:, s % 2], z[:, s], ACT.Square, accum_out=ss[:, s:s + 1]).then_inc(e_ss, 1)
                    act.wait_ge(e_ss, NSUB)
                    act.wait_ge(e_c, 1)
                    act.activation(ra[:], ss[:], ACT.Sqrt, scale=1.0 / L, bias=epsb[:]).then_inc(e_rt, 1)
                    for s in range(NSUB):
                        i = s % 2
                        act.wait_ge(e_tp, s + 1)
                        if s >= 2:
                            act.wait_ge(e_y, s - 1)
                        act.activation(qT[:, i], ps_tp[i], ACT.Copy).then_inc(e_qt, 1)
                        act.wait_ge(e_yb, s + 1)
                        if s >= 2:
                            act.wait_ge(e_o2, s - 1)
                        act.activation(gb[:, i], yb[:, i], ACT.Gelu).then_inc(e_gb, 1)

                @block.tensor
                def _(pe):
                    pe.wait_ge(e_ws, 1)
                    pe.wait_ge(e_id, 5)
                    pe.matmul(ps_d[:, 3, 0:1], ones[:], wsum[:], start=True, stop=True).then_inc(e_wp, 1)
                    for s in range(NSUB + 1):
                        if s < NSUB:
                            i = s % 2
                            pe.wait_ge(e_q, s + 1)
                            if s >= 2:
                                pe.wait_ge(e_qt, s - 1)
                            for k in range(KB):
                                last = pe.transpose(ps_tp[i][:, k * P:(k + 1) * P], qb[:, i, k * P:(k + 1) * P], ident_b[:])
                            last.then_inc(e_tp, 1)
                            if s >= 2:
                                pe.wait_ge(e_o1, s - 1)
                            for k in range(KB):
                                sl = slice(s * P, (s + 1) * P)
                                pe.matmul(ps_x[i][:, k * P:(k + 1) * P], a_hi[:, k, sl], ident_r[:], start=True, stop=False,
                                          skip_group_check=True)
                                last = pe.matmul(ps_x[i][:, k * P:(k + 1) * P], a_lo[:, k, sl], ident_r[:], start=False, stop=True,
                                                 skip_group_check=True)
                            last.then_inc(e_x, 1)
                        if s:
                            v = s - 1
                            i = v % 2
                            pe.wait_ge(e_qt, v + 1)
                            if v == 0:
                                pe.wait_ge(e_wq, 1)
                            if v >= 2:
                                pe.wait_ge(e_yb, v - 1)
                            for k in range(KB):
                                last = pe.matmul(ps_y[i], qT[:, i, k * P:(k + 1) * P], w_q[:, k], start=(k == 0), stop=(k == KB - 1))
                            last.then_inc(e_y, 1)


def kernel(**inputs):
    import concourse.bacc as bacc
    from concourse.bass_utils import run_bass_kernel_spmd

    a = {k: np.asarray(v) for k, v in inputs.items()}

    def stack2(v):
        return np.concatenate([v, v], axis=0)

    def padded(v, axis, n):
        shape = list(v.shape)
        shape[axis] = n
        w = np.zeros(shape, v.dtype)
        w[tuple(slice(0, k) for k in v.shape)] = v
        return w

    def by_block(w, rows_reversed):
        w = w.reshape(-1, P, KB, P)
        if rows_reversed:
            w = w[..., ::-1]
        return w.transpose(0, 3, 2, 1).reshape(-1, P, KB * P)

    def slots(gate, up, down, rows_reversed):
        return np.stack([by_block(gate, rows_reversed), by_block(up, rows_reversed),
                         down.reshape(L, -1, P).transpose(1, 2, 0)], axis=2).reshape(-1, P, 3 * L)

    lay = {
        "x_t": a["x"].reshape(TOK, L).T.reshape(KB, P, TOK).transpose(1, 0, 2),
        "par": stack2(np.stack([np.broadcast_to(a["L0_cond_log_dt"][None, :], (NSTATE, HEADS)),
                                a["L0_cond_log_A_real"].T, a["L0_cond_A_imag"].T,
                                a["L0_cond_C"][..., 0].T, a["L0_cond_C"][..., 1].T], axis=1)),
        "d_row": a["L0_cond_D"][None, :],
        "length": a["itok_B_78_3631"],
        "idx": a["itok_B_2_6"][None, :],
        "w0": slots(a["L0_ffn_w1"], a["L0_ffn_w3"], a["L0_ffn_w2"], True),
        "sc0": np.concatenate([a["L0_ffn_w1_scale"], a["L0_ffn_w3_scale"], a["L0_ffn_w2_scale"].T], axis=1),
        "w1": slots(padded(a["L1_cond_W_gate"], 0, 2 * NC1 * P), padded(a["L1_cond_W_up"], 0, 2 * NC1 * P),
                    padded(a["L1_cond_W_down"], 1, 2 * NC1 * P), False),
        "tab_a": np.stack([a["L1_cond_A_gate"][0], a["L1_cond_A_up"][0]], axis=1)
                 .reshape(EXP, 2, RANK, KB, P).transpose(0, 4, 3, 1, 2).reshape(EXP, P, KB * 2 * RANK),
        "tab_b": padded(np.stack([a["L1_cond_B_gate"][0], a["L1_cond_B_up"][0]], axis=1), 2, 2 * NC1 * P)
                 .reshape(EXP, 2, 2 * NC1, P, RANK).transpose(2, 0, 4, 1, 3).reshape(2 * NC1 * EXP * RANK, 2 * P),
        "tab_ad": padded(a["L1_cond_A_down"][0], 2, 2 * NC1 * P)
                  .reshape(EXP, RANK, NC1, 2, P).transpose(2, 0, 4, 3, 1).reshape(NC1 * EXP, P, 2 * RANK),
        "tab_bd": a["L1_cond_B_down"][0].transpose(0, 2, 1),
        "wq": a["L1_ffn_W"].T.reshape(KB, P, L).transpose(1, 0, 2),
        "bias": a["L1_ffn_b"][None, :],
        "rowbase": np.repeat((np.arange(P)[:, None] % RANK + EXP * RANK * np.arange(2)[None, :]).astype(np.int32), NG, axis=1),
    }
    nc = bacc.Bacc("TRN2", target_bir_lowering=False, num_devices=1)
    arrays, args = {}, []
    for name, v in lay.items():
        v = np.ascontiguousarray(v)
        arrays["in_" + name] = v
        args.append(nc.dram_tensor("in_" + name, v.shape, mybir.dt.from_np(v.dtype), kind="ExternalInput").ap())
    args.append(nc.dram_tensor("out_0", (BATCH, HEADS, L), F32, kind="ExternalOutput").ap())
    build(nc, *args)
    r = run_bass_kernel_spmd(nc, [arrays], core_ids=[0])
    return r.results[0]["out_0"]
```

```python
from contextlib import ExitStack

import numpy as np

import concourse.bass as bass
from concourse import mybir

F32 = mybir.dt.float32
F32R = mybir.dt.float32r
BF16 = mybir.dt.bfloat16
I32 = mybir.dt.int32
ALU = mybir.AluOpType
ACT = mybir.ActivationFunctionType
AX = mybir.AxisListType

P = 128
BATCH, HEADS, L = 64, 32, 512
TOK = BATCH * HEADS
KB = L // P
NT = 4
TT = TOK // NT
HPT = HEADS // NT
BPT = BATCH // NT
F0, F1 = 1792, 1376
NF0 = F0 // P
NF1 = -(-F1 // P)
NC0 = NF0 // 2
NC1 = -(-NF1 // 2)
EXP, RANK = 16, 16
GB = P // RANK
NG = BATCH // GB
GT = GB * HEADS
NSTATE = 64
NA, NB = 16, 32
KROW = L + P
MAGIC = float(3 << 22)
LN2_HI, LN2_LO = 0.693359375, -2.12194440e-4
LOG2E = 1.4426950408889634
TWO_PI = 6.283185
EPS = 1e-5


def bc(ap, dim, n):
    ap = ap.unsqueeze(dim)
    shape = list(ap.shape)
    shape[dim] = n
    return ap.to_broadcast(shape)


def build(nc, x_t, par, d_row, length, idx, w0, sc0, w1, tab_a, tab_l, tab_bd, wq, bias, rowbase, out):
    with ExitStack() as top:
        scope = [top]

        def sb(name, shape, dt=F32):
            return scope[0].enter_context(nc.sbuf_tensor(name, shape, dt))

        def sem(name):
            return top.enter_context(nc.semaphore(name))

        krev = nc.dram_tensor("krev", (HEADS, KROW), F32, kind="Internal").ap()

        ps_gu = [top.enter_context(nc.psum_tensor(f"ps_gu{i}", [P, 512], F32))[:] for i in range(3)]
        ps_d = top.enter_context(nc.psum_tensor("ps_d", [P, 4, 512], F32))
        ps_t = top.enter_context(nc.psum_tensor("ps_t", [P, 512], F32))
        G_BANK, U_BANK = (0, 2), (1, 0)

        acc = sb("acc", [P, KB, TOK])
        a_hi = sb("a_hi", [P, KB, TOK], F32R)
        a_lo = sb("a_lo", [P, KB, TOK], F32R)
        gu_hi = sb("gu_hi", [P, 2, 2, KB, P], F32R)
        gu_lo = sb("gu_lo", [P, 2, 2, KB, P], F32R)
        dn_hi = sb("dn_hi", [P, 2, L], F32R)
        dn_lo = sb("dn_lo", [P, 2, L], F32R)
        raw = sb("raw", [P, 2, 3, L])
        s_act = sb("s_act", [P, 2, TT])
        h_hi = sb("h_hi", [P, 2, TT], F32R)
        h_lo = sb("h_lo", [P, 2, TT], F32R)
        lmask = sb("lmask", [P, GT])
        ident_f = sb("ident_f", [P, P])
        rows0 = sb("rows0", [P, NG], I32)
        rows = sb("rows", [P, NG], I32)
        z = acc[:].rearrange("p k t -> p (k t)").rearrange("p (s n) -> p s n", n=L)

        chain = [0]
        s_chain = sem("s_chain")

        def by_head(t):
            return t[:].rearrange("p k (b h) -> p k b h", h=HEADS)

        def mm3(pe, out_ap, st_hi, st_lo, mv_hi, mv_lo, start, stop, skip=False):
            pe.matmul(out_ap, st_hi, mv_hi, start=start, stop=False, skip_group_check=skip)
            pe.matmul(out_ap, st_hi, mv_lo, start=False, stop=False, skip_group_check=skip)
            return pe.matmul(out_ap, st_lo, mv_hi, start=False, stop=stop, skip_group_check=skip)

        s_par, s_drow, s_len, s_ix, s_rb, s_id = (sem(n) for n in ("s_par", "s_drow", "s_len", "s_ix", "s_rb", "s_id"))
        r_row, r_next = sem("r_row"), sem("r_next")
        s_x = sem("s_x")
        s_raw0 = [sem(f"s_raw0_{f}") for f in range(2)]
        s_sc0 = sem("s_sc0")
        s_grid, s_sin, s_theta, s_sf, s_kp, s_ks, s_kw, s_kz = (sem(n) for n in (
            "s_grid", "s_sin", "s_theta", "s_sf", "s_kp", "s_ks", "s_kw", "s_kz"))
        s_wsc = [sem(f"s_wsc{f}") for f in range(2)]
        s_whg = [sem(f"s_whg{f}") for f in range(2)]
        s_wlg = [sem(f"s_wlg{f}") for f in range(2)]
        s_whd = [sem(f"s_whd{f}") for f in range(2)]
        s_wld = [sem(f"s_wld{f}") for f in range(2)]
        s_T = sem("s_T")

        with ExitStack() as l0:
            scope[0] = l0
            scale0 = sb("scale0", [P, NF0, 12])
            cmask = sb("cmask", [P, KB, BATCH])
            toep = sb("toep", [P, HPT, L])
            ytmp = sb("ytmp", [P, 2, 2, KB * BATCH])

            with ExitStack() as pa:
                scope[0] = pa
                par_sb = sb("par_sb", [P, 5, HEADS])
                drow = sb("drow", [1, HEADS])
                ixr = sb("ixr", [P, NG], I32)
                rowb = sb("rowb", [P, NG], I32)
                len_i = sb("len_i", [P, BATCH], I32)
                len_f = sb("len_f", [P, BATCH])
                pos = sb("pos", [P, KB, BATCH])
                pow2 = sb("pow2", [P, 9])
                lgrid = sb("lgrid", [P, 64])
                phase = sb("phase", [P, 64])
                dm = sb("dm", [1, HEADS, NB])
                onehot = sb("onehot", [1, NA])
                zero = sb("zero", [HEADS, P])
                k_sb = sb("k_sb", [NA, HEADS, NB])
                e2 = sb("e2", [P, 2, HEADS])
                sm = [sb(f"sm{i}", [P, HEADS]) for i in range(16)]
                pin = sb("pin", [P, 9, HEADS])
                pw = sb("pw", [P, 9, HEADS])
                tmp = [sb(f"tmp{i}", [P, 9 * HEADS]) for i in range(4)]
                kint = sb("kint", [P, 9 * HEADS], I32)
                mag = sb("mag", [P, HEADS, NA + NB])
                theta = toep[:, 0:4].rearrange("p a n -> p (a n)").rearrange("p (h n) -> p h n", n=64)
                trig = toep[:, 4:8].rearrange("p a n -> p (a n)").rearrange("p (h n) -> p h n", n=64)
                rnd = trig
                S = sb("S", [P, HEADS, NA])
                S2 = sb("S2", [P, HEADS, NA])
                Fm = sb("Fm", [P, HEADS, NB])
                trig_small = (sb("sin1", [P, HEADS])[:], sb("sin2", [P, HEADS])[:])
                pk = ps_d[0:NA, 0:2, :].rearrange("a c (h b) -> a (c h) b", b=NB)

                with nc.Block() as block:
                    @block.sync
                    def _(sp):
                        sp.dma_start(par_sb[:], par).then_inc(s_par, 16)
                        sp.dma_start(drow[:], d_row).then_inc(s_drow, 16)
                        sp.dma_start(len_i[:], bass.AP(tensor=length.tensor, offset=0, ap=[[0, P], [1, BATCH]])).then_inc(s_len, 16)
                        sp.dma_start(scale0[:].rearrange("p f c -> p (f c)"),
                                     bass.AP(tensor=sc0.tensor, offset=0, ap=[[0, P], [1, NF0 * 12]])).then_inc(s_sc0, 16)
                        for f in range(2):
                            sp.dma_start(raw[:, f].rearrange("p a n -> p (a n)"), w0[f]).then_inc(s_raw0[f], 16)
                        sp.dma_start(acc[:], x_t).then_inc(s_x, 16)
                        sp.dma_start(rowb[:], rowbase).then_inc(s_rb, 16)
                        with nc.allow_non_contiguous_dma(reason="512 small integers"):
                            for b in range(GB):
                                sp.dma_start(ixr[b * RANK:(b + 1) * RANK, :],
                                             bass.AP(tensor=idx.tensor, offset=b, ap=[[0, RANK], [GB, NG]])).then_inc(s_ix, 16)
                        sp.wait_ge(s_grid, 1)
                        sp.dma_start(krev[:, L:KROW], zero[:]).then_inc(s_kz, 16)
                        sp.wait_ge(s_ks, 1)
                        sp.dma_start(krev[:, 0:L].rearrange("h (a b) -> a h b", b=NB), k_sb[:]).then_inc(s_kw, 16)
                        sp.wait_ge(s_kw, 16)
                        sp.wait_ge(s_kz, 16)
                        sp.dma_start(toep[:], bass.AP(tensor=krev.tensor, offset=0,
                                                      ap=[[1, P], [KROW, HPT], [1, L]])).then_inc(s_T, 16)

                    @block.gpsimd
                    def _(pool):
                        pool.memset(zero[:], 0.0).then_inc(s_grid, 1)
                        pool.memset(dm[:], 0.0)
                        pool.memset(onehot[:], 0.0)
                        for k in range(9):
                            pool.memset(pow2[:, k:k + 1], float(1 << k))
                        pool.memset(phase[:, 0:NA], 0.25)
                        pool.memset(phase[:, NA:2 * NA], 0.0)
                        pool.memset(phase[:, 2 * NA:64], 0.25).then_inc(s_grid, 1)
                        pool.iota(lgrid[:, 0:2 * NA], [[0, 2], [-NB, NA]], base=NB * (NA - 1), channel_multiplier=0,
                                  allow_small_or_imprecise_dtypes=True)
                        pool.iota(lgrid[:, 2 * NA:64], [[-1, NB]], base=NB - 1, channel_multiplier=0,
                                  allow_small_or_imprecise_dtypes=True).then_inc(s_grid, 1)
                        pool.iota(pos[:], [[P, KB], [0, BATCH]], base=P - 1, channel_multiplier=-1,
                                  allow_small_or_imprecise_dtypes=True).then_inc(s_grid, 1)
                        pool.memset(lmask[:], 0.5).then_inc(s_grid, 1)
                        pool.wait_ge(s_grid, 5)
                        lm = lmask[:].rearrange("p (b h) -> p b h", h=HEADS)
                        pool.affine_select(out=lm, in_=lm, compare_op=ALU.is_ge, fill=0.0, base=0,
                                           pattern=[[-RANK, GB], [0, HEADS]], channel_multiplier=1).then_inc(s_grid, 1)
                        pool.wait_ge(s_grid, 6)
                        pool.affine_select(out=lm, in_=lm, compare_op=ALU.is_ge, fill=0.0, base=RANK - 1,
                                           pattern=[[RANK, GB], [0, HEADS]], channel_multiplier=-1).then_inc(s_grid, 1)
                        pool.memset(ident_f[:], 0.0).then_inc(s_id, 1)
                        pool.wait_ge(s_id, 1)
                        pool.affine_select(out=ident_f[:], in_=ident_f[:], compare_op=ALU.not_equal, fill=1.0, base=0,
                                           pattern=[[-1, P]], channel_multiplier=1).then_inc(s_id, 1)
                        pool.wait_ge(s_ix, 16 * GB)
                        pool.wait_ge(s_rb, 16)
                        pool.tensor_scalar(ixr[:], ixr[:], float(RANK), 0.0, ALU.mult, ALU.add).then_inc(r_row, 1)
                        pool.wait_ge(r_row, 1)
                        pool.tensor_tensor(rows0[:], ixr[:], rowb[:], ALU.add).then_inc(r_row, 1)
                        pool.tensor_tensor(rows[:], ixr[:], rowb[:], ALU.add).then_inc(r_row, 1)

                    @block.vector
                    def _(dve):
                        def link(ins):
                            chain[0] += 1
                            ins.then_inc(s_chain, 1)
                            dve.wait_ge(s_chain, chain[0])

                        def ts(o, i, a, b, op0, op1=None):
                            link(dve.tensor_scalar(o, i, a, b, op0, op1) if op1 is not None
                                 else dve.tensor_scalar(o, i, a, None, op0))

                        def tt(o, i, j, op):
                            link(dve.tensor_tensor(o, i, j, op))

                        def stt(o, i, s, j, op0, op1):
                            link(dve.scalar_tensor_tensor(out=o, in0=i, scalar=s, in1=j, op0=op0, op1=op1))

                        def poly_expm1(p, r):
                            ts(p, r, 1.0 / 5040, None, ALU.mult)
                            for c in (1.0 / 720, 1.0 / 120, 1.0 / 24, 1.0 / 6, 0.5, 1.0):
                                stt(p, p, c, r, ALU.add, ALU.mult)

                        def exp32(o, i, n):
                            xc, k, r, p = (t[:, 0:n] for t in tmp)
                            ki = kint[:, 0:n]
                            ts(xc, i, -87.0, 88.0, ALU.max, ALU.min)
                            ts(k, xc, LOG2E, MAGIC, ALU.mult, ALU.add)
                            ts(k, k, MAGIC, None, ALU.subtract)
                            stt(r, k, -LN2_HI, xc, ALU.mult, ALU.add)
                            stt(r, k, -LN2_LO, r, ALU.mult, ALU.add)
                            poly_expm1(p, r)
                            ts(ki, k, 127.0, float(1 << 23), ALU.add, ALU.mult)
                            stt(o, p, 1.0, ki.bitcast(F32), ALU.add, ALU.mult)

                        dve.wait_ge(s_par, 16)
                        exp32(e2[:].rearrange("p a h -> p (a h)"), par_sb[:, 0:2].rearrange("p a h -> p (a h)"), 2 * HEADS)
                        dt, ea = e2[:, 0], e2[:, 1]
                        ai_in, c_re, c_im = par_sb[:, 2], par_sb[:, 3], par_sb[:, 4]
                        ar, ai, ut, r0, em, y, nr, ni, den, wr, wi, cr, ci, c1, c2, t0 = (t[:] for t in sm)
                        stt(ar, ea, -1.0, dt, ALU.mult, ALU.mult)
                        tt(ai, ai_in, dt, ALU.mult)
                        ts(ut, ai, 0.15915494309189535, None, ALU.mult)
                        ts(r0, ut, MAGIC, MAGIC, ALU.add, ALU.subtract)
                        tt(r0, ut, r0, ALU.subtract)
                        dve.wait_ge(s_grid, 3)
                        link(dve.memset(phase[64:P, 2 * NA:64], 0.0))
                        tt(theta, bc(r0, 2, 64), bc(lgrid[:], 1, HEADS), ALU.mult)
                        tt(theta, theta, bc(phase[:], 1, HEADS), ALU.add)
                        ts(rnd, theta, MAGIC, MAGIC, ALU.add, ALU.subtract)
                        dve.tensor_tensor(theta, theta, rnd, ALU.subtract).then_inc(s_theta, 1)
                        tt(pin[:], bc(ar, 1, 9), bc(pow2[:], 2, HEADS), ALU.mult)
                        exp32(pw[:].rearrange("p a h -> p (a h)"), pin[:].rearrange("p a h -> p (a h)"), 9 * HEADS)
                        link(dve.memset(mag[:, :, NA - 1:NA], 1.0))
                        link(dve.memset(mag[:, :, NA + NB - 1:NA + NB], 1.0))
                        for k in range(5):
                            n, e = 1 << k, NA + NB
                            tt(mag[:, :, e - 2 * n:e - n], mag[:, :, e - n:e], bc(pw[:, k], 2, n), ALU.mult)
                        for k in range(4):
                            n, e = 1 << k, NA
                            tt(mag[:, :, e - 2 * n:e - n], mag[:, :, e - n:e], bc(pw[:, 5 + k], 2, n), ALU.mult)
                        ts(y, ar, -60.0, 1.0 / 64, ALU.max, ALU.mult)
                        poly_expm1(em, y)
                        for _ in range(6):
                            stt(em, em, 2.0, em, ALU.add, ALU.mult)
                        dve.wait_ge(s_sin, 2)
                        sn, sh = trig_small[0], trig_small[1]
                        tt(t0, sh, sh, ALU.mult)
                        ts(t0, t0, 2.0, None, ALU.mult)
                        tt(nr, em, t0, ALU.mult)
                        tt(nr, em, nr, ALU.subtract)
                        tt(nr, nr, t0, ALU.subtract)
                        stt(ni, em, 1.0, sn, ALU.add, ALU.mult)
                        tt(den, ea, ea, ALU.mult)
                        tt(t0, ai_in, ai_in, ALU.mult)
                        tt(den, den, t0, ALU.add)
                        link(dve.reciprocal(den, den))
                        tt(wr, ni, ai_in, ALU.mult)
                        tt(t0, nr, ea, ALU.mult)
                        tt(wr, wr, t0, ALU.subtract)
                        tt(wr, wr, den, ALU.mult)
                        tt(wi, ni, ea, ALU.mult)
                        tt(t0, nr, ai_in, ALU.mult)
                        tt(wi, wi, t0, ALU.add)
                        stt(wi, wi, -1.0, den, ALU.mult, ALU.mult)
                        tt(cr, c_re, wr, ALU.mult)
                        tt(t0, c_im, wi, ALU.mult)
                        tt(cr, cr, t0, ALU.subtract)
                        tt(ci, c_re, wi, ALU.mult)
                        tt(t0, c_im, wr, ALU.mult)
                        tt(ci, ci, t0, ALU.add)
                        ts(c1[0:64], cr[0:64], 2.0, None, ALU.mult)
                        ts(c1[64:P], ci[64:P], -2.0, None, ALU.mult)
                        ts(c2[0:64], ci[0:64], -2.0, None, ALU.mult)
                        ts(c2[64:P], cr[64:P], -2.0, None, ALU.mult)
                        dve.wait_ge(s_sin, 3)
                        tt(S[:], bc(c1, 2, NA), trig[:, :, 0:NA], ALU.mult)
                        tt(S2[:], bc(c2, 2, NA), trig[:, :, NA:2 * NA], ALU.mult)
                        tt(S[:], S[:], S2[:], ALU.add)
                        dve.tensor_tensor(S[:], S[:], mag[:, :, 0:NA], ALU.mult).then_inc(s_sf, 1)
                        dve.tensor_tensor(Fm[:], trig[:, :, 2 * NA:64], mag[:, :, NA:NA + NB], ALU.mult).then_inc(s_sf, 1)
                        dve.wait_ge(s_drow, 16)
                        dve.tensor_copy(dm[:, :, NB - 1], drow[:]).then_inc(s_sf, 1)
                        dve.memset(onehot[:, NA - 1:NA], 1.0).then_inc(s_sf, 1)
                        dve.wait_ge(s_kp, 1)
                        dve.tensor_copy(k_sb[:], pk).then_inc(s_ks, 1)
                        dve.wait_ge(s_len, 16)
                        link(dve.tensor_copy(len_f[:], len_i[:]))
                        dve.wait_ge(s_grid, 4)
                        link(dve.tensor_tensor(cmask[:], pos[:], bc(len_f[:], 1, KB), ALU.is_lt))
                        dve.wait_ge(s_sc0, 16)
                        for f in range(2):
                            dve.wait_ge(s_raw0[f], 16)
                            w = raw[:, f].rearrange("p a (k n) -> p (a k) n", n=P)
                            dve.tensor_tensor(w, w, bc(scale0[:, f], 2, P), ALU.mult).then_inc(s_wsc[f], 1)
                        for f in range(2):
                            dve.wait_ge(s_whg[f], 1)
                            dve.tensor_tensor(gu_lo[:, f].rearrange("p a k n -> p (a k n)"), raw[:, f, 0:2].rearrange("p a n -> p (a n)"),
                                              gu_hi[:, f].rearrange("p a k n -> p (a k n)").bitcast(F32),
                                              ALU.subtract).then_inc(s_wlg[f], 1)
                            dve.wait_ge(s_whd[f], 1)
                            dve.tensor_tensor(dn_lo[:, f], raw[:, f, 2], dn_hi[:, f].bitcast(F32), ALU.subtract).then_inc(s_wld[f], 1)

                    @block.scalar
                    def _(act):
                        act.wait_ge(s_theta, 1)
                        act.activation(trig_small[0], sm[3][:], ACT.Sin, scale=TWO_PI).then_inc(s_sin, 1)
                        act.activation(trig_small[1], sm[3][:], ACT.Sin, scale=TWO_PI / 2).then_inc(s_sin, 1)
                        act.activation(trig, theta, ACT.Sin, scale=TWO_PI).then_inc(s_sin, 1)
                        for f in range(2):
                            act.wait_ge(s_wsc[f], 1)
                            act.activation(gu_hi[:, f].rearrange("p a k n -> p (a k n)"),
                                           raw[:, f, 0:2].rearrange("p a n -> p (a n)"), ACT.Copy).then_inc(s_whg[f], 1)
                            act.activation(dn_hi[:, f], raw[:, f, 2], ACT.Copy).then_inc(s_whd[f], 1)

                    @block.tensor
                    def _(pe):
                        pe.wait_ge(s_sf, 4)
                        pe.wait_ge(s_grid, 2)
                        hb = HEADS // 2
                        for c in range(2):
                            pe.matmul(pk[:, c * hb:(c + 1) * hb, :], onehot[:], dm[:, c * hb:(c + 1) * hb, :],
                                      start=True, stop=True)
                            for h in range(c * hb, (c + 1) * hb):
                                last = pe.matmul(pk[:, h, :], S[:, h, :], Fm[:, h, :], start=False, stop=True,
                                                 skip_group_check=True)
                        last.then_inc(s_kp, 1)

            scope[0] = l0
            s_conv, s_cmul, s_yhi, s_ylo = sem("s_conv"), sem("s_cmul"), sem("s_yhi"), sem("s_ylo")
            s_x1h, s_x1l = sem("s_x1h"), sem("s_x1l")
            s_g = [sem(f"s_g{f}") for f in range(2)]
            s_u = [sem(f"s_u{f}") for f in range(2)]
            s_silu = [sem(f"s_silu{f}") for f in range(2)]
            s_mul = [sem(f"s_mul{f}") for f in range(2)]
            s_hh = [sem(f"s_hh{f}") for f in range(2)]
            s_hl = [sem(f"s_hl{f}") for f in range(2)]
            s_d = [sem(f"s_d{f}") for f in range(2)]
            s_ev = sem("s_ev")
            a_hi4, a_lo4, acc4 = by_head(a_hi), by_head(a_lo), by_head(acc)
            conv_bank = (ps_t[:], ps_gu[2])
            acc_tile = [acc4[:, :, :, t * HPT:(t + 1) * HPT] for t in range(NT)]

            with nc.Block() as block:
                @block.sync
                def _(sp):
                    def weights(c):
                        for f in range(2):
                            sp.wait_ge(s_wlg[f], c)
                            sp.wait_ge(s_wld[f], c)
                            sp.dma_start(raw[:, f].rearrange("p a n -> p (a n)"),
                                         w0[bass.ds(c * 2 + f, 1)].rearrange("a p n -> p (a n)")).then_inc(s_raw0[f], 16)

                    weights(1)
                    for t in range(1, NT):
                        sp.wait_ge(s_conv, 4 * t)
                        sp.dma_start(toep[:], bass.AP(tensor=krev.tensor, offset=t * HPT * KROW,
                                                      ap=[[1, P], [KROW, HPT], [1, L]])).then_inc(s_T, 16)
                    with sp.Fori(2, NC0) as c:
                        weights(c)

                @block.tensor
                def _(pe):
                    def conv(t):
                        pe.wait_ge(s_T, 16 * (t + 1))
                        for q in range(4):
                            j = 4 * t + q
                            bank = conv_bank[q % 2].rearrange("p (i k b) -> p i k b", i=2, k=KB)
                            if j >= 2:
                                pe.wait_ge(s_cmul, j - 1)
                            if q == 1 and t:
                                pe.wait_ge(s_silu[1], t)
                            for i in range(2):
                                hh = 2 * q + i
                                for d in range(KB):
                                    last = pe.matmul(bank[:, i, d:KB, :], toep[:, hh, L - P * (d + 1):L - P * d],
                                                     acc4[:, 0:KB - d, :, t * HPT + hh], start=(d == 0), stop=True,
                                                     skip_group_check=True)
                            last.then_inc(s_conv, 1)

                    def chunk(c, first, last_chunk):
                        for t in range(NT):
                            m = c * NT + t
                            if first:
                                conv(t)
                                pe.wait_ge(s_ylo, 4 * (t + 1))
                            for f in range(2):
                                if t == 0:
                                    pe.wait_ge(s_wlg[f], c + 1)
                                if not (first and t == 0):
                                    pe.wait_ge((s_mul, s_silu)[f][1], m)
                                for k in range(KB):
                                    mv = (a_hi4[:, k, :, t * HPT:(t + 1) * HPT], a_lo4[:, k, :, t * HPT:(t + 1) * HPT])
                                    last = mm3(pe, ps_gu[G_BANK[f]], gu_hi[:, f, 0, k], gu_lo[:, f, 0, k], *mv,
                                               start=(k == 0), stop=(k == KB - 1))
                                last.then_inc(s_g[f], 1)
                                if f:
                                    pe.wait_ge(s_silu[0], m + 1)
                                elif not (first and t == 0):
                                    pe.wait_ge(s_mul[0], m)
                                for k in range(KB):
                                    mv = (a_hi4[:, k, :, t * HPT:(t + 1) * HPT], a_lo4[:, k, :, t * HPT:(t + 1) * HPT])
                                    last = mm3(pe, ps_gu[U_BANK[f]], gu_hi[:, f, 1, k], gu_lo[:, f, 1, k], *mv,
                                               start=(k == 0), stop=(k == KB - 1))
                                last.then_inc(s_u[f], 1)
                            for f in range(2):
                                if t == 0:
                                    pe.wait_ge(s_wld[f], c + 1)
                                pe.wait_ge(s_hl[f], m + 1)
                                if f == 0 and not (first and t == 0):
                                    pe.wait_ge(s_ev, m)
                                for k in range(KB):
                                    last = mm3(pe, ps_d[:, k], dn_hi[:, f, k * P:(k + 1) * P], dn_lo[:, f, k * P:(k + 1) * P],
                                               h_hi[:, f], h_lo[:, f], start=(f == 0), stop=(f == 1), skip=True)
                                last.then_inc(s_d[f], 1)

                    chunk(0, True, False)
                    with pe.Fori(1, NC0 - 1) as c:
                        chunk(c, False, False)
                    chunk(NC0 - 1, False, True)

                @block.scalar
                def _(act):
                    def chunk(c, first, last_chunk):
                        for t in range(NT):
                            m = c * NT + t
                            if first:
                                for q in range(4):
                                    h0 = t * HPT + 2 * q
                                    act.wait_ge(s_cmul, 4 * t + q + 1)
                                    act.activation(a_hi4[:, :, :, h0:h0 + 2].rearrange("p k b h -> p h k b"),
                                                   ytmp[:, q % 2].rearrange("p h (k b) -> p h k b", k=KB), ACT.Copy).then_inc(s_yhi, 1)
                            for f in range(2):
                                act.wait_ge(s_g[f], m + 1)
                                if not (first and t == 0):
                                    act.wait_ge(s_hl[f], m)
                                act.activation(s_act[:, f], ps_gu[G_BANK[f]], ACT.Silu).then_inc(s_silu[f], 1)
                                act.wait_ge(s_mul[f], m + 1)
                                if not (first and t == 0):
                                    act.wait_ge(s_d[f], m)
                                act.activation(h_hi[:, f], s_act[:, f], ACT.Copy).then_inc(s_hh[f], 1)
                                if t == NT - 1 and not last_chunk:
                                    act.wait_ge(s_wsc[f], c + 2)
                                    act.wait_ge(s_u[f], m + 1)
                                    act.activation(gu_hi[:, f].rearrange("p a k n -> p (a k n)"),
                                                   raw[:, f, 0:2].rearrange("p a n -> p (a n)"), ACT.Copy).then_inc(s_whg[f], 1)
                            if t == NT - 1 and not last_chunk:
                                for f in range(2):
                                    act.wait_ge(s_d[f], m + 1)
                                    act.activation(dn_hi[:, f], raw[:, f, 2], ACT.Copy).then_inc(s_whd[f], 1)
                            if last_chunk:
                                act.wait_ge(s_ev, m + 1)
                                act.activation(a_hi4[:, :, :, t * HPT:(t + 1) * HPT], acc_tile[t], ACT.Copy).then_inc(s_x1h, 1)

                    chunk(0, True, False)
                    with act.Fori(1, NC0 - 1) as c:
                        chunk(c, False, False)
                    chunk(NC0 - 1, False, True)

                @block.vector
                def _(dve):
                    def low_half(t, q):
                        j = 4 * t + q
                        h0 = t * HPT + 2 * q
                        dve.wait_ge(s_yhi, j + 1)
                        hv = a_hi4[:, :, :, h0:h0 + 2].rearrange("p k b h -> p h k b").bitcast(F32)
                        dve.tensor_tensor(a_lo4[:, :, :, h0:h0 + 2].rearrange("p k b h -> p h k b"),
                                          ytmp[:, q % 2].rearrange("p h (k b) -> p h k b", k=KB), hv, ALU.subtract).then_inc(s_ylo, 1)

                    def chunk(c, first, last_chunk):
                        for t in range(NT):
                            m = c * NT + t
                            if first:
                                for q in range(4):
                                    dve.wait_ge(s_conv, 4 * t + q + 1)
                                    if 4 * t + q >= 2:
                                        dve.wait_ge(s_yhi, 4 * t + q - 1)
                                        dve.wait_ge(s_ylo, 4 * t + q - 1)
                                    dve.tensor_tensor(ytmp[:, q % 2], conv_bank[q % 2].rearrange("p (i n) -> p i n", i=2),
                                                      bc(cmask[:].rearrange("p k b -> p (k b)"), 1, 2), ALU.mult).then_inc(s_cmul, 1)
                                    if q:
                                        low_half(t, q - 1)
                                low_half(t, 3)
                            for f in range(2):
                                dve.wait_ge(s_u[f], m + 1)
                                dve.wait_ge(s_silu[f], m + 1)
                                dve.tensor_tensor(s_act[:, f], s_act[:, f], ps_gu[U_BANK[f]], ALU.mult).then_inc(s_mul[f], 1)
                                dve.wait_ge(s_hh[f], m + 1)
                                if not (first and t == 0):
                                    dve.wait_ge(s_d[f], m)
                                dve.tensor_tensor(h_lo[:, f], s_act[:, f], h_hi[:, f].bitcast(F32), ALU.subtract).then_inc(s_hl[f], 1)
                                if t == NT - 1 and not last_chunk:
                                    dve.wait_ge(s_whg[f], c + 2)
                                    dve.tensor_tensor(gu_lo[:, f].rearrange("p a k n -> p (a k n)"),
                                                      raw[:, f, 0:2].rearrange("p a n -> p (a n)"),
                                                      gu_hi[:, f].rearrange("p a k n -> p (a k n)").bitcast(F32),
                                                      ALU.subtract).then_inc(s_wlg[f], 1)
                            if t == 1 and not last_chunk:
                                for f in range(2):
                                    dve.wait_ge(s_raw0[f], c * 16 + 32)
                                    w = raw[:, f].rearrange("p a (k n) -> p (a k) n", n=P)
                                    sc = scale0[:, bass.ds(c * 2 + (2 + f), 1)].rearrange("p a c -> p (a c)")
                                    dve.tensor_tensor(w, w, bc(sc, 2, P), ALU.mult).then_inc(s_wsc[f], 1)
                            dve.wait_ge(s_d[1], m + 1)
                            dve.tensor_tensor(acc_tile[t], acc_tile[t],
                                              ps_d[:].rearrange("p k (b h) -> p k b h", h=HPT), ALU.add).then_inc(s_ev, 1)
                            if t == NT - 1 and not last_chunk:
                                for f in range(2):
                                    dve.wait_ge(s_whd[f], c + 2)
                                    dve.tensor_tensor(dn_lo[:, f], raw[:, f, 2], dn_hi[:, f].bitcast(F32),
                                                      ALU.subtract).then_inc(s_wld[f], 1)
                            if last_chunk:
                                dve.wait_ge(s_x1h, t + 1)
                                dve.tensor_tensor(a_lo4[:, :, :, t * HPT:(t + 1) * HPT], acc_tile[t],
                                                  a_hi4[:, :, :, t * HPT:(t + 1) * HPT].bitcast(F32), ALU.subtract).then_inc(s_x1l, 1)

                    chunk(0, True, False)
                    with dve.Fori(1, NC0 - 1) as c:
                        chunk(c, False, False)
                    chunk(NC0 - 1, False, True)

        with ExitStack() as l1:
            scope[0] = l1
            t_hi = sb("t_hi", [P, 2, TOK], F32R)
            t_lo = sb("t_lo", [P, 2, TOK], F32R)

            c_a = [sem(f"c_a{i}") for i in range(2)]
            c_tr = [sem(f"c_tr{i}") for i in range(2)]
            c_ah = [sem(f"c_ah{i}") for i in range(2)]
            c_al = [sem(f"c_al{i}") for i in range(2)]
            c_tp = [sem(f"c_tp{i}") for i in range(2)]
            c_tm = [sem(f"c_tm{i}") for i in range(2)]
            c_th = [sem(f"c_th{i}") for i in range(2)]
            c_tl = [sem(f"c_tl{i}") for i in range(2)]
            s_raw1 = [sem(f"s_raw1_{f}") for f in range(2)]
            v_hg = [sem(f"v_hg{f}") for f in range(2)]
            v_lg = [sem(f"v_lg{f}") for f in range(2)]
            v_hd = [sem(f"v_hd{f}") for f in range(2)]
            v_ld = [sem(f"v_ld{f}") for f in range(2)]
            v_zero = sem("v_zero")

            def gather(pool, dst, table, group):
                return pool.indirect_dma_start(out=dst, out_offset=None, in_=table,
                                               in_offset=bass.IndirectOffsetOnAxis(ap=group, axis=0))

            with ExitStack() as pc:
                scope[0] = pc
                ar_raw = sb("ar_raw", [P, 2, 2 * L])
                ar_hi = sb("ar_hi", [P, 2, 2 * KB, P], F32R)
                ar_lo = sb("ar_lo", [P, 2, 2 * KB, P], F32R)
                tm = sb("tm", [P, 2, 2 * GT])
                t_bank = [b.rearrange("p (a n) -> p a n", a=2) for b in (ps_t[:], ps_gu[2])]
                a_bank = [ps_d[:, 2 * u:2 * u + 2].rearrange("p c n -> p (c n)") for u in range(2)]

                with nc.Block() as block:
                    @block.sync
                    def _(sp):
                        for f in range(2):
                            sp.dma_start(raw[:, f].rearrange("p a n -> p (a n)"), w1[f]).then_inc(s_raw1[f], 16)

                    @block.gpsimd
                    def _(pool):
                        for g in range(NG):
                            if g >= 2:
                                pool.wait_ge(c_tr[g % 2], g // 2)
                            gather(pool, ar_raw[:, g % 2], tab_a, rows0[:, g:g + 1]).then_inc(c_a[g % 2], 16)
                            if g == 1:
                                pool.memset(acc[:], 0.0).then_inc(v_zero, 1)

                    @block.tensor
                    def _(pe):
                        def transposes(u, n):
                            pe.wait_ge(c_a[u], n * 16 + 16)
                            pe.wait_ge(c_al[u], n)
                            for j in range(2 * KB):
                                last = pe.transpose(a_bank[u][:, j * P:(j + 1) * P], ar_raw[:, u, j * P:(j + 1) * P], ident_f[:])
                            last.then_inc(c_tr[u], 1)

                        def pair(i, last_pair):
                            for u in range(2):
                                if not (last_pair and u):
                                    transposes(1 - u, i + u)
                                pe.wait_ge(c_al[u], i + 1)
                                pe.wait_ge(c_tm[u], i)
                                at = bass.ds(i * (2 * GT) + u * GT, GT)
                                for w in range(2):
                                    for k in range(KB):
                                        last = mm3(pe, t_bank[u][:, w], ar_hi[:, u, w * KB + k], ar_lo[:, u, w * KB + k],
                                                   a_hi[:, k, at], a_lo[:, k, at], start=(k == 0), stop=(k == KB - 1), skip=True)
                                last.then_inc(c_tp[u], 1)

                        transposes(0, 0)
                        with pe.Fori(0, NG // 2 - 1) as i:
                            pair(i, False)
                        pair(NG // 2 - 1, True)

                    @block.scalar
                    def _(act):
                        def split(u, n):
                            act.wait_ge(c_tr[u], n + 1)
                            act.wait_ge(c_tp[u], n)
                            act.activation(ar_hi[:, u].rearrange("p k n -> p (k n)"), a_bank[u], ACT.Copy).then_inc(c_ah[u], 1)

                        def pair(i, last_pair):
                            for u in range(2):
                                if not (last_pair and u):
                                    split(1 - u, i + u)
                                act.wait_ge(c_tm[u], i + 1)
                                act.activation(t_hi[:, :, bass.ds(i * (2 * GT) + u * GT, GT)],
                                               tm[:, u].rearrange("p (a n) -> p a n", a=2), ACT.Copy).then_inc(c_th[u], 1)

                        split(0, 0)
                        for f in range(2):
                            act.wait_ge(s_raw1[f], 16)
                            act.activation(gu_hi[:, f].rearrange("p a k n -> p (a k n)"),
                                           raw[:, f, 0:2].rearrange("p a n -> p (a n)"), ACT.Copy).then_inc(v_hg[f], 1)
                            act.activation(dn_hi[:, f], raw[:, f, 2], ACT.Copy).then_inc(v_hd[f], 1)
                        with act.Fori(0, NG // 2 - 1) as i:
                            pair(i, False)
                        pair(NG // 2 - 1, True)

                    @block.vector
                    def _(dve):
                        def split(u, n):
                            dve.wait_ge(c_ah[u], n + 1)
                            dve.tensor_tensor(ar_lo[:, u].rearrange("p k n -> p (k n)"), a_bank[u],
                                              ar_hi[:, u].rearrange("p k n -> p (k n)").bitcast(F32), ALU.subtract).then_inc(c_al[u], 1)

                        def pair(i, last_pair):
                            for u in range(2):
                                if not (last_pair and u):
                                    split(1 - u, i + u)
                                dve.wait_ge(c_tp[u], i + 1)
                                dve.wait_ge(c_tl[u], i)
                                dve.tensor_tensor(tm[:, u].rearrange("p (a n) -> p a n", a=2), t_bank[u],
                                                  bc(lmask[:], 1, 2), ALU.mult).then_inc(c_tm[u], 1)
                                dve.wait_ge(c_th[u], i + 1)
                                at = bass.ds(i * (2 * GT) + u * GT, GT)
                                dve.tensor_tensor(t_lo[:, :, at], tm[:, u].rearrange("p (a n) -> p a n", a=2),
                                                  t_hi[:, :, at].bitcast(F32), ALU.subtract).then_inc(c_tl[u], 1)

                        split(0, 0)
                        for f in range(2):
                            dve.wait_ge(v_hg[f], 1)
                            dve.tensor_tensor(gu_lo[:, f].rearrange("p a k n -> p (a k n)"), raw[:, f, 0:2].rearrange("p a n -> p (a n)"),
                                              gu_hi[:, f].rearrange("p a k n -> p (a k n)").bitcast(F32),
                                              ALU.subtract).then_inc(v_lg[f], 1)
                            dve.wait_ge(v_hd[f], 1)
                            dve.tensor_tensor(dn_lo[:, f], raw[:, f, 2], dn_hi[:, f].bitcast(F32), ALU.subtract).then_inc(v_ld[f], 1)
                        with dve.Fori(0, NG // 2 - 1) as i:
                            pair(i, False)
                        pair(NG // 2 - 1, True)

            scope[0] = l1
            with ExitStack() as pd:
                scope[0] = pd
                lr_raw = sb("lr_raw", [P, 2, 6 * P])
                b_hi = sb("b_hi", [P, 2, 2, 2 * P], F32R)
                b_lo = sb("b_lo", [P, 2, 2, 2 * P], F32R)
                ad_hi = sb("ad_hi", [P, 2, 2 * P], F32R)
                ad_lo = sb("ad_lo", [P, 2, 2 * P], F32R)
                td = sb("td", [P, TOK])

                r_l, r_lt, r_turn = sem("r_l"), sem("r_lt"), sem("r_turn")
                r_bh, r_bl, r_bl0, r_adh, r_adl = sem("r_bh"), sem("r_bl"), sem("r_bl0"), sem("r_adh"), sem("r_adl")
                q_g = [sem(f"q_g{f}") for f in range(2)]
                q_u = [sem(f"q_u{f}") for f in range(2)]
                q_silu = [sem(f"q_silu{f}") for f in range(2)]
                q_mul = [sem(f"q_mul{f}") for f in range(2)]
                q_hh = [sem(f"q_hh{f}") for f in range(2)]
                q_hl = [sem(f"q_hl{f}") for f in range(2)]
                q_d, q_td, q_ev, q_tev = sem("q_d"), sem("q_td"), sem("q_ev"), sem("q_tev")
                r_tdm, r_tdh, r_tdl = sem("r_tdm"), sem("r_tdh"), sem("r_tdl")
                r_bd, r_bdh, r_bdl, q_bd = sem("r_bd"), sem("r_bdh"), sem("r_bdl"), sem("q_bd")
                CL = NC1 - 1
                ML = CL * NT

                tdm = s_act[:, 1]
                bd_raw = raw[:, 1, 0:2]
                bd_hi = gu_hi[:, 1].rearrange("p a k n -> p a (k n)")
                bd_lo = gu_lo[:, 1].rearrange("p a k n -> p a (k n)")

                def lanes(t):
                    return t[:, 0:2].rearrange("p a n -> p (a n)")

                def b_rows(f):
                    return lr_raw[:, :, f * 2 * P:(f + 1) * 2 * P]

                with nc.Block() as block:
                    @block.sync
                    def _(sp):
                        with sp.Fori(0, CL) as c:
                            for f in range(2):
                                sp.wait_ge(v_lg[f], c + 1)
                                sp.wait_ge(v_ld[f], c + 1)
                                sp.dma_start(raw[:, f].rearrange("p a n -> p (a n)"),
                                             w1[bass.ds(c * 2 + (2 + f), 1)].rearrange("a p n -> p (a n)")).then_inc(s_raw1[f], 16)

                    @block.gpsimd
                    def _(pool):
                        def step(t):
                            for g in range(2):
                                gather(pool, lr_raw[:, g], tab_l, rows[:, 2 * t + g:2 * t + g + 1]).then_inc(r_l, 16)

                        def lora_down_rows(t):
                            for g in range(2):
                                gather(pool, bd_raw[:, g], tab_bd, rows0[:, 2 * t + g:2 * t + g + 1]).then_inc(r_bd, 16)

                        step(0)
                        pool.memset(td[:], 0.0).then_inc(v_zero, 1)
                        with pool.Fori(0, CL) as c:
                            for t in range(1, NT):
                                pool.wait_ge(r_bl, c * NT + t)
                                pool.wait_ge(r_lt, c * NT + t)
                                pool.sem_inc(r_turn, 1)
                                step(t)
                            pool.wait_ge(r_l, c * (32 * NT) + 32 * NT)
                            pool.sem_inc(r_turn, 1)
                            pool.tensor_scalar(rows[:], rows[:], float(EXP * RANK), 0.0, ALU.add, ALU.add).then_inc(r_next, 1)
                            pool.wait_ge(r_next, c + 1)
                            pool.wait_ge(r_bl, c * NT + NT)
                            pool.wait_ge(r_lt, c * NT + NT)
                            pool.sem_inc(r_turn, 1)
                            step(0)
                        pool.wait_ge(v_lg[1], NC1)
                        pool.wait_ge(v_ld[1], NC1)
                        lora_down_rows(0)
                        for t in range(1, NT):
                            pool.wait_ge(r_bl, ML + t)
                            pool.wait_ge(r_lt, ML + t)
                            step(t)
                            pool.wait_ge(r_bdl, t)
                            lora_down_rows(t)

                    @block.tensor
                    def _(pe):
                        def gate_up(bank, w, f, slot, t, b_ready):
                            at = slice(t * TT, (t + 1) * TT)
                            for k in range(KB):
                                mm3(pe, bank, gu_hi[:, f, w, k], gu_lo[:, f, w, k], a_hi[:, k, at], a_lo[:, k, at],
                                    start=(k == 0), stop=(k == KB - 1))
                            pe.wait_ge(r_bl, b_ready)
                            for g in range(2):
                                at = slice((2 * t + g) * GT, (2 * t + g + 1) * GT)
                                wn = slice(w * P, (w + 1) * P)
                                last = mm3(pe, bank[:, g * GT:(g + 1) * GT], b_hi[:, slot, g, wn], b_lo[:, slot, g, wn],
                                           t_hi[:, w, at], t_lo[:, w, at], start=False, stop=True, skip=True)
                            return last

                        def transposes(bank, nf, m):
                            pe.wait_ge(r_l, m * 32 + 32)
                            for f in range(nf):
                                for g in range(2):
                                    last = pe.transpose(bank[:, (2 * f + g) * P:(2 * f + g + 1) * P],
                                                        lr_raw[:, g, (4 + f) * P:(5 + f) * P], ident_f[:])
                            last.then_inc(r_lt, 1)

                        def down(nf, c, t, m):
                            for f in range(nf):
                                if t == 0:
                                    pe.wait_ge(v_ld[f], c + 1)
                                pe.wait_ge(q_hl[f], m + 1)
                                if f == 0:
                                    pe.wait_ge(q_ev, m)
                                for s in range(4):
                                    sl = slice(s * P, (s + 1) * P)
                                    last = mm3(pe, ps_d[:, s], h_hi[:, f, sl], h_lo[:, f, sl], dn_hi[:, f], dn_lo[:, f],
                                               start=(f == 0), stop=(f == nf - 1 and nf == 2), skip=True)
                            last.then_inc(q_d, 1)

                        def lora_hidden(slots, m):
                            for f, slot in enumerate(slots):
                                pe.wait_ge(q_hl[f], m + 1)
                                for g in range(2):
                                    sl = slice(g * P, (g + 1) * P)
                                    last = mm3(pe, ps_t[:, g * GT:(g + 1) * GT], ad_hi[:, slot, sl], ad_lo[:, slot, sl],
                                               h_hi[:, f, g * GT:(g + 1) * GT], h_lo[:, f, g * GT:(g + 1) * GT],
                                               start=(f == 0 and g == 0), stop=(f == len(slots) - 1), skip=True)
                            last.then_inc(q_td, 1)

                        with pe.Fori(0, CL) as c:
                            for t in range(NT):
                                m = c * NT + t
                                for f in range(2):
                                    if t == 0:
                                        pe.wait_ge(v_lg[f], c + 1)
                                    pe.wait_ge((q_mul, q_silu)[f][1], m)
                                    gate_up(ps_gu[G_BANK[f]], 0, f, f, t, m + 1).then_inc(q_g[f], 1)
                                    if f:
                                        pe.wait_ge(q_silu[0], m + 1)
                                    else:
                                        pe.wait_ge(q_mul[0], m)
                                    gate_up(ps_gu[U_BANK[f]], 1, f, f, t, m + 1).then_inc(q_u[f], 1)
                                    if f == 0:
                                        pe.wait_ge(q_tev, m)
                                        transposes(ps_t, 2, m)
                                down(2, c, t, m)
                                pe.wait_ge(r_adl, m + 1)
                                lora_hidden((0, 1), m)

                        def ahead(t):
                            m = ML + t
                            if t == 0:
                                pe.wait_ge(v_lg[0], NC1)
                                pe.wait_ge(q_mul[1], m)
                                pe.wait_ge(q_silu[1], m)
                            else:
                                pe.wait_ge(q_silu[0], m)
                                pe.wait_ge(r_adl, m)
                            gate_up(ps_gu[0], 0, 0, t % 2, t, m + 1).then_inc(q_g[0], 1)
                            transposes(ps_gu[2], 1, m)
                            pe.wait_ge(q_mul[0], m)
                            gate_up(ps_gu[1], 1, 0, t % 2, t, m + 1).then_inc(q_u[0], 1)

                        ahead(0)
                        for t in range(NT):
                            m = ML + t
                            if t + 1 < NT:
                                ahead(t + 1)
                            pe.wait_ge(r_adl, m + 1)
                            pe.wait_ge(q_tev, m)
                            lora_hidden((t % 2,), m)
                            down(1, CL, t, m)
                            pe.wait_ge(r_tdl, t + 1)
                            pe.wait_ge(r_bdl, t + 1)
                            for s in range(4):
                                sl = slice(s * P, (s + 1) * P)
                                last = mm3(pe, ps_d[:, s], h_hi[:, 1, sl], h_lo[:, 1, sl], bd_hi[:, s // 2], bd_lo[:, s // 2],
                                           start=False, stop=True, skip=True)
                            last.then_inc(q_bd, 1)

                    @block.scalar
                    def _(act):
                        def gate(f, m):
                            act.wait_ge(q_g[f], m + 1)
                            act.wait_ge(q_hl[f], m)
                            act.activation(s_act[:, f], ps_gu[G_BANK[f]], ACT.Silu).then_inc(q_silu[f], 1)

                        def hidden_high(f, m):
                            act.wait_ge(q_mul[f], m + 1)
                            act.wait_ge(q_d, m)
                            act.wait_ge(q_td, m)
                            act.activation(h_hi[:, f], s_act[:, f], ACT.Copy).then_inc(q_hh[f], 1)

                        def down_rows(bank, slots, m):
                            act.wait_ge(r_lt, m + 1)
                            n = 2 * P * len(slots)
                            act.activation(ad_hi[:, slots[0]:slots[-1] + 1].rearrange("p f n -> p (f n)"), bank[:, 0:n],
                                           ACT.Copy).then_inc(r_adh, 1)

                        def b_split(m):
                            act.wait_ge(r_l, m * 32 + 32)
                            for f in range(2):
                                act.activation(b_hi[:, f], b_rows(f), ACT.Copy).then_inc(r_bh, 1)

                        b_split(0)
                        with act.Fori(0, CL) as c:
                            for t in range(NT):
                                m = c * NT + t
                                last_tile = t == NT - 1
                                for f in range(2):
                                    gate(f, m)
                                    hidden_high(f, m)
                                    if f == 0:
                                        act.wait_ge(q_td, m)
                                        down_rows(ps_t, (0, 1), m)
                                    if last_tile:
                                        act.wait_ge(s_raw1[f], c * 16 + 32)
                                        act.wait_ge(q_u[f], m + 1)
                                        act.activation(gu_hi[:, f].rearrange("p a k n -> p (a k n)"), lanes(raw[:, f]),
                                                       ACT.Copy).then_inc(v_hg[f], 1)
                                act.wait_ge(q_u[1], m + 1)
                                b_split(m + 1)
                                if last_tile:
                                    act.wait_ge(q_d, m + 1)
                                    for f in range(2):
                                        act.activation(dn_hi[:, f], raw[:, f, 2], ACT.Copy).then_inc(v_hd[f], 1)

                        def b_split_last(t):
                            act.wait_ge(r_l, (ML + t) * 32 + 32)
                            if t >= 2:
                                act.wait_ge(q_u[0], ML + t - 1)
                            act.activation(b_hi[:, t % 2], b_rows(0), ACT.Copy).then_inc(r_bh, 1)

                        def bd_split(t):
                            act.wait_ge(r_bd, (t + 1) * 32)
                            act.wait_ge(q_u[1], ML)
                            if t:
                                act.wait_ge(q_bd, t)
                            act.activation(bd_hi, bd_raw, ACT.Copy).then_inc(r_bdh, 1)

                        act.wait_ge(q_td, ML)
                        down_rows(ps_gu[2], (0,), ML)
                        gate(0, ML)
                        hidden_high(0, ML)
                        b_split_last(1)
                        bd_split(0)
                        for t in range(NT):
                            m = ML + t
                            if t + 1 < NT:
                                if t + 1 >= 2:
                                    act.wait_ge(q_td, m)
                                gate(0, m + 1)
                                down_rows(ps_gu[2], ((t + 1) % 2,), m + 1)
                            act.wait_ge(r_tdm, t + 1)
                            if t:
                                act.wait_ge(q_bd, t)
                            act.activation(h_hi[:, 1], tdm, ACT.Copy).then_inc(r_tdh, 1)
                            if t + 1 < NT:
                                hidden_high(0, m + 1)
                            if t + 2 < NT:
                                b_split_last(t + 2)
                            if t + 1 < NT:
                                bd_split(t + 1)

                    @block.vector
                    def _(dve):
                        def up(f, m):
                            dve.wait_ge(q_u[f], m + 1)
                            dve.wait_ge(q_silu[f], m + 1)
                            dve.tensor_tensor(s_act[:, f], s_act[:, f], ps_gu[U_BANK[f]], ALU.mult).then_inc(q_mul[f], 1)

                        def hidden_low(f, m):
                            dve.wait_ge(q_hh[f], m + 1)
                            dve.tensor_tensor(h_lo[:, f], s_act[:, f], h_hi[:, f].bitcast(F32), ALU.subtract).then_inc(q_hl[f], 1)

                        def down_rows(bank, slots, m):
                            dve.wait_ge(r_adh, m + 1)
                            n = 2 * P * len(slots)
                            sl = slice(slots[0], slots[-1] + 1)
                            dve.tensor_tensor(ad_lo[:, sl].rearrange("p f n -> p (f n)"), bank[:, 0:n],
                                              ad_hi[:, sl].rearrange("p f n -> p (f n)").bitcast(F32), ALU.subtract).then_inc(r_adl, 1)

                        def td_add(t, m):
                            dve.wait_ge(q_td, m + 1)
                            ts = td[:, t * TT:(t + 1) * TT]
                            dve.tensor_tensor(ts, ts, ps_t[:], ALU.add).then_inc(q_tev, 1)

                        def z_add(t):
                            zt = z[:, 4 * t:4 * t + 4]
                            dve.tensor_tensor(zt, zt, ps_d[:], ALU.add).then_inc(q_ev, 1)

                        def b_split(n):
                            for f in range(2):
                                dve.wait_ge(r_bh, n + f + 1)
                                ins = dve.tensor_tensor(b_lo[:, f], b_rows(f), b_hi[:, f].bitcast(F32), ALU.subtract)
                                ins.then_inc(r_bl, 1) if f else ins.then_inc(r_bl0, 1)

                        b_split(0)
                        dve.wait_ge(v_zero, 2)
                        with dve.Fori(0, CL) as c:
                            for t in range(NT):
                                m = c * NT + t
                                last_tile = t == NT - 1
                                for f in range(2):
                                    up(f, m)
                                    hidden_low(f, m)
                                    if f == 0:
                                        down_rows(ps_t, (0, 1), m)
                                    if last_tile:
                                        dve.wait_ge(v_hg[f], c + 2)
                                        dve.tensor_tensor(gu_lo[:, f].rearrange("p a k n -> p (a k n)"), lanes(raw[:, f]),
                                                          gu_hi[:, f].rearrange("p a k n -> p (a k n)").bitcast(F32),
                                                          ALU.subtract).then_inc(v_lg[f], 1)
                                b_split(m * 2 + 2)
                                dve.wait_ge(q_d, m + 1)
                                z_add(t)
                                td_add(t, m)
                                if last_tile:
                                    for f in range(2):
                                        dve.wait_ge(v_hd[f], c + 2)
                                        dve.tensor_tensor(dn_lo[:, f], raw[:, f, 2], dn_hi[:, f].bitcast(F32),
                                                          ALU.subtract).then_inc(v_ld[f], 1)

                        def b_split_last(t):
                            dve.wait_ge(r_bh, 2 * ML + 2 + t)
                            dve.tensor_tensor(b_lo[:, t % 2], b_rows(0), b_hi[:, t % 2].bitcast(F32), ALU.subtract).then_inc(r_bl, 1)

                        def bd_split(t):
                            dve.wait_ge(r_bdh, t + 1)
                            dve.tensor_tensor(bd_lo, bd_raw, bd_hi.bitcast(F32), ALU.subtract).then_inc(r_bdl, 1)

                        down_rows(ps_gu[2], (0,), ML)
                        up(0, ML)
                        hidden_low(0, ML)
                        b_split_last(1)
                        bd_split(0)
                        for t in range(NT):
                            m = ML + t
                            if t + 1 < NT:
                                down_rows(ps_gu[2], ((t + 1) % 2,), m + 1)
                                up(0, m + 1)
                            td_add(t, m)
                            dve.wait_ge(q_tev, m + 1)
                            if t:
                                dve.wait_ge(r_tdl, t)
                            dve.tensor_tensor(tdm.rearrange("p (g n) -> p g n", g=2),
                                              td[:, t * TT:(t + 1) * TT].rearrange("p (g n) -> p g n", g=2),
                                              bc(lmask[:], 1, 2), ALU.mult).then_inc(r_tdm, 1)
                            dve.wait_ge(r_tdh, t + 1)
                            dve.tensor_tensor(h_lo[:, 1], tdm, h_hi[:, 1].bitcast(F32), ALU.subtract).then_inc(r_tdl, 1)
                            if t + 1 < NT:
                                hidden_low(0, m + 1)
                            if t + 2 < NT:
                                b_split_last(t + 2)
                            dve.wait_ge(q_bd, t + 1)
                            z_add(t)
                            if t + 1 < NT:
                                bd_split(t + 1)

        with ExitStack() as pe_scope:
            scope[0] = pe_scope
            NSUB = TOK // P
            w_sb = sb("w_sb", [P, KB, L])
            w_t = sb("w_t", [P, KB * L])
            w_q = sb("w_q", [P, KB, L], BF16)
            bias_sb = sb("bias_sb", [P, L])
            ident_b = sb("ident_b", [P, P], BF16)
            ident_r = sb("ident_r", [P, P], F32R)
            ones = sb("ones", [P, P])
            wsum = sb("wsum", [P, 1])
            wm = sb("wm", [P, 1])
            wi = sb("wi", [P, 1])
            ss = sb("ss", [P, NSUB])
            am = sb("am", [P, NSUB])
            ra = sb("ra", [P, NSUB])
            cc = sb("cc", [P, NSUB])
            dq = sb("dq", [P, NSUB])
            epsb = sb("epsb", [P, 1])
            junk = sb("junk", [P, 2, L])
            qf = sb("qf", [P, 2, L])
            qb = sb("qb", [P, 2, L], BF16)
            qT = sb("qT", [P, 2, L], BF16)
            yb = sb("yb", [P, 2, L])
            gb = sb("gb", [P, 2, L])
            o1 = sb("o1", [P, 2, L])
            o2 = sb("o2", [P, 2, L])
            e_w, e_b, e_id, e_ws, e_wp, e_wq, e_ss, e_am, e_rt, e_c = (sem(n) for n in (
                "e_w", "e_b", "e_id", "e_ws", "e_wp", "e_wq", "e_ss", "e_am", "e_rt", "e_c"))
            e_q, e_tp, e_qt, e_y, e_x, e_yb, e_gb, e_o1, e_o2 = (sem(n) for n in (
                "e_q", "e_tp", "e_qt", "e_y", "e_x", "e_yb", "e_gb", "e_o1", "e_o2"))
            e_out = [sem(f"e_out{i}") for i in range(2)]
            ps_tp = [ps_gu[i].bitcast(BF16)[:, 0:L] for i in range(2)]
            ps_y = [ps_gu[2], ps_t[:]]
            ps_x = [ps_d[:, i] for i in range(2)]
            o_rows = out.rearrange("b h n -> (b h) n")

            with nc.Block() as block:
                @block.sync
                def _(sp):
                    sp.dma_start(w_sb[:], wq).then_inc(e_w, 16)
                    sp.dma_start(bias_sb[:], bass.AP(tensor=bias.tensor, offset=0, ap=[[0, P], [1, L]])).then_inc(e_b, 16)
                    for s in range(NSUB):
                        sp.wait_ge(e_o2, s + 1)
                        sp.dma_start(o_rows[s * P:(s + 1) * P, :], o2[:, s % 2]).then_inc(e_out[s % 2], 16)
                    for i in range(2):
                        sp.wait_ge(e_out[i], 16 * (NSUB // 2))

                @block.gpsimd
                def _(pool):
                    pool.memset(epsb[:], EPS).then_inc(e_c, 1)
                    pool.memset(ones[:], 1.0).then_inc(e_id, 1)
                    for s in range(NSUB):
                        pool.wait_ge(e_gb, s + 1)
                        pool.wait_ge(e_o1, s + 1)
                        if s >= 2:
                            pool.wait_ge(e_out[s % 2], 16 * (s // 2))
                        pool.tensor_tensor(o2[:, s % 2], o1[:, s % 2], gb[:, s % 2], ALU.add).then_inc(e_o2, 1)

                @block.vector
                def _(dve):
                    def link(ins):
                        chain[0] += 1
                        ins.then_inc(s_chain, 1)
                        dve.wait_ge(s_chain, chain[0])

                    dve.tensor_copy(ident_b[:], ident_f[:]).then_inc(e_id, 1)
                    dve.tensor_copy(ident_r[:], ident_f[:]).then_inc(e_id, 1)
                    dve.wait_ge(e_w, 16)
                    wf = w_sb[:].rearrange("p k n -> p (k n)")
                    dve.tensor_reduce(wsum[:], wf, AX.X, ALU.add, apply_absolute_value=True).then_inc(e_ws, 1)
                    for s in range(NSUB):
                        dve.tensor_reduce(am[:, s:s + 1], z[:, s], AX.X, ALU.max, apply_absolute_value=True).then_inc(e_am, 1)
                    dve.wait_ge(e_wp, 1)
                    link(dve.tensor_scalar(wm[:], ps_d[:, 3, 0:1], 1.0 / (L * L), EPS, ALU.mult, ALU.max))
                    link(dve.reciprocal(wi[:], wm[:]))
                    link(dve.tensor_scalar(w_t[:], wf, wi[:], MAGIC, ALU.mult, ALU.add))
                    link(dve.tensor_scalar(w_t[:], w_t[:], MAGIC, 1.0, ALU.subtract, ALU.min))
                    dve.tensor_scalar(w_q[:].rearrange("p k n -> p (k n)"), w_t[:], -1.0, None, ALU.max).then_inc(e_wq, 1)
                    dve.wait_ge(e_rt, 1)
                    link(dve.reciprocal(ra[:], ra[:]))
                    dve.wait_ge(e_am, NSUB)
                    link(dve.tensor_tensor(am[:], am[:], ra[:], ALU.mult))
                    link(dve.tensor_scalar(am[:], am[:], EPS, None, ALU.max))
                    link(dve.reciprocal(cc[:], am[:]))
                    link(dve.scalar_tensor_tensor(out=cc[:], in0=cc[:], scalar=127.0, in1=ra[:], op0=ALU.mult, op1=ALU.mult))
                    link(dve.tensor_scalar(dq[:], am[:], wm[:], 1.0 / 127, ALU.mult, ALU.mult))

                    def quant(s):
                        i = s % 2
                        link(dve.tensor_scalar(qf[:, i], z[:, s], cc[:, s:s + 1], MAGIC, ALU.mult, ALU.add))
                        link(dve.tensor_scalar(qf[:, i], qf[:, i], MAGIC, 127.0, ALU.subtract, ALU.min))
                        if s >= 2:
                            dve.wait_ge(e_tp, s - 1)
                        dve.tensor_scalar(qb[:, i], qf[:, i], -128.0, None, ALU.max).then_inc(e_q, 1)

                    quant(0)
                    for s in range(NSUB):
                        i = s % 2
                        if s + 1 < NSUB:
                            quant(s + 1)
                        if s == 0:
                            dve.wait_ge(e_b, 16)
                        dve.wait_ge(e_x, s + 1)
                        if s >= 2:
                            dve.wait_ge(e_o2, s - 1)
                        dve.tensor_tensor(o1[:, i], z[:, s], ps_x[i], ALU.add).then_inc(e_o1, 1)
                        dve.wait_ge(e_y, s + 1)
                        if s >= 2:
                            dve.wait_ge(e_gb, s - 1)
                        dve.scalar_tensor_tensor(out=yb[:, i], in0=ps_y[i], scalar=dq[:, s:s + 1], in1=bias_sb[:],
                                                 op0=ALU.mult, op1=ALU.add).then_inc(e_yb, 1)

                @block.scalar
                def _(act):
                    for s in range(NSUB):
                        if s >= 2:
                            act.wait_ge(e_ss, s - 1)
                        act.activation(junk[:, s % 2], z[:, s], ACT.Square, accum_out=ss[:, s:s + 1]).then_inc(e_ss, 1)
                    act.wait_ge(e_ss, NSUB)
                    act.wait_ge(e_c, 1)
                    act.activation(ra[:], ss[:], ACT.Sqrt, scale=1.0 / L, bias=epsb[:]).then_inc(e_rt, 1)
                    for s in range(NSUB):
                        i = s % 2
                        act.wait_ge(e_tp, s + 1)
                        if s >= 2:
                            act.wait_ge(e_y, s - 1)
                        act.activation(qT[:, i], ps_tp[i], ACT.Copy).then_inc(e_qt, 1)
                        act.wait_ge(e_yb, s + 1)
                        if s >= 2:
                            act.wait_ge(e_o2, s - 1)
                        act.activation(gb[:, i], yb[:, i], ACT.Gelu).then_inc(e_gb, 1)

                @block.tensor
                def _(pe):
                    pe.wait_ge(e_ws, 1)
                    pe.wait_ge(e_id, 3)
                    pe.matmul(ps_d[:, 3, 0:1], ones[:], wsum[:], start=True, stop=True).then_inc(e_wp, 1)
                    for s in range(NSUB + 1):
                        if s < NSUB:
                            i = s % 2
                            pe.wait_ge(e_q, s + 1)
                            if s >= 2:
                                pe.wait_ge(e_qt, s - 1)
                            for k in range(KB):
                                last = pe.transpose(ps_tp[i][:, k * P:(k + 1) * P], qb[:, i, k * P:(k + 1) * P], ident_b[:])
                            last.then_inc(e_tp, 1)
                            if s >= 2:
                                pe.wait_ge(e_o1, s - 1)
                            for k in range(KB):
                                sl = slice(s * P, (s + 1) * P)
                                pe.matmul(ps_x[i][:, k * P:(k + 1) * P], a_hi[:, k, sl], ident_r[:], start=True, stop=False,
                                          skip_group_check=True)
                                last = pe.matmul(ps_x[i][:, k * P:(k + 1) * P], a_lo[:, k, sl], ident_r[:], start=False, stop=True,
                                                 skip_group_check=True)
                            last.then_inc(e_x, 1)
                        if s:
                            v = s - 1
                            i = v % 2
                            pe.wait_ge(e_qt, v + 1)
                            if v == 0:
                                pe.wait_ge(e_wq, 1)
                            if v >= 2:
                                pe.wait_ge(e_yb, v - 1)
                            for k in range(KB):
                                last = pe.matmul(ps_y[i], qT[:, i, k * P:(k + 1) * P], w_q[:, k], start=(k == 0), stop=(k == KB - 1))
                            last.then_inc(e_y, 1)


def kernel(**inputs):
    import concourse.bacc as bacc
    from concourse.bass_utils import run_bass_kernel_spmd

    a = {k: np.asarray(v) for k, v in inputs.items()}

    def stack2(v):
        return np.concatenate([v, v], axis=0)

    def padded(v, axis, n):
        shape = list(v.shape)
        shape[axis] = n
        w = np.zeros(shape, v.dtype)
        w[tuple(slice(0, k) for k in v.shape)] = v
        return w

    def by_block(w, rows_reversed):
        w = w.reshape(-1, P, KB, P)
        if rows_reversed:
            w = w[..., ::-1]
        return w.transpose(0, 3, 2, 1).reshape(-1, P, KB * P)

    def slots(gate, up, down, rows_reversed):
        return np.stack([by_block(gate, rows_reversed), by_block(up, rows_reversed),
                         down.reshape(L, -1, P).transpose(1, 2, 0)], axis=2).reshape(-1, P, 3 * L)

    lay = {
        "x_t": a["x"].reshape(TOK, L).T.reshape(KB, P, TOK).transpose(1, 0, 2),
        "par": stack2(np.stack([np.broadcast_to(a["L0_cond_log_dt"][None, :], (NSTATE, HEADS)),
                                a["L0_cond_log_A_real"].T, a["L0_cond_A_imag"].T,
                                a["L0_cond_C"][..., 0].T, a["L0_cond_C"][..., 1].T], axis=1)),
        "d_row": a["L0_cond_D"][None, :],
        "length": a["itok_B_78_3631"],
        "idx": a["itok_B_2_6"],
        "w0": slots(a["L0_ffn_w1"], a["L0_ffn_w3"], a["L0_ffn_w2"], True),
        "sc0": np.concatenate([a["L0_ffn_w1_scale"], a["L0_ffn_w3_scale"], a["L0_ffn_w2_scale"].T], axis=1),
        "w1": slots(padded(a["L1_cond_W_gate"], 0, 2 * NC1 * P), padded(a["L1_cond_W_up"], 0, 2 * NC1 * P),
                    padded(a["L1_cond_W_down"], 1, 2 * NC1 * P), False),
        "tab_a": np.stack([a["L1_cond_A_gate"][0], a["L1_cond_A_up"][0]], axis=2).reshape(EXP * RANK, 2 * L),
        "tab_l": np.concatenate([
            padded(np.stack([a["L1_cond_B_gate"][0], a["L1_cond_B_up"][0]], axis=1), 2, 2 * NC1 * P)
            .reshape(EXP, 2, NC1, 2, P, RANK).transpose(2, 0, 5, 3, 1, 4).reshape(NC1, EXP, RANK, 4 * P),
            padded(a["L1_cond_A_down"][0], 2, 2 * NC1 * P)
            .reshape(EXP, RANK, NC1, 2 * P).transpose(2, 0, 1, 3)], axis=3).reshape(NC1 * EXP * RANK, 6 * P),
        "tab_bd": a["L1_cond_B_down"][0].transpose(0, 2, 1).reshape(EXP * RANK, L),
        "wq": a["L1_ffn_W"].T.reshape(KB, P, L).transpose(1, 0, 2),
        "bias": a["L1_ffn_b"][None, :],
        "rowbase": np.repeat((np.arange(P)[:, None] % RANK).astype(np.int32), NG, axis=1),
    }
    nc = bacc.Bacc("TRN2", target_bir_lowering=False, num_devices=1)
    arrays, args = {}, []
    for name, v in lay.items():
        v = np.ascontiguousarray(v)
        arrays["in_" + name] = v
        args.append(nc.dram_tensor("in_" + name, v.shape, mybir.dt.from_np(v.dtype), kind="ExternalInput").ap())
    args.append(nc.dram_tensor("out_0", (BATCH, HEADS, L), F32, kind="ExternalOutput").ap())
    build(nc, *args)
    r = run_bass_kernel_spmd(nc, [arrays], core_ids=[0])
    return r.results[0]["out_0"]
```

```python
from contextlib import ExitStack

import numpy as np

import concourse.bass as bass
from concourse import mybir

F32 = mybir.dt.float32
F32R = mybir.dt.float32r
BF16 = mybir.dt.bfloat16
I32 = mybir.dt.int32
ALU = mybir.AluOpType
ACT = mybir.ActivationFunctionType
AX = mybir.AxisListType

P = 128
BATCH, HEADS, L = 64, 32, 512
TOK = BATCH * HEADS
KB = L // P
NT = 4
TT = TOK // NT
HPT = HEADS // NT
F0, F1 = 1792, 1376
NF0 = F0 // P
NF1 = -(-F1 // P)
NC0 = NF0 // 2
NC1 = -(-NF1 // 2)
EXP, RANK = 16, 16
GB = P // RANK
NG = BATCH // GB
NSUB = TOK // P
GT = GB * HEADS
NSTATE = 64
NA, NB = 16, 32
KROW = L + P
YD, GD = 3, 4
ON_VECTOR = (3, 7, 11, 13, 15)
MAGIC = float(3 << 22)
LN2_HI, LN2_LO = 0.693359375, -2.12194440e-4
LOG2E = 1.4426950408889634
TWO_PI = 6.283185
EPS = 1e-5


def bc(ap, dim, n):
    ap = ap.unsqueeze(dim)
    shape = list(ap.shape)
    shape[dim] = n
    return ap.to_broadcast(shape)


def build(nc, x_t, par, d_row, length, idx, w0, sc0, w1, tab_a, tab_l, tab_bd, wq, bias, rowbase, out):
    with ExitStack() as top:
        scope = [top]

        def sb(name, shape, dt=F32):
            return scope[0].enter_context(nc.sbuf_tensor(name, shape, dt))

        def sem(name):
            return top.enter_context(nc.semaphore(name))

        krev = nc.dram_tensor("krev", (HEADS, KROW), F32, kind="Internal").ap()

        ps_gu = [top.enter_context(nc.psum_tensor(f"ps_gu{i}", [P, 512], F32))[:] for i in range(3)]
        ps_d = top.enter_context(nc.psum_tensor("ps_d", [P, 4, 512], F32))
        ps_t = top.enter_context(nc.psum_tensor("ps_t", [P, 512], F32))
        G_BANK, U_BANK = (0, 2), (1, 0)

        acc = sb("acc", [P, KB, TOK])
        a_hi = sb("a_hi", [P, KB, TOK], F32R)
        a_lo = sb("a_lo", [P, KB, TOK], F32R)
        gu_hi = sb("gu_hi", [P, 2, 2, KB, P], F32R)
        gu_lo = sb("gu_lo", [P, 2, 2, KB, P], F32R)
        with ExitStack() as same_place:
            scope[0] = same_place
            dn_f = sb("dn_f", [P, 4, L])
            scope[0] = top
        dn_hi = sb("dn_hi", [P, 2, L], F32R)
        dn_lo = sb("dn_lo", [P, 2, L], F32R)
        raw = sb("raw", [P, 2, 3, L])
        s_act = sb("s_act", [P, 2, TT])
        h_hi = sb("h_hi", [P, 2, TT], F32R)
        h_lo = sb("h_lo", [P, 2, TT], F32R)
        lmask = sb("lmask", [P, GT])
        ident_f = sb("ident_f", [P, P])
        rows0 = sb("rows0", [P, NG], I32)
        rows = sb("rows", [P, NG], I32)
        ident_b = sb("ident_b", [P, P], BF16)
        ones = sb("ones", [P, P])
        wsum = sb("wsum", [P, 1])
        wm = sb("wm", [P, 1])
        w_inv = sb("w_inv", [P, 1])
        epsb = sb("epsb", [P, 1])
        z = acc[:].rearrange("p k t -> p (k t)").rearrange("p (s n) -> p s n", n=L)

        chain = [0]
        pool_chain = [0]
        s_chain = sem("s_chain")

        def by_head(t):
            return t[:].rearrange("p k (b h) -> p k b h", h=HEADS)

        def past(eng, s, n):
            if not (isinstance(n, int) and n == 0):
                eng.wait_ge(s, n)

        def mm3(pe, out_ap, st_hi, st_lo, mv_hi, mv_lo, start, stop, skip=False):
            pe.matmul(out_ap, st_hi, mv_hi, start=start, stop=False, skip_group_check=skip)
            pe.matmul(out_ap, st_hi, mv_lo, start=False, stop=False, skip_group_check=skip)
            return pe.matmul(out_ap, st_lo, mv_hi, start=False, stop=stop, skip_group_check=skip)

        s_par, s_drow, s_len, s_ix, s_rb, s_id = (sem(n) for n in ("s_par", "s_drow", "s_len", "s_ix", "s_rb", "s_id"))
        r_row, r_next = sem("r_row"), sem("r_next")
        s_x, s_sc0, s_T = sem("s_x"), sem("s_sc0"), sem("s_T")
        s_grid, s_sin, s_theta, s_sf, s_kp, s_ks, s_kz = (sem(n) for n in (
            "s_grid", "s_sin", "s_theta", "s_sf", "s_kp", "s_ks", "s_kz"))
        s_kw = [sem(f"s_kw{i}") for i in range(2)]
        s_step, s_pw, s_mag, s_coef, s_plink, s_T0, s_den = (
            sem(n) for n in ("s_step", "s_pw", "s_mag", "s_coef", "s_plink", "s_T0", "s_den"))
        s_raw0, s_wsc, s_whg, s_wlg, s_whd, s_wld = ([sem(f"{n}{f}") for f in range(2)] for n in (
            "s_raw0_", "s_wsc", "s_whg", "s_wlg", "s_whd", "s_wld"))
        s_conv, s_cmul, s_yhi, s_ylo = sem("s_conv"), sem("s_cmul"), sem("s_yhi"), sem("s_ylo")
        s_g, s_u, s_silu, s_mul, s_hh, s_hl, s_d = ([sem(f"{n}{f}") for f in range(2)] for n in (
            "s_g", "s_u", "s_silu", "s_mul", "s_hh", "s_hl", "s_d"))
        s_ev, s_evk, s_x1h, s_x1l = sem("s_ev"), sem("s_evk"), sem("s_x1h"), sem("s_x1l")
        s_wall, s_wsum, v_zero = sem("s_wall"), sem("s_wsum"), sem("v_zero")
        c_a, c_tr, c_ah, c_al, c_tp, c_tm, c_th, c_tl = ([sem(f"{n}{i}") for i in range(2)] for n in (
            "c_a", "c_tr", "c_ah", "c_al", "c_tp", "c_tm", "c_th", "c_tl"))
        r_l, r_lt, r_turn = sem("r_l"), sem("r_lt"), sem("r_turn")
        r_bh, r_bl, r_bl0, r_adh, r_adl = sem("r_bh"), sem("r_bl"), sem("r_bl0"), sem("r_adh"), sem("r_adl")
        r_tdm, r_tdh, r_tdl = sem("r_tdm"), sem("r_tdh"), sem("r_tdl")
        r_bd, r_bdh, r_bdl, q_bd = sem("r_bd"), sem("r_bdh"), sem("r_bdl"), sem("q_bd")
        q_td, q_tev = sem("q_td"), sem("q_tev")
        e_b, e_cc, e_qm, e_wp, e_wm, e_wq, e_ss, e_am, e_rt, e_cl, e_qb, e_tp, e_qt = (sem(n) for n in (
            "e_b", "e_cc", "e_qm", "e_wp", "e_wm", "e_wq", "e_ss", "e_am", "e_rt", "e_cl", "e_qb", "e_tp", "e_qt"))
        e_w = [sem(f"e_w{i}") for i in range(2)]
        e_zf, e_xs, e_xt, e_y, e_yb, e_gb, e_op, e_od, e_out = (sem(n) for n in (
            "e_zf", "e_xs", "e_xt", "e_y", "e_yb", "e_gb", "e_op", "e_od", "e_out"))
        ss, am, ra, cc, dq = (sb(n, [P, NSUB]) for n in ("ss", "am", "ra", "cc", "dq"))

        with ExitStack() as layer0:
            scope[0] = layer0
            scale0 = sb("scale0", [P, NF0, 12])
            cmask = sb("cmask", [P, KB, BATCH])
            toep = sb("toep", [P, HPT, L])
            ytmp = sb("ytmp", [P, 2, 2, KB * BATCH])
            w_all = sb("w_all", [P, KB * L])
            par_sb = sb("par_sb", [P, 5, HEADS])
            drow = sb("drow", [1, HEADS])
            ixr = sb("ixr", [P, NG], I32)
            rowb = sb("rowb", [P, NG], I32)
            len_i = sb("len_i", [P, BATCH], I32)
            len_f = sb("len_f", [P, BATCH])
            pos = sb("pos", [P, KB, BATCH])
            pow2 = sb("pow2", [P, 9])
            lgrid = sb("lgrid", [P, 64])
            dm = sb("dm", [1, HEADS, NB])
            onehot = sb("onehot", [1, NA])
            zero = sb("zero", [HEADS, P])
            k_sb = sb("k_sb", [NA, HEADS, NB])
            e2 = sb("e2", [P, 2, HEADS])
            sm = [sb(f"sm{i}", [P, HEADS]) for i in range(18)]
            pin = sb("pin", [P, 9, HEADS])
            pw = sb("pw", [P, 9, HEADS])
            tmp = [sb(f"tmp{i}", [P, 9 * HEADS]) for i in range(4)]
            kint = sb("kint", [P, 9 * HEADS], I32)
            S = sb("S", [P, HEADS, NA])
            S2 = sb("S2", [P, HEADS, NA])
            Fm = sb("Fm", [P, HEADS, NB])
            trig_small = (sb("sin1", [P, HEADS])[:], sb("sin2", [P, HEADS])[:])
            mag = w_all[:, 0:HEADS * (NA + NB)].rearrange("p (h n) -> p h n", h=HEADS)
            theta = toep[:, 0:4].rearrange("p a n -> p (a n)").rearrange("p (h n) -> p h n", n=64)
            trig = toep[:, 4:8].rearrange("p a n -> p (a n)").rearrange("p (h n) -> p h n", n=64)
            rnd = trig
        pk = ps_d[0:NA, :, 0:HPT * NB].rearrange("a t (h b) -> a t h b", b=NB)
        a_hi4, a_lo4, acc4 = by_head(a_hi), by_head(a_lo), by_head(acc)
        conv_bank = (ps_t[:], ps_gu[2])
        acc_tile = [acc4[:, :, :, t * HPT:(t + 1) * HPT] for t in range(NT)]

        with ExitStack() as projections:
            scope[0] = projections
            t_hi = sb("t_hi", [P, 2, TOK], F32R)
            t_lo = sb("t_lo", [P, 2, TOK], F32R)
            ar_raw = sb("ar_raw", [P, 2, 2 * L])
            ar_hi = sb("ar_hi", [P, 2, 2 * KB, P], F32R)
            ar_lo = sb("ar_lo", [P, 2, 2 * KB, P], F32R)
            tm = sb("tm", [P, 2, 2 * GT])
        t_bank = [b.rearrange("p (a n) -> p a n", a=2) for b in (ps_t[:], ps_gu[2])]
        a_bank = [ps_d[:, 2 * u:2 * u + 2].rearrange("p c n -> p (c n)") for u in range(2)]

        first_bank = [(ps_t[:], ps_gu[2]), (ps_gu[1], ps_gu[0])]

        scope[0] = top
        q_t = sb("q_t", [P, 2, NT, 2 * L], BF16)
        z_new = sb("z_new", [P, 2, TOK])
        zf = z_new[:, :, 0:2 * TT]
        qb = z_new[:].bitcast(BF16)[:, :, 4 * TT:6 * TT]
        with ExitStack() as last_stage:
            scope[0] = last_stage
            yb = sb("yb", [P, YD, L])
        scope[0] = top
        lr_raw = sb("lr_raw", [P, 2, 6 * P])
        junk = sb("junk", [P, 2, L], BF16)
        b_hi = sb("b_hi", [P, 2, 2, 2 * P], F32R)
        ad_hi = sb("ad_hi", [P, 2, 2 * P], F32R)
        ad_lo = sb("ad_lo", [P, 2, 2 * P], F32R)
        b_lo = sb("b_lo", [P, 2, 2, 2 * P], F32R)
        with ExitStack() as last_stage:
            scope[0] = last_stage
            gb = sb("gb", [P, GD, L])
        scope[0] = top
        td = sb("td", [P, TOK])

        CL = NC0 + NC1 - 1
        M1, ML = NC0 * NT, CL * NT
        RL = ML - M1

        tdm = s_act[:, 1]
        bd_raw = raw[:, 1, 0:2]
        bd_hi = gu_hi[:, 1].rearrange("p a k n -> p a (k n)")
        bd_lo = gu_lo[:, 1].rearrange("p a k n -> p a (k n)")
        bias_sb = raw[:, 1, 2]
        x_sum = [dn_f[:, 1], dn_f[:, 3], raw[:, 0, 2]]
        w_q = raw[:, 0, 0:2].rearrange("p a n -> p (a n)").bitcast(BF16).rearrange("p (k n) -> p k n", n=L)
        w_blk = [raw[:, i, 2] for i in range(2)]
        ps_y = [ps_gu[1], ps_gu[0]]
        q_bank = [ps_gu[2].bitcast(BF16), ps_t[:].bitcast(BF16)]
        o_rows = out.rearrange("b h n -> (b h) n")

        def x_tile(a, t, k):
            return a[:, k, :, t * HPT:(t + 1) * HPT]

        def wait_whole(eng, s):
            on_vector = sum(v <= s for v in ON_VECTOR)
            if s in ON_VECTOR:
                eng.wait_ge(e_od, on_vector)
            else:
                eng.wait_ge(e_op, s + 1 - on_vector)

        def lanes(t):
            return t[:, 0:2].rearrange("p a n -> p (a n)")

        def b_rows(f):
            return lr_raw[:, :, f * 2 * P:(f + 1) * 2 * P]

        def gather(pool, dst, table, group):
            return pool.indirect_dma_start(out=dst, out_offset=None, in_=table,
                                           in_offset=bass.IndirectOffsetOnAxis(ap=group, axis=0))

        with nc.Block() as block:
            @block.sync
            def _(sp):
                sp.dma_start(par_sb[:], par).then_inc(s_par, 16)
                sp.dma_start(drow[:], d_row).then_inc(s_drow, 16)
                sp.dma_start(len_i[:], bass.AP(tensor=length.tensor, offset=0, ap=[[0, P], [1, BATCH]])).then_inc(s_len, 16)
                sp.dma_start(scale0[:].rearrange("p f c -> p (f c)"),
                             bass.AP(tensor=sc0.tensor, offset=0, ap=[[0, P], [1, NF0 * 12]])).then_inc(s_sc0, 16)
                for f in range(2):
                    sp.dma_start(raw[:, f].rearrange("p a n -> p (a n)"), w0[f]).then_inc(s_raw0[f], 16)
                sp.dma_start(acc[:], x_t).then_inc(s_x, 16)
                sp.dma_start(rowb[:], rowbase).then_inc(s_rb, 16)
                with nc.allow_non_contiguous_dma(reason="512 small integers"):
                    for b in range(GB):
                        sp.dma_start(ixr[b * RANK:(b + 1) * RANK, :],
                                     bass.AP(tensor=idx.tensor, offset=b, ap=[[0, RANK], [GB, NG]])).then_inc(s_ix, 16)
                sp.wait_ge(s_grid, 1)
                sp.dma_start(krev[:, L:KROW], zero[:]).then_inc(s_kz, 16)
                for i, hs in enumerate((slice(0, HPT), slice(HPT, HEADS))):
                    sp.wait_ge(s_ks, (1, NT)[i])
                    sp.dma_start(krev[hs, 0:L].rearrange("h (a b) -> a h b", b=NB), k_sb[:, hs]).then_inc(s_kw[i], 16)
                    if i == 0:
                        sp.wait_ge(s_kw[0], 16)
                        sp.wait_ge(s_kz, 16)
                        for n in range(2):
                            sp.dma_start(toep[:, n * (HPT // 2):(n + 1) * (HPT // 2)],
                                         bass.AP(tensor=krev.tensor, offset=n * (HPT // 2) * KROW,
                                                 ap=[[1, P], [KROW, HPT // 2], [1, L]])).then_inc((s_T0, s_T)[n], 16)

                def weights(c):
                    for f in range(2):
                        sp.wait_ge(s_wlg[f], c)
                        sp.wait_ge(s_wld[f], c)
                        sp.dma_start(raw[:, f].rearrange("p a n -> p (a n)"),
                                     w0[bass.ds(c * 2 + f, 1)].rearrange("a p n -> p (a n)")).then_inc(s_raw0[f], 16)

                weights(1)
                sp.wait_ge(s_kw[1], 16)
                for t in range(1, NT):
                    sp.wait_ge(s_conv, 4 * t)
                    sp.dma_start(toep[:], bass.AP(tensor=krev.tensor, offset=t * HPT * KROW,
                                                  ap=[[1, P], [KROW, HPT], [1, L]])).then_inc(s_T, 16)
                sp.dma_start(w_all[:], wq.rearrange("p k n -> p (k n)")).then_inc(s_wall, 16)
                with sp.Fori(2, NC0) as c:
                    weights(c)

                for f in range(2):
                    sp.wait_ge(s_wlg[f], NC0)
                    sp.wait_ge(s_wld[f], NC0)
                    sp.dma_start(raw[:, f].rearrange("p a n -> p (a n)"), w1[f]).then_inc(s_raw0[f], 16)
                with sp.Fori(NC0, CL) as c:
                    for f in range(2):
                        sp.wait_ge(s_wlg[f], c + 1)
                        sp.wait_ge(s_wld[f], c + 1)
                        sp.dma_start(raw[:, f].rearrange("p a n -> p (a n)"),
                                     w1[bass.ds(c * 2 + (2 + f - 2 * NC0), 1)].rearrange("a p n -> p (a n)")).then_inc(s_raw0[f], 16)
                for f in range(2):
                    sp.wait_ge(s_wlg[f], CL + 1)
                    sp.wait_ge(s_wld[f], CL + 1)
                for k in range(KB):
                    if k >= 2:
                        sp.wait_ge(e_wq, k - 1)
                    sp.dma_start(w_blk[k % 2], wq[:, k]).then_inc(e_w[k % 2], 16)
                sp.wait_ge(e_wq, KB)
                sp.dma_start(bias_sb, bass.AP(tensor=bias.tensor, offset=0, ap=[[0, P], [1, L]])).then_inc(e_b, 16)
                for s in range(NSUB):
                    wait_whole(sp, s)
                    sp.dma_start(o_rows[s * P:(s + 1) * P, :], z[:, s]).then_inc(e_out, 16)
                sp.wait_ge(e_out, 16 * NSUB)

            @block.gpsimd
            def _(pool):
                pool.memset(zero[:], 0.0).then_inc(s_grid, 1)
                pool.memset(dm[:], 0.0)
                pool.memset(onehot[:], 0.0)
                for k in range(9):
                    last = pool.memset(pow2[:, k:k + 1], float(1 << k))
                last.then_inc(s_grid, 1)
                pool.iota(lgrid[:, 0:2 * NA], [[0, 2], [-NB, NA]], base=NB * (NA - 1), channel_multiplier=0,
                          allow_small_or_imprecise_dtypes=True)
                pool.iota(lgrid[:, 2 * NA:64], [[-1, NB]], base=NB - 1, channel_multiplier=0,
                          allow_small_or_imprecise_dtypes=True).then_inc(s_grid, 1)
                pool.iota(pos[:], [[P, KB], [0, BATCH]], base=P - 1, channel_multiplier=-1,
                          allow_small_or_imprecise_dtypes=True).then_inc(s_grid, 1)

                def link(ins):
                    pool_chain[0] += 1
                    ins.then_inc(s_plink, 1)
                    pool.wait_ge(s_plink, pool_chain[0])

                def ts(o, i, a, b, op0, op1=None):
                    link(pool.tensor_scalar(o, i, a, b, op0, op1) if op1 is not None
                         else pool.tensor_scalar(o, i, a, 0.0, op0, ALU.add))

                def tt(o, i, j, op):
                    link(pool.tensor_tensor(o, i, j, op))

                def stt(o, i, s, j, op0, op1):
                    ts(t2, i, s, None, op0)
                    tt(o, t2, j, op1)

                def poly_expm1(p, r):
                    ts(p, r, 1.0 / 5040, None, ALU.mult)
                    for c in (1.0 / 720, 1.0 / 120, 1.0 / 24, 1.0 / 6, 0.5, 1.0):
                        stt(p, p, c, r, ALU.add, ALU.mult)

                dt, ea = e2[:, 0], e2[:, 1]
                ai_in, c_re, c_im = par_sb[:, 2], par_sb[:, 3], par_sb[:, 4]
                ar, ai, ut, r0, em, y, nr, ni, den, wr, wi, cr, ci, c1, c2, t0, t1, t2 = (t[:] for t in sm)
                pool.wait_ge(s_par, 16)
                pool.wait_ge(s_step, 1)
                ts(y, ar, -60.0, 1.0 / 64, ALU.max, ALU.mult)
                poly_expm1(em, y)
                for _ in range(6):
                    stt(em, em, 2.0, em, ALU.add, ALU.mult)
                pool.wait_ge(s_sin, 2)
                sn, sh = trig_small[0], trig_small[1]
                tt(t0, sh, sh, ALU.mult)
                ts(t0, t0, 2.0, None, ALU.mult)
                tt(nr, em, t0, ALU.mult)
                tt(nr, em, nr, ALU.subtract)
                tt(nr, nr, t0, ALU.subtract)
                stt(ni, em, 1.0, sn, ALU.add, ALU.mult)
                pool.wait_ge(s_den, 1)
                tt(wr, ni, ai_in, ALU.mult)
                tt(t0, nr, ea, ALU.mult)
                tt(wr, wr, t0, ALU.subtract)
                tt(wr, wr, den, ALU.mult)
                tt(wi, ni, ea, ALU.mult)
                tt(t0, nr, ai_in, ALU.mult)
                tt(wi, wi, t0, ALU.add)
                stt(wi, wi, -1.0, den, ALU.mult, ALU.mult)
                tt(cr, c_re, wr, ALU.mult)
                tt(t0, c_im, wi, ALU.mult)
                tt(cr, cr, t0, ALU.subtract)
                tt(ci, c_re, wi, ALU.mult)
                tt(t0, c_im, wr, ALU.mult)
                tt(ci, ci, t0, ALU.add)
                ts(c1[0:64], cr[0:64], 2.0, None, ALU.mult)
                ts(c1[64:P], ci[64:P], -2.0, None, ALU.mult)
                ts(c2[0:64], ci[0:64], -2.0, None, ALU.mult)
                pool.tensor_scalar(c2[64:P], cr[64:P], -2.0, 0.0, ALU.mult, ALU.add).then_inc(s_coef, 1)

                pool.wait_ge(s_coef, 1)
                link(pool.memset(mag[:, :, NA - 1:NA], 1.0))
                pool.wait_ge(s_pw, 1)
                for k in range(4):
                    n, e = 1 << k, NA
                    tt(mag[:, :, e - 2 * n:e - n], mag[:, :, e - n:e], bc(pw[:, 5 + k], 2, n), ALU.mult)
                pool.sem_inc(s_mag, 1)

                pool.memset(lmask[:], 0.5).then_inc(s_grid, 1)
                pool.wait_ge(s_grid, 5)
                lm = lmask[:].rearrange("p (b h) -> p b h", h=HEADS)
                pool.affine_select(out=lm, in_=lm, compare_op=ALU.is_ge, fill=0.0, base=0,
                                   pattern=[[-RANK, GB], [0, HEADS]], channel_multiplier=1).then_inc(s_grid, 1)
                pool.wait_ge(s_grid, 6)
                pool.affine_select(out=lm, in_=lm, compare_op=ALU.is_ge, fill=0.0, base=RANK - 1,
                                   pattern=[[RANK, GB], [0, HEADS]], channel_multiplier=-1).then_inc(s_grid, 1)
                pool.memset(ident_f[:], 0.0).then_inc(s_id, 1)
                pool.wait_ge(s_id, 1)
                pool.affine_select(out=ident_f[:], in_=ident_f[:], compare_op=ALU.not_equal, fill=1.0, base=0,
                                   pattern=[[-1, P]], channel_multiplier=1).then_inc(s_id, 1)
                pool.memset(ones[:], 1.0).then_inc(s_id, 1)
                pool.memset(epsb[:], EPS).then_inc(s_id, 1)
                pool.wait_ge(s_ix, 16 * GB)
                pool.wait_ge(s_rb, 16)
                pool.tensor_scalar(ixr[:], ixr[:], float(RANK), 0.0, ALU.mult, ALU.add).then_inc(r_row, 1)
                pool.wait_ge(r_row, 1)
                pool.tensor_tensor(rows0[:], ixr[:], rowb[:], ALU.add).then_inc(r_row, 1)
                pool.tensor_tensor(rows[:], ixr[:], rowb[:], ALU.add).then_inc(r_row, 1)

                pool.wait_ge(r_row, 3)
                pool.wait_ge(s_d[1], M1 - NT)
                for g in range(NG):
                    if g >= 2:
                        pool.wait_ge(c_tr[g % 2], g // 2)
                    gather(pool, ar_raw[:, g % 2], tab_a, rows0[:, g:g + 1]).then_inc(c_a[g % 2], 16)
                    if g == 3:
                        pool.wait_ge(s_x1l, KB * NT)
                        pool.memset(acc[:], 0.0).then_inc(v_zero, 1)

                def step(t):
                    for g in range(2):
                        gather(pool, lr_raw[:, g], tab_l, rows[:, 2 * t + g:2 * t + g + 1]).then_inc(r_l, 16)

                def lora_down_rows(t):
                    for g in range(2):
                        gather(pool, bd_raw[:, g], tab_bd, rows0[:, 2 * t + g:2 * t + g + 1]).then_inc(r_bd, 16)

                for i in range(2):
                    pool.wait_ge(c_tr[i], NG // 2)
                step(0)
                for i in range(2):
                    pool.wait_ge(c_tp[i], NG // 2)
                    pool.wait_ge(c_tl[i], NG // 2)
                pool.memset(td[:], 0.0).then_inc(q_tev, 1)
                with pool.Fori(NC0, CL) as c:
                    for t in range(1, NT):
                        pool.wait_ge(r_bl, c * NT + (t - M1))
                        pool.wait_ge(r_lt, c * NT + (t - M1))
                        pool.sem_inc(r_turn, 1)
                        step(t)
                    pool.wait_ge(r_l, c * (32 * NT) + 32 * (NT - M1))
                    pool.sem_inc(r_turn, 1)
                    pool.tensor_scalar(rows[:], rows[:], float(EXP * RANK), 0.0, ALU.add, ALU.add).then_inc(r_next, 1)
                    pool.wait_ge(r_next, c + (1 - NC0))
                    pool.wait_ge(r_bl, c * NT + (NT - M1))
                    pool.wait_ge(r_lt, c * NT + (NT - M1))
                    pool.sem_inc(r_turn, 1)
                    step(0)
                pool.wait_ge(s_wlg[1], CL + 1)
                pool.wait_ge(s_wld[1], CL + 1)
                lora_down_rows(0)

                def x_sums(first, end):
                    for s in range(first, end):
                        if s >= 3:
                            pool.wait_ge(e_xt, s - 2)
                        elif s == 2:
                            pool.wait_ge(e_wq, KB)
                        sl = slice(s * P, (s + 1) * P)
                        pool.tensor_tensor(x_sum[s % 3].rearrange("p (k n) -> p k n", k=KB), a_hi[:, :, sl].bitcast(F32),
                                           a_lo[:, :, sl].bitcast(F32), ALU.add).then_inc(e_xs, 1)

                for t in range(1, NT):
                    pool.wait_ge(r_bl, RL + t)
                    pool.wait_ge(r_lt, RL + t)
                    step(t)
                    if t == 2:
                        pool.wait_ge(s_d[1], ML)
                    if t >= 2:
                        x_sums(4 * t - 8, 4 * t - 4)
                    pool.wait_ge(r_bdl, t)
                    lora_down_rows(t)
                x_sums(8, NSUB)
                for s in range(NSUB):
                    if s in ON_VECTOR:
                        continue
                    pool.wait_ge(e_gb, s + 1)
                    pool.wait_ge(s_ev, ML + s // 4 + 1)
                    pool.tensor_tensor(z[:, s], z[:, s], gb[:, s % GD], ALU.add).then_inc(e_op, 1)

            @block.tensor
            def _(pe):
                pe.wait_ge(s_sf, 4)
                pe.wait_ge(s_grid, 2)
                for t in range(NT):
                    pe.matmul(pk[:, t], onehot[:], dm[:, t * HPT:(t + 1) * HPT, :], start=True, stop=True)
                    for h in range(HPT):
                        last = pe.matmul(pk[:, t, h, :], S[:, t * HPT + h, :], Fm[:, t * HPT + h, :], start=False, stop=True,
                                         skip_group_check=True)
                    last.then_inc(s_kp, 1)

                pe.wait_ge(s_x, 16)
                pe.wait_ge(s_id, 2)

                def conv(t):
                    if t:
                        pe.wait_ge(s_T, 16 * (t + 1))
                    for q in range(4):
                        if t == 0 and q % 2 == 0:
                            pe.wait_ge((s_T0, s_T)[q // 2], 16)
                        j = 4 * t + q
                        bank = conv_bank[q % 2].rearrange("p (i k b) -> p i k b", i=2, k=KB)
                        if j >= 2:
                            pe.wait_ge(s_cmul, j - 1)
                        if q == 1 and t:
                            pe.wait_ge(s_silu[1], t)
                        for i in range(2):
                            hh = 2 * q + i
                            for d in range(KB):
                                last = pe.matmul(bank[:, i, d:KB, :], toep[:, hh, L - P * (d + 1):L - P * d],
                                                 acc4[:, 0:KB - d, :, t * HPT + hh], start=(d == 0), stop=True,
                                                 skip_group_check=True)
                        last.then_inc(s_conv, 1)

                def chunk(c, first, last_chunk):
                    for t in range(NT):
                        m = c * NT + t
                        if first:
                            pe.wait_ge(s_ylo, 4 * (t + 1))
                        for f in range(2):
                            if t == 0:
                                pe.wait_ge(s_wlg[f], c + 1)
                            if not (first and t == 0):
                                pe.wait_ge((s_mul, s_silu)[f][1], m)
                            for k in range(KB):
                                mv = (a_hi4[:, k, :, t * HPT:(t + 1) * HPT], a_lo4[:, k, :, t * HPT:(t + 1) * HPT])
                                last = mm3(pe, ps_gu[G_BANK[f]], gu_hi[:, f, 0, k], gu_lo[:, f, 0, k], *mv,
                                           start=(k == 0), stop=(k == KB - 1))
                            last.then_inc(s_g[f], 1)
                            if f:
                                pe.wait_ge(s_silu[0], m + 1)
                            elif not (first and t == 0):
                                pe.wait_ge(s_mul[0], m)
                            for k in range(KB):
                                mv = (a_hi4[:, k, :, t * HPT:(t + 1) * HPT], a_lo4[:, k, :, t * HPT:(t + 1) * HPT])
                                last = mm3(pe, ps_gu[U_BANK[f]], gu_hi[:, f, 1, k], gu_lo[:, f, 1, k], *mv,
                                           start=(k == 0), stop=(k == KB - 1))
                            last.then_inc(s_u[f], 1)
                        if first and t + 1 < NT:
                            conv(t + 1)
                        for f in range(2):
                            if last_chunk and t == NT - 1:
                                first_group(f)
                            if t == 0:
                                pe.wait_ge(s_wld[f], c + 1)
                            pe.wait_ge(s_hl[f], m + 1)
                            if f == 0 and not (first and t == 0):
                                pe.wait_ge(s_ev, m)
                            for k in range(KB):
                                last = mm3(pe, ps_d[:, k], dn_hi[:, f, k * P:(k + 1) * P], dn_lo[:, f, k * P:(k + 1) * P],
                                           h_hi[:, f], h_lo[:, f], start=(f == 0), stop=(f == 1), skip=True)
                            last.then_inc(s_d[f], 1)

                def first_group(u):
                    pe.wait_ge(c_a[u], 16)
                    if u:
                        pe.wait_ge(s_mul[1], M1)
                    else:
                        pe.wait_ge(s_silu[1], M1)
                    for j in range(2 * KB):
                        last = pe.transpose(first_bank[u][j // KB][:, (j % KB) * P:(j % KB + 1) * P],
                                            ar_raw[:, u, j * P:(j + 1) * P], ident_f[:])
                    last.then_inc(c_tr[u], 1)

                conv(0)
                chunk(0, True, False)
                with pe.Fori(1, NC0 - 1) as c:
                    chunk(c, False, False)
                chunk(NC0 - 1, False, True)

                def transposes(u, n):
                    pe.wait_ge(c_a[u], n * 16 + 16)
                    past(pe, c_al[u], n)
                    for j in range(2 * KB):
                        last = pe.transpose(a_bank[u][:, j * P:(j + 1) * P], ar_raw[:, u, j * P:(j + 1) * P], ident_f[:])
                    last.then_inc(c_tr[u], 1)

                def pair(i, last_pair):
                    for u in range(2):
                        first = isinstance(i, int) and i == 0
                        if first and u:
                            pe.wait_ge(s_ev, M1)
                        if not (last_pair and u or first and not u):
                            transposes(1 - u, i + u)
                        pe.wait_ge(c_al[u], i + 1)
                        past(pe, c_tm[u], i)
                        at = bass.ds(i * (2 * GT) + u * GT, GT)
                        for w in range(2):
                            for k in range(KB):
                                if first and u == 0 and w == 0:
                                    pe.wait_ge(s_x1l, KB * (NT - 1) + k + 1)
                                last = mm3(pe, t_bank[u][:, w], ar_hi[:, u, w * KB + k], ar_lo[:, u, w * KB + k],
                                           a_hi[:, k, at], a_lo[:, k, at], start=(k == 0), stop=(k == KB - 1), skip=True)
                        last.then_inc(c_tp[u], 1)

                pair(0, False)
                with pe.Fori(1, NG // 2 - 1) as i:
                    pair(i, False)
                pair(NG // 2 - 1, True)

                def gate_up(bank, w, f, slot, t, b_ready):
                    at = slice(t * TT, (t + 1) * TT)
                    for k in range(KB):
                        mm3(pe, bank, gu_hi[:, f, w, k], gu_lo[:, f, w, k], a_hi[:, k, at], a_lo[:, k, at],
                            start=(k == 0), stop=(k == KB - 1))
                    pe.wait_ge(r_bl, b_ready)
                    for g in range(2):
                        at = slice((2 * t + g) * GT, (2 * t + g + 1) * GT)
                        wn = slice(w * P, (w + 1) * P)
                        last = mm3(pe, bank[:, g * GT:(g + 1) * GT], b_hi[:, slot, g, wn], b_lo[:, slot, g, wn],
                                   t_hi[:, w, at], t_lo[:, w, at], start=False, stop=True, skip=True)
                    return last

                def transposes(bank, nf, r):
                    pe.wait_ge(r_l, r * 32 + 32)
                    for f in range(nf):
                        for g in range(2):
                            last = pe.transpose(bank[:, (2 * f + g) * P:(2 * f + g + 1) * P],
                                                lr_raw[:, g, (4 + f) * P:(5 + f) * P], ident_f[:])
                    last.then_inc(r_lt, 1)

                def down(nf, c, t, m):
                    for f in range(nf):
                        if t == 0:
                            pe.wait_ge(s_wld[f], c + 1)
                        pe.wait_ge(s_hl[f], m + 1)
                        if f == 0:
                            pe.wait_ge(s_ev, m)
                        for s in range(4):
                            sl = slice(s * P, (s + 1) * P)
                            last = mm3(pe, ps_d[:, s], h_hi[:, f, sl], h_lo[:, f, sl], dn_hi[:, f], dn_lo[:, f],
                                       start=(f == 0), stop=(f == nf - 1 and nf == 2), skip=True)
                    last.then_inc(s_d[1], 1)

                def lora_hidden(slots, m):
                    for f, slot in enumerate(slots):
                        pe.wait_ge(s_hl[f], m + 1)
                        for g in range(2):
                            sl = slice(g * P, (g + 1) * P)
                            last = mm3(pe, ps_t[:, g * GT:(g + 1) * GT], ad_hi[:, slot, sl], ad_lo[:, slot, sl],
                                       h_hi[:, f, g * GT:(g + 1) * GT], h_lo[:, f, g * GT:(g + 1) * GT],
                                       start=(f == 0 and g == 0), stop=(f == len(slots) - 1), skip=True)
                    last.then_inc(q_td, 1)

                pe.sem_inc(q_td, 1)
                with pe.Fori(NC0, CL) as c:
                    for t in range(NT):
                        m = c * NT + t
                        r = c * NT + (t - M1)
                        for f in range(2):
                            if t == 0:
                                pe.wait_ge(s_wlg[f], c + 1)
                            pe.wait_ge((s_mul, s_silu)[f][1], m)
                            gate_up(ps_gu[G_BANK[f]], 0, f, f, t, r + 1).then_inc(s_g[f], 1)
                            if f:
                                pe.wait_ge(s_silu[0], m + 1)
                            else:
                                pe.wait_ge(s_mul[0], m)
                            gate_up(ps_gu[U_BANK[f]], 1, f, f, t, r + 1).then_inc(s_u[f], 1)
                            if f == 0:
                                pe.wait_ge(q_tev, r + 1)
                                transposes(ps_t, 2, r)
                        down(2, c, t, m)
                        pe.wait_ge(r_adl, r + 1)
                        lora_hidden((0, 1), m)

                def x_rows(t):
                    pe.wait_ge(e_zf, t + 1)
                    for s in range(4):
                        pe.wait_ge(e_xs, 4 * t + s + 1)
                        for k in range(KB):
                            sl = slice(k * P, (k + 1) * P)
                            last = pe.transpose(ps_d[:, s, sl], x_sum[(4 * t + s) % 3][:, sl], ident_f[:])
                        last.then_inc(e_xt, 1)

                def quantised(t):
                    pe.wait_ge(r_adl, RL + min(t + 3, NT))
                    pe.wait_ge(q_tev, RL + (t + 3, t + 3, NT + 1, NT + 1)[t])
                    for j in range(2):
                        if t:
                            pe.wait_ge(e_qt, 2 * t - 1 + j)
                        pe.wait_ge(e_qb, 4 * t + 2 * j + 2)
                        for n in range(2 * KB):
                            last = pe.transpose(q_bank[j][:, n * P:(n + 1) * P], qb[:, j, n * P:(n + 1) * P], ident_b[:])
                        last.then_inc(e_tp, 1)

                def ahead(t):
                    m = ML + t
                    if t == 0:
                        pe.wait_ge(s_wlg[0], CL + 1)
                        pe.wait_ge(s_mul[1], m)
                        pe.wait_ge(s_silu[1], m)
                        pe.wait_ge(s_wsum, 1)
                        pe.wait_ge(s_id, 4)
                        pe.matmul(ps_gu[2][:, 0:1], ones[:], wsum[:], start=True, stop=True).then_inc(e_wp, 1)
                    else:
                        pe.wait_ge(s_silu[0], m)
                    gate_up(ps_gu[0], 0, 0, t % 2, t, RL + t + 1).then_inc(s_g[0], 1)
                    if t == 0:
                        pe.wait_ge(e_wm, 1)
                        transposes(ps_gu[2], 1, RL)
                    if t == 3:
                        quantised(0)
                    if t >= 2:
                        x_rows(t - 2)
                    pe.wait_ge(s_mul[0], m)
                    gate_up(ps_gu[1], 1, 0, t % 2, t, RL + t + 1).then_inc(s_u[0], 1)
                    if t:
                        pe.wait_ge(r_adl, RL + t)
                        if t == 3:
                            pe.wait_ge(e_qt, 1)
                        transposes(ps_gu[2], 1, RL + t)

                def products(first, end):
                    for s in range(first, end):
                        t = s // 4
                        pe.wait_ge(e_qt, s // 2 + 1)
                        if s >= 2:
                            pe.wait_ge(e_yb, s - 1)
                        for k in range(KB):
                            at = (s % 2) * L + k * P
                            last = pe.matmul(ps_y[s % 2], q_t[:, (s % 4) // 2, t, at:at + P], w_q[:, k],
                                             start=(k == 0), stop=(k == KB - 1))
                        last.then_inc(e_y, 1)

                ahead(0)
                for t in range(NT):
                    m = ML + t
                    if t + 1 < NT:
                        ahead(t + 1)
                    else:
                        quantised(1)
                        x_rows(2)
                    pe.wait_ge(r_adl, RL + t + 1)
                    if t >= 2:
                        pe.wait_ge(e_qt, 2 * t - 2)
                    pe.wait_ge(q_tev, RL + t + 1)
                    lora_hidden((t % 2,), m)
                    if t == NT - 1:
                        pe.wait_ge(e_wq, KB)
                        pe.wait_ge(s_mul[0], ML + NT)
                        pe.wait_ge(s_silu[0], ML + NT)
                        products(0, 2)
                    down(1, CL, t, m)
                    pe.wait_ge(r_tdl, t + 1)
                    pe.wait_ge(r_bdl, t + 1)
                    for s in range(4):
                        sl = slice(s * P, (s + 1) * P)
                        last = mm3(pe, ps_d[:, s], h_hi[:, 1, sl], h_lo[:, 1, sl], bd_hi[:, s // 2], bd_lo[:, s // 2],
                                   start=False, stop=True, skip=True)
                    last.then_inc(q_bd, 1)
                products(2, 3)
                quantised(2)
                x_rows(3)
                products(3, 7)
                quantised(3)
                products(7, NSUB)

            @block.scalar
            def _(act):
                act.wait_ge(s_step, 1)
                act.activation(trig_small[0], sm[3][:], ACT.Sin, scale=TWO_PI).then_inc(s_sin, 1)
                act.activation(trig_small[1], sm[3][:], ACT.Sin, scale=TWO_PI / 2).then_inc(s_sin, 1)
                act.wait_ge(s_theta, 1)
                act.activation(trig, theta, ACT.Sin, scale=TWO_PI).then_inc(s_sin, 1)
                for t in range(NT):
                    act.wait_ge(s_kp, t + 1)
                    act.activation(k_sb[:, t * HPT:(t + 1) * HPT], pk[:, t], ACT.Copy).then_inc(s_ks, 1)
                for f in range(2):
                    act.wait_ge(s_wsc[f], 1)
                    act.activation(gu_hi[:, f].rearrange("p a k n -> p (a k n)"),
                                   raw[:, f, 0:2].rearrange("p a n -> p (a n)"), ACT.Copy).then_inc(s_whg[f], 1)
                    act.activation(dn_hi[:, f], raw[:, f, 2], ACT.Copy).then_inc(s_whd[f], 1)

                def conv_high(t):
                    for q in range(4):
                        h0 = t * HPT + 2 * q
                        act.wait_ge(s_cmul, 4 * t + q + 1)
                        act.activation(a_hi4[:, :, :, h0:h0 + 2].rearrange("p k b h -> p h k b"),
                                       ytmp[:, q % 2].rearrange("p h (k b) -> p h k b", k=KB), ACT.Copy).then_inc(s_yhi, 1)

                conv_high(0)

                def chunk(c, first, last_chunk):
                    for t in range(NT):
                        m = c * NT + t
                        for f in range(2):
                            act.wait_ge(s_g[f], m + 1)
                            if not (first and t == 0):
                                act.wait_ge(s_hl[f], m)
                            act.activation(s_act[:, f], ps_gu[G_BANK[f]], ACT.Silu).then_inc(s_silu[f], 1)
                            act.wait_ge(s_mul[f], m + 1)
                            if not (first and t == 0):
                                act.wait_ge(s_d[f], m)
                            act.activation(h_hi[:, f], s_act[:, f], ACT.Copy).then_inc(s_hh[f], 1)
                            if t == NT - 1:
                                if last_chunk:
                                    act.wait_ge(s_raw0[f], 16 * (NC0 + 1))
                                else:
                                    act.wait_ge(s_wsc[f], c + 2)
                                act.wait_ge(s_u[f], m + 1)
                                act.activation(gu_hi[:, f].rearrange("p a k n -> p (a k n)"),
                                               raw[:, f, 0:2].rearrange("p a n -> p (a n)"), ACT.Copy).then_inc(s_whg[f], 1)
                        if first and t + 1 < NT:
                            conv_high(t + 1)
                        if last_chunk and t == NT - 1:
                            for u in range(2):
                                act.wait_ge(c_tr[u], 1)
                                for w in range(2):
                                    ins = act.activation(ar_hi[:, u, w * KB:(w + 1) * KB].rearrange("p k n -> p (k n)"),
                                                         first_bank[u][w], ACT.Copy)
                                ins.then_inc(c_ah[u], 1)
                        if last_chunk:
                            for k in range(KB):
                                if k < KB - 1:
                                    act.wait_ge(s_evk, (KB - 1) * t + k + 1)
                                else:
                                    act.wait_ge(s_ev, m + 1)
                                act.activation(x_tile(a_hi4, t, k), x_tile(acc4, t, k), ACT.Copy).then_inc(s_x1h, 1)
                        if t == NT - 1:
                            for f in range(2):
                                act.wait_ge(s_d[f], m + 1)
                                act.activation(dn_hi[:, f], raw[:, f, 2], ACT.Copy).then_inc(s_whd[f], 1)

                chunk(0, True, False)
                with act.Fori(1, NC0 - 1) as c:
                    chunk(c, False, False)
                chunk(NC0 - 1, False, True)

                def split(u, n):
                    act.wait_ge(c_tr[u], n + 1)
                    past(act, c_tp[u], n)
                    act.activation(ar_hi[:, u].rearrange("p k n -> p (k n)"), a_bank[u], ACT.Copy).then_inc(c_ah[u], 1)

                def pair(i, last_pair):
                    for u in range(2):
                        first = isinstance(i, int) and i == 0
                        if not (last_pair and u or first and not u):
                            split(1 - u, i + u)
                        act.wait_ge(c_tm[u], i + 1)
                        act.activation(t_hi[:, :, bass.ds(i * (2 * GT) + u * GT, GT)],
                                       tm[:, u].rearrange("p (a n) -> p a n", a=2), ACT.Copy).then_inc(c_th[u], 1)

                pair(0, False)
                with act.Fori(1, NG // 2 - 1) as i:
                    pair(i, False)
                pair(NG // 2 - 1, True)

                def gate(f, m):
                    act.wait_ge(s_g[f], m + 1)
                    act.wait_ge(s_hl[f], m)
                    act.activation(s_act[:, f], ps_gu[G_BANK[f]], ACT.Silu).then_inc(s_silu[f], 1)

                def hidden_high(f, m, r):
                    act.wait_ge(s_mul[f], m + 1)
                    act.wait_ge(s_d[1], m)
                    act.wait_ge(q_td, r + 1)
                    act.activation(h_hi[:, f], s_act[:, f], ACT.Copy).then_inc(s_hh[f], 1)

                def down_rows(bank, slots, r):
                    act.wait_ge(r_lt, r + 1)
                    n = 2 * P * len(slots)
                    act.activation(ad_hi[:, slots[0]:slots[-1] + 1].rearrange("p f n -> p (f n)"), bank[:, 0:n],
                                   ACT.Copy).then_inc(r_adh, 1)

                def b_split(r):
                    act.wait_ge(r_l, r * 32 + 32)
                    for f in range(2):
                        act.activation(b_hi[:, f], b_rows(f), ACT.Copy).then_inc(r_bh, 1)

                act.wait_ge(c_tp[0], NG // 2)
                b_split(0)
                with act.Fori(NC0, CL) as c:
                    for t in range(NT):
                        m = c * NT + t
                        r = c * NT + (t - M1)
                        last_tile = t == NT - 1
                        for f in range(2):
                            gate(f, m)
                            hidden_high(f, m, r)
                            if f == 0:
                                act.wait_ge(q_td, r + 1)
                                down_rows(ps_t, (0, 1), r)
                            if last_tile:
                                act.wait_ge(s_raw0[f], c * 16 + 32)
                                act.wait_ge(s_u[f], m + 1)
                                act.activation(gu_hi[:, f].rearrange("p a k n -> p (a k n)"), lanes(raw[:, f]),
                                               ACT.Copy).then_inc(s_whg[f], 1)
                        act.wait_ge(s_u[1], m + 1)
                        b_split(r + 1)
                        if last_tile:
                            act.wait_ge(s_d[1], m + 1)
                            for f in range(2):
                                act.activation(dn_hi[:, f], raw[:, f, 2], ACT.Copy).then_inc(s_whd[f], 1)

                def b_split_last(t):
                    act.wait_ge(r_l, (RL + t) * 32 + 32)
                    if t >= 2:
                        act.wait_ge(s_u[0], ML + t - 1)
                    act.activation(b_hi[:, t % 2], b_rows(0), ACT.Copy).then_inc(r_bh, 1)

                def bd_split(t):
                    act.wait_ge(r_bd, (t + 1) * 32)
                    act.wait_ge(s_u[1], ML)
                    if t:
                        act.wait_ge(q_bd, t)
                    act.activation(bd_hi, bd_raw, ACT.Copy).then_inc(r_bdh, 1)

                def statistics(t):
                    act.wait_ge(e_zf, t + 1)
                    for i in range(4):
                        s = 4 * t + i
                        if s >= 2:
                            act.wait_ge(e_ss, s - 1)
                        act.activation(junk[:, s % 2], zf[:, i // 2, (i % 2) * L:(i % 2 + 1) * L], ACT.Square,
                                       accum_out=ss[:, s:s + 1]).then_inc(e_ss, 1)
                    act.wait_ge(e_ss, 4 * t + 4)
                    act.activation(ra[:, 4 * t:4 * t + 4], ss[:, 4 * t:4 * t + 4], ACT.Sqrt, scale=1.0 / L,
                                   bias=epsb[:]).then_inc(e_rt, 1)

                def z_sub(i):
                    return zf[:, i // 2, (i % 2) * L:(i % 2 + 1) * L]

                def scaled(t):
                    act.wait_ge(e_cc, t + 1)
                    act.wait_ge(s_ev, ML + t + 1)
                    for i in range(4):
                        act.activation(z_sub(i), z_sub(i), ACT.Copy, scale=cc[:, 4 * t + i:4 * t + i + 1],
                                       bias=MAGIC).then_inc(e_qm, 1)

                def to_bf16(t):
                    for i in range(4):
                        act.wait_ge(e_cl, 4 * t + i + 1)
                        if t == 0:
                            act.wait_ge(s_u[0], ML + 3)
                        else:
                            act.wait_ge(e_tp, 2 * t)
                        at = slice((i % 2) * L, (i % 2 + 1) * L)
                        act.activation(qb[:, i // 2, at], z_sub(i), ACT.Copy, bias=-MAGIC).then_inc(e_qb, 1)

                def keep_quantised(t):
                    for j in range(2):
                        act.wait_ge(e_tp, 2 * t + j + 1)
                        act.activation(q_t[:, j, t], q_bank[j], ACT.Copy).then_inc(e_qt, 1)

                def tile_rows(t):
                    act.wait_ge(q_td, RL + t if t >= 2 else RL + 1)
                    down_rows(ps_gu[2], (t % 2,), RL + t)

                gate(0, ML)
                hidden_high(0, ML, RL)
                tile_rows(0)
                b_split_last(1)
                bd_split(0)
                gate(0, ML + 1)
                tile_rows(1)
                for t in range(NT):
                    act.wait_ge(r_tdm, t + 1)
                    if t:
                        act.wait_ge(q_bd, t)
                    act.activation(h_hi[:, 1], tdm, ACT.Copy).then_inc(r_tdh, 1)
                    if t + 1 < NT:
                        hidden_high(0, ML + t + 1, RL + t + 1)
                        if t:
                            tile_rows(t + 1)
                    if t + 2 < NT:
                        b_split_last(t + 2)
                    if t:
                        to_bf16(t - 1)
                    if t + 1 < NT:
                        bd_split(t + 1)
                    if t == 2:
                        keep_quantised(t - 1)
                    statistics(t)
                    if t in (1, 3):
                        keep_quantised(t - 1)
                    if t + 2 < NT:
                        gate(0, ML + t + 2)
                    if t + 1 < NT:
                        scaled(t)

                def gelu(first, end):
                    for s in range(first, end):
                        act.wait_ge(e_yb, s + 1)
                        if s >= GD:
                            wait_whole(act, s - GD)
                        act.activation(gb[:, s % GD], yb[:, s % YD], ACT.Gelu).then_inc(e_gb, 1)

                gelu(0, 1)
                scaled(3)
                gelu(1, YD)
                to_bf16(3)
                gelu(YD, 5)
                keep_quantised(3)
                gelu(5, NSUB)

            @block.vector
            def _(dve):
                def link(ins):
                    chain[0] += 1
                    ins.then_inc(s_chain, 1)
                    dve.wait_ge(s_chain, chain[0])

                def ts(o, i, a, b, op0, op1=None):
                    link(dve.tensor_scalar(o, i, a, b, op0, op1) if op1 is not None
                         else dve.tensor_scalar(o, i, a, None, op0))

                def tt(o, i, j, op):
                    link(dve.tensor_tensor(o, i, j, op))

                def stt(o, i, s, j, op0, op1):
                    link(dve.scalar_tensor_tensor(out=o, in0=i, scalar=s, in1=j, op0=op0, op1=op1))

                def poly_expm1(p, r):
                    ts(p, r, 1.0 / 5040, None, ALU.mult)
                    for c in (1.0 / 720, 1.0 / 120, 1.0 / 24, 1.0 / 6, 0.5, 1.0):
                        stt(p, p, c, r, ALU.add, ALU.mult)

                def exp32(o, i, n):
                    xc, k, r, p = (t[:, 0:n] for t in tmp)
                    ki = kint[:, 0:n]
                    ts(xc, i, -87.0, 88.0, ALU.max, ALU.min)
                    ts(k, xc, LOG2E, MAGIC, ALU.mult, ALU.add)
                    ts(k, k, MAGIC, None, ALU.subtract)
                    stt(r, k, -LN2_HI, xc, ALU.mult, ALU.add)
                    stt(r, k, -LN2_LO, r, ALU.mult, ALU.add)
                    poly_expm1(p, r)
                    ts(ki, k, 127.0, float(1 << 23), ALU.add, ALU.mult)
                    stt(o, p, 1.0, ki.bitcast(F32), ALU.add, ALU.mult)

                dve.wait_ge(s_par, 16)
                exp32(e2[:].rearrange("p a h -> p (a h)"), par_sb[:, 0:2].rearrange("p a h -> p (a h)"), 2 * HEADS)
                dt, ea = e2[:, 0], e2[:, 1]
                ai_in, c_re, c_im = par_sb[:, 2], par_sb[:, 3], par_sb[:, 4]
                ar, ai, ut, r0, em, y, nr, ni, den, wr, wi, cr, ci, c1, c2, t0, t1, t2 = (t[:] for t in sm)
                stt(ar, ea, -1.0, dt, ALU.mult, ALU.mult)
                tt(ai, ai_in, dt, ALU.mult)
                ts(ut, ai, 0.15915494309189535, None, ALU.mult)
                ts(r0, ut, MAGIC, MAGIC, ALU.add, ALU.subtract)
                tt(r0, ut, r0, ALU.subtract)
                dve.sem_inc(s_step, 1)
                dve.wait_ge(s_grid, 3)
                tt(theta, bc(r0, 2, 64), bc(lgrid[:], 1, HEADS), ALU.mult)
                ts(theta[:, :, 0:NA], theta[:, :, 0:NA], 0.25, None, ALU.add)
                ts(theta[0:64, :, 2 * NA:64], theta[0:64, :, 2 * NA:64], 0.25, None, ALU.add)
                ts(rnd, theta, MAGIC, MAGIC, ALU.add, ALU.subtract)
                dve.tensor_tensor(theta, theta, rnd, ALU.subtract).then_inc(s_theta, 1)
                tt(den, ea, ea, ALU.mult)
                tt(t1, ai_in, ai_in, ALU.mult)
                tt(den, den, t1, ALU.add)
                dve.reciprocal(den, den).then_inc(s_den, 1)
                tt(pin[:], bc(ar, 1, 9), bc(pow2[:], 2, HEADS), ALU.mult)
                exp32(pw[:].rearrange("p a h -> p (a h)"), pin[:].rearrange("p a h -> p (a h)"), 9 * HEADS)
                dve.sem_inc(s_pw, 1)
                link(dve.memset(mag[:, :, NA + NB - 1:NA + NB], 1.0))
                for k in range(5):
                    n, e = 1 << k, NA + NB
                    tt(mag[:, :, e - 2 * n:e - n], mag[:, :, e - n:e], bc(pw[:, k], 2, n), ALU.mult)
                dve.wait_ge(s_sin, 3)
                dve.wait_ge(s_coef, 1)
                tt(S[:], bc(c1, 2, NA), trig[:, :, 0:NA], ALU.mult)
                tt(S2[:], bc(c2, 2, NA), trig[:, :, NA:2 * NA], ALU.mult)
                tt(S[:], S[:], S2[:], ALU.add)
                dve.tensor_tensor(Fm[:], trig[:, :, 2 * NA:64], mag[:, :, NA:NA + NB], ALU.mult).then_inc(s_sf, 1)
                dve.wait_ge(s_mag, 1)
                dve.tensor_tensor(S[:], S[:], mag[:, :, 0:NA], ALU.mult).then_inc(s_sf, 1)
                dve.wait_ge(s_drow, 16)
                dve.tensor_copy(dm[:, :, NB - 1], drow[:]).then_inc(s_sf, 1)
                dve.memset(onehot[:, NA - 1:NA], 1.0).then_inc(s_sf, 1)
                dve.wait_ge(s_len, 16)
                link(dve.tensor_copy(len_f[:], len_i[:]))
                dve.wait_ge(s_grid, 4)
                link(dve.tensor_tensor(cmask[:], pos[:], bc(len_f[:], 1, KB), ALU.is_lt))
                dve.wait_ge(s_sc0, 16)
                for f in range(2):
                    dve.wait_ge(s_raw0[f], 16)
                    w = raw[:, f].rearrange("p a (k n) -> p (a k) n", n=P)
                    dve.tensor_tensor(w, w, bc(scale0[:, f], 2, P), ALU.mult).then_inc(s_wsc[f], 1)
                for f in range(2):
                    dve.wait_ge(s_whg[f], 1)
                    dve.tensor_tensor(gu_lo[:, f].rearrange("p a k n -> p (a k n)"), raw[:, f, 0:2].rearrange("p a n -> p (a n)"),
                                      gu_hi[:, f].rearrange("p a k n -> p (a k n)").bitcast(F32),
                                      ALU.subtract).then_inc(s_wlg[f], 1)
                    dve.wait_ge(s_whd[f], 1)
                    dve.tensor_tensor(dn_lo[:, f], raw[:, f, 2], dn_hi[:, f].bitcast(F32), ALU.subtract).then_inc(s_wld[f], 1)

                def low_half(t, q):
                    j = 4 * t + q
                    h0 = t * HPT + 2 * q
                    dve.wait_ge(s_yhi, j + 1)
                    hv = a_hi4[:, :, :, h0:h0 + 2].rearrange("p k b h -> p h k b").bitcast(F32)
                    dve.tensor_tensor(a_lo4[:, :, :, h0:h0 + 2].rearrange("p k b h -> p h k b"),
                                      ytmp[:, q % 2].rearrange("p h (k b) -> p h k b", k=KB), hv, ALU.subtract).then_inc(s_ylo, 1)

                def masked(t):
                    for q in range(4):
                        dve.wait_ge(s_conv, 4 * t + q + 1)
                        if 4 * t + q >= 2:
                            dve.wait_ge(s_yhi, 4 * t + q - 1)
                            dve.wait_ge(s_ylo, 4 * t + q - 1)
                        dve.tensor_tensor(ytmp[:, q % 2], conv_bank[q % 2].rearrange("p (i n) -> p i n", i=2),
                                          bc(cmask[:].rearrange("p k b -> p (k b)"), 1, 2), ALU.mult).then_inc(s_cmul, 1)
                        if q:
                            low_half(t, q - 1)
                    low_half(t, 3)

                def chunk(c, first, last_chunk):
                    for t in range(NT):
                        m = c * NT + t
                        for f in range(2):
                            dve.wait_ge(s_u[f], m + 1)
                            dve.wait_ge(s_silu[f], m + 1)
                            dve.tensor_tensor(s_act[:, f], s_act[:, f], ps_gu[U_BANK[f]], ALU.mult).then_inc(s_mul[f], 1)
                            dve.wait_ge(s_hh[f], m + 1)
                            if not (first and t == 0):
                                dve.wait_ge(s_d[f], m)
                            dve.tensor_tensor(h_lo[:, f], s_act[:, f], h_hi[:, f].bitcast(F32), ALU.subtract).then_inc(s_hl[f], 1)
                            if t == NT - 1:
                                dve.wait_ge(s_whg[f], c + 2)
                                dve.tensor_tensor(gu_lo[:, f].rearrange("p a k n -> p (a k n)"),
                                                  raw[:, f, 0:2].rearrange("p a n -> p (a n)"),
                                                  gu_hi[:, f].rearrange("p a k n -> p (a k n)").bitcast(F32),
                                                  ALU.subtract).then_inc(s_wlg[f], 1)
                        if first and t + 1 < NT:
                            masked(t + 1)
                        if t == 1 and not last_chunk:
                            for f in range(2):
                                dve.wait_ge(s_raw0[f], c * 16 + 32)
                                w = raw[:, f].rearrange("p a (k n) -> p (a k) n", n=P)
                                sc = scale0[:, bass.ds(c * 2 + (2 + f), 1)].rearrange("p a c -> p (a c)")
                                dve.tensor_tensor(w, w, bc(sc, 2, P), ALU.mult).then_inc(s_wsc[f], 1)
                        if last_chunk and t == NT - 1:
                            for u in range(2):
                                dve.wait_ge(c_ah[u], 1)
                                for w in range(2):
                                    sl = slice(w * KB, (w + 1) * KB)
                                    ins = dve.tensor_tensor(ar_lo[:, u, sl].rearrange("p k n -> p (k n)"), first_bank[u][w],
                                                            ar_hi[:, u, sl].rearrange("p k n -> p (k n)").bitcast(F32), ALU.subtract)
                                ins.then_inc(c_al[u], 1)
                        dve.wait_ge(s_d[1], m + 1)
                        if last_chunk:
                            for k in range(KB + 1):
                                if k < KB:
                                    v = x_tile(acc4, t, k)
                                    dve.tensor_tensor(v, v, ps_d[:, k].rearrange("p (b h) -> p b h", h=HPT),
                                                      ALU.add).then_inc(s_evk if k < KB - 1 else s_ev, 1)
                                if k:
                                    dve.wait_ge(s_x1h, KB * t + k)
                                    dve.tensor_tensor(x_tile(a_lo4, t, k - 1), x_tile(acc4, t, k - 1),
                                                      x_tile(a_hi4, t, k - 1).bitcast(F32), ALU.subtract).then_inc(s_x1l, 1)
                        else:
                            dve.tensor_tensor(acc_tile[t], acc_tile[t],
                                              ps_d[:].rearrange("p k (b h) -> p k b h", h=HPT), ALU.add).then_inc(s_ev, 1)
                        if t == NT - 1:
                            for f in range(2):
                                dve.wait_ge(s_whd[f], c + 2)
                                dve.tensor_tensor(dn_lo[:, f], raw[:, f, 2], dn_hi[:, f].bitcast(F32),
                                                  ALU.subtract).then_inc(s_wld[f], 1)

                dve.wait_ge(s_id, 2)
                dve.tensor_copy(ident_b[:], ident_f[:]).then_inc(s_id, 1)
                masked(0)
                chunk(0, True, False)
                dve.wait_ge(s_wall, 16)
                dve.tensor_reduce(wsum[:], w_all[:], AX.X, ALU.add, apply_absolute_value=True).then_inc(s_wsum, 1)
                with dve.Fori(1, NC0 - 1) as c:
                    chunk(c, False, False)
                chunk(NC0 - 1, False, True)

                def split(u, n):
                    dve.wait_ge(c_ah[u], n + 1)
                    dve.tensor_tensor(ar_lo[:, u].rearrange("p k n -> p (k n)"), a_bank[u],
                                      ar_hi[:, u].rearrange("p k n -> p (k n)").bitcast(F32), ALU.subtract).then_inc(c_al[u], 1)

                def pair(i, last_pair):
                    for u in range(2):
                        first = isinstance(i, int) and i == 0
                        if not (last_pair and u or first and not u):
                            split(1 - u, i + u)
                        dve.wait_ge(c_tp[u], i + 1)
                        past(dve, c_tl[u], i)
                        dve.tensor_tensor(tm[:, u].rearrange("p (a n) -> p a n", a=2), t_bank[u],
                                          bc(lmask[:], 1, 2), ALU.mult).then_inc(c_tm[u], 1)
                        dve.wait_ge(c_th[u], i + 1)
                        at = bass.ds(i * (2 * GT) + u * GT, GT)
                        dve.tensor_tensor(t_lo[:, :, at], tm[:, u].rearrange("p (a n) -> p a n", a=2),
                                          t_hi[:, :, at].bitcast(F32), ALU.subtract).then_inc(c_tl[u], 1)

                pair(0, False)
                with dve.Fori(1, NG // 2 - 1) as i:
                    pair(i, False)
                pair(NG // 2 - 1, True)

                def link(ins):
                    chain[0] += 1
                    ins.then_inc(s_chain, 1)
                    dve.wait_ge(s_chain, chain[0])

                def up(f, m):
                    dve.wait_ge(s_u[f], m + 1)
                    dve.wait_ge(s_silu[f], m + 1)
                    dve.tensor_tensor(s_act[:, f], s_act[:, f], ps_gu[U_BANK[f]], ALU.mult).then_inc(s_mul[f], 1)

                def hidden_low(f, m):
                    dve.wait_ge(s_hh[f], m + 1)
                    dve.tensor_tensor(h_lo[:, f], s_act[:, f], h_hi[:, f].bitcast(F32), ALU.subtract).then_inc(s_hl[f], 1)

                def down_rows(bank, slots, r):
                    dve.wait_ge(r_adh, r + 1)
                    n = 2 * P * len(slots)
                    sl = slice(slots[0], slots[-1] + 1)
                    dve.tensor_tensor(ad_lo[:, sl].rearrange("p f n -> p (f n)"), bank[:, 0:n],
                                      ad_hi[:, sl].rearrange("p f n -> p (f n)").bitcast(F32), ALU.subtract).then_inc(r_adl, 1)

                def td_add(t, r):
                    dve.wait_ge(q_td, r + 2)
                    ts = td[:, t * TT:(t + 1) * TT]
                    dve.tensor_tensor(ts, ts, ps_t[:], ALU.add).then_inc(q_tev, 1)

                def b_split(n):
                    for f in range(2):
                        dve.wait_ge(r_bh, n + f + 1)
                        ins = dve.tensor_tensor(b_lo[:, f], b_rows(f), b_hi[:, f].bitcast(F32), ALU.subtract)
                        ins.then_inc((r_bl0, r_bl)[f], 1)

                b_split(0)
                dve.wait_ge(v_zero, 1)
                dve.wait_ge(q_tev, 1)
                with dve.Fori(NC0, CL) as c:
                    for t in range(NT):
                        m = c * NT + t
                        r = c * NT + (t - M1)
                        last_tile = t == NT - 1
                        for f in range(2):
                            up(f, m)
                            hidden_low(f, m)
                            if f == 0:
                                down_rows(ps_t, (0, 1), r)
                            if last_tile:
                                dve.wait_ge(s_whg[f], c + 2)
                                dve.tensor_tensor(gu_lo[:, f].rearrange("p a k n -> p (a k n)"), lanes(raw[:, f]),
                                                  gu_hi[:, f].rearrange("p a k n -> p (a k n)").bitcast(F32),
                                                  ALU.subtract).then_inc(s_wlg[f], 1)
                        b_split(c * (2 * NT) + 2 * (t - M1) + 2)
                        dve.wait_ge(s_d[1], m + 1)
                        zt = z[:, 4 * t:4 * t + 4]
                        dve.tensor_tensor(zt, zt, ps_d[:], ALU.add).then_inc(s_ev, 1)
                        td_add(t, r)
                        if last_tile:
                            for f in range(2):
                                dve.wait_ge(s_whd[f], c + 2)
                                dve.tensor_tensor(dn_lo[:, f], raw[:, f, 2], dn_hi[:, f].bitcast(F32),
                                                  ALU.subtract).then_inc(s_wld[f], 1)

                def b_split_last(t):
                    dve.wait_ge(r_bh, 2 * RL + 2 + t)
                    dve.tensor_tensor(b_lo[:, t % 2], b_rows(0), b_hi[:, t % 2].bitcast(F32), ALU.subtract).then_inc(r_bl, 1)

                def bd_split(t):
                    dve.wait_ge(r_bdh, t + 1)
                    dve.tensor_tensor(bd_lo, bd_raw, bd_hi.bitcast(F32), ALU.subtract).then_inc(r_bdl, 1)

                def ternary(k):
                    w = w_blk[k % 2]
                    dve.wait_ge(e_w[k % 2], 16 * (k // 2 + 1))
                    link(dve.tensor_scalar(w, w, w_inv[:], MAGIC, ALU.mult, ALU.add))
                    link(dve.tensor_scalar(w, w, MAGIC, 1.0, ALU.subtract, ALU.min))
                    dve.tensor_scalar(w_q[:, k], w, -1.0, None, ALU.max).then_inc(e_wq, 1)

                def factors(t):
                    q = slice(4 * t, 4 * t + 4)
                    dve.wait_ge(e_rt, t + 1)
                    dve.wait_ge(e_am, t + 1)
                    link(dve.reciprocal(ra[:, q], ra[:, q]))
                    link(dve.tensor_tensor(am[:, q], am[:, q], ra[:, q], ALU.mult))
                    link(dve.tensor_scalar(am[:, q], am[:, q], EPS, None, ALU.max))
                    link(dve.reciprocal(cc[:, q], am[:, q]))
                    dve.scalar_tensor_tensor(out=cc[:, q], in0=cc[:, q], scalar=127.0, in1=ra[:, q],
                                             op0=ALU.mult, op1=ALU.mult).then_inc(e_cc, 1)
                    link(dve.tensor_scalar(dq[:, q], am[:, q], wm[:], 1.0 / 127, ALU.mult, ALU.mult))

                def clip(t, subs):
                    for i in subs:
                        v = zf[:, i // 2, (i % 2) * L:(i % 2 + 1) * L]
                        dve.wait_ge(e_qm, 4 * t + i + 1)
                        dve.tensor_scalar(v, v, MAGIC + 127.0, MAGIC - 128.0, ALU.min, ALU.max).then_inc(e_cl, 1)

                def finish(t):
                    dve.wait_ge(q_bd, t + 1)
                    if t:
                        dve.wait_ge(e_qb, 4 * t)
                    zt = z[:, 4 * t:4 * t + 4]
                    zv = zf.rearrange("p j (i n) -> p j i n", n=L)
                    dve.tensor_tensor(zv, zt.rearrange("p (j i) n -> p j i n", i=2),
                                      ps_d[:].rearrange("p (j i) n -> p j i n", i=2), ALU.add).then_inc(e_zf, 1)
                    if t + 1 < NT:
                        bd_split(t + 1)
                    dve.wait_ge(e_zf, t + 1)
                    dve.tensor_reduce(am[:, 4 * t:4 * t + 4].rearrange("p (j i) -> p j i", i=2), zv, AX.X, ALU.max,
                                      apply_absolute_value=True).then_inc(e_am, 1)
                    dve.wait_ge(e_xt, 4 * t + 4)
                    dve.tensor_tensor(zt.rearrange("p (j i) n -> p j i n", i=2), zv,
                                      ps_d[:].rearrange("p (j i) n -> p j i n", i=2), ALU.add).then_inc(s_ev, 1)
                    factors(t)

                def logits(first, end):
                    for s in range(first, end):
                        dve.wait_ge(e_y, s + 1)
                        if s >= YD:
                            dve.wait_ge(e_gb, s - YD + 1)
                        dve.scalar_tensor_tensor(out=yb[:, s % YD], in0=ps_y[s % 2], scalar=dq[:, s:s + 1], in1=bias_sb,
                                                 op0=ALU.mult, op1=ALU.add).then_inc(e_yb, 1)
                        v = s - YD + 1
                        if v in ON_VECTOR:
                            whole(v)

                def whole(s):
                    dve.wait_ge(e_gb, s + 1)
                    dve.tensor_tensor(z[:, s], z[:, s], gb[:, s % GD], ALU.add).then_inc(e_od, 1)

                dve.wait_ge(e_wp, 1)
                link(dve.tensor_scalar(wm[:], ps_gu[2][:, 0:1], 1.0 / (L * L), EPS, ALU.mult, ALU.max))
                dve.reciprocal(w_inv[:], wm[:]).then_inc(e_wm, 1)
                dve.wait_ge(e_wm, 1)
                for k in range(2):
                    ternary(k)
                up(0, ML)
                hidden_low(0, ML)
                down_rows(ps_gu[2], (0,), RL)
                b_split_last(1)
                bd_split(0)
                for t in range(NT):
                    m, r = ML + t, RL + t
                    if t + 1 < NT:
                        up(0, m + 1)
                    td_add(t, r)
                    dve.wait_ge(q_tev, r + 2)
                    if t:
                        dve.wait_ge(r_tdl, t)
                    dve.tensor_tensor(tdm.rearrange("p (g n) -> p g n", g=2),
                                      td[:, t * TT:(t + 1) * TT].rearrange("p (g n) -> p g n", g=2),
                                      bc(lmask[:], 1, 2), ALU.mult).then_inc(r_tdm, 1)
                    dve.wait_ge(r_tdh, t + 1)
                    dve.tensor_tensor(h_lo[:, 1], tdm, h_hi[:, 1].bitcast(F32), ALU.subtract).then_inc(r_tdl, 1)
                    if t + 1 < NT:
                        hidden_low(0, m + 1)
                        down_rows(ps_gu[2], ((t + 1) % 2,), r + 1)
                    if t + 2 < NT:
                        b_split_last(t + 2)
                    if t == 0:
                        for k in range(2, KB):
                            ternary(k)
                    else:
                        clip(t - 1, range(4))
                    if t == NT - 1:
                        dve.wait_ge(e_b, 16)
                        logits(0, 2)
                    finish(t)
                clip(3, range(4))
                logits(2, YD)
                logits(YD, NSUB)
                whole(NSUB - 1)

def kernel(**inputs):
    import concourse.bacc as bacc
    from concourse.bass_utils import run_bass_kernel_spmd

    a = {k: np.asarray(v) for k, v in inputs.items()}

    def stack2(v):
        return np.concatenate([v, v], axis=0)

    def padded(v, axis, n):
        shape = list(v.shape)
        shape[axis] = n
        w = np.zeros(shape, v.dtype)
        w[tuple(slice(0, k) for k in v.shape)] = v
        return w

    def by_block(w, rows_reversed):
        w = w.reshape(-1, P, KB, P)
        if rows_reversed:
            w = w[..., ::-1]
        return w.transpose(0, 3, 2, 1).reshape(-1, P, KB * P)

    def slots(gate, up, down, rows_reversed):
        return np.stack([by_block(gate, rows_reversed), by_block(up, rows_reversed),
                         down.reshape(L, -1, P).transpose(1, 2, 0)], axis=2).reshape(-1, P, 3 * L)

    lay = {
        "x_t": a["x"].reshape(TOK, L).T.reshape(KB, P, TOK).transpose(1, 0, 2),
        "par": stack2(np.stack([np.broadcast_to(a["L0_cond_log_dt"][None, :], (NSTATE, HEADS)),
                                a["L0_cond_log_A_real"].T, a["L0_cond_A_imag"].T,
                                a["L0_cond_C"][..., 0].T, a["L0_cond_C"][..., 1].T], axis=1)),
        "d_row": a["L0_cond_D"][None, :],
        "length": a["itok_B_78_3631"],
        "idx": a["itok_B_2_6"],
        "w0": slots(a["L0_ffn_w1"], a["L0_ffn_w3"], a["L0_ffn_w2"], True),
        "sc0": np.concatenate([a["L0_ffn_w1_scale"], a["L0_ffn_w3_scale"], a["L0_ffn_w2_scale"].T], axis=1),
        "w1": slots(padded(a["L1_cond_W_gate"], 0, 2 * NC1 * P), padded(a["L1_cond_W_up"], 0, 2 * NC1 * P),
                    padded(a["L1_cond_W_down"], 1, 2 * NC1 * P), False),
        "tab_a": np.stack([a["L1_cond_A_gate"][0], a["L1_cond_A_up"][0]], axis=2).reshape(EXP * RANK, 2 * L),
        "tab_l": np.concatenate([
            padded(np.stack([a["L1_cond_B_gate"][0], a["L1_cond_B_up"][0]], axis=1), 2, 2 * NC1 * P)
            .reshape(EXP, 2, NC1, 2, P, RANK).transpose(2, 0, 5, 3, 1, 4).reshape(NC1, EXP, RANK, 4 * P),
            padded(a["L1_cond_A_down"][0], 2, 2 * NC1 * P)
            .reshape(EXP, RANK, NC1, 2 * P).transpose(2, 0, 1, 3)], axis=3).reshape(NC1 * EXP * RANK, 6 * P),
        "tab_bd": a["L1_cond_B_down"][0].transpose(0, 2, 1).reshape(EXP * RANK, L),
        "wq": a["L1_ffn_W"].T.reshape(KB, P, L).transpose(1, 0, 2),
        "bias": a["L1_ffn_b"][None, :],
        "rowbase": np.repeat((np.arange(P)[:, None] % RANK).astype(np.int32), NG, axis=1),
    }
    nc = bacc.Bacc("TRN2", target_bir_lowering=False, num_devices=1)
    arrays, args = {}, []
    for name, v in lay.items():
        v = np.ascontiguousarray(v)
        arrays["in_" + name] = v
        args.append(nc.dram_tensor("in_" + name, v.shape, mybir.dt.from_np(v.dtype), kind="ExternalInput").ap())
    args.append(nc.dram_tensor("out_0", (BATCH, HEADS, L), F32, kind="ExternalOutput").ap())
    build(nc, *args)
    r = run_bass_kernel_spmd(nc, [arrays], core_ids=[0])
    return r.results[0]["out_0"]
```
